# Optimizing a Trainium2 kernel written in Bass

```python
import numpy as np
import jax
import jax.numpy as jnp

def _softmax(x, axis=-1):
    return jax.nn.softmax(x, axis=axis)

def _gelu(x):
    return jax.nn.gelu(x, approximate=True)

def _silu(x):
    return jax.nn.silu(x)

def _sigmoid(x):
    return jax.nn.sigmoid(x)

def _layernorm(x, axis=-1, eps=1e-05):
    m = jnp.mean(x, axis=axis, keepdims=True)
    v = jnp.var(x, axis=axis, keepdims=True)
    return (x - m) / jnp.sqrt(v + eps)

def _scatter_add(tgt, idx, src, axis=0):
    return tgt.at[idx].add(src)

def _segment_sum(src, seg, n):
    return jax.ops.segment_sum(src, seg, n)
kernel_name = 'mk_hybrid_d1_jaxref_r8_1381dd'

def setup_inputs(seed: int=0):
    np.random.seed(seed)
    _w = jnp.asarray

    def _L0_attn_a_setup():
        import jax, jax.numpy as jnp
        import numpy as np
        EPS = 1e-05

        def layer_norm(x, g, b):
            mu = jnp.mean(x, axis=-1, keepdims=True)
            var = jnp.mean((x - mu) ** 2, axis=-1, keepdims=True)
            return (x - mu) * jax.lax.rsqrt(var + EPS) * g + b

        def quantum_circuit(v):
            return jnp.cumprod(jnp.cos(v), axis=-1)
        key = jax.random.key(seed)
        ks = jax.random.split(key, 8)
        B, T, C, H = (4, 256, 128, 16)
        dk = C // H
        nq_ffn, ffn_dim = (16, 512)
        return {'x': jax.random.normal(ks[0], (B, T, C), dtype=jnp.float32) * 0.5, 'attn_circuit_params': jax.random.normal(ks[1], (H, dk), dtype=jnp.float32), 'ffn_circuit_params': jax.random.normal(ks[2], (nq_ffn,), dtype=jnp.float32), 'w1': jax.random.normal(ks[3], (ffn_dim, nq_ffn), dtype=jnp.float32) * 0.1, 'b1': jnp.zeros((ffn_dim,), dtype=jnp.float32), 'w2': jax.random.normal(ks[4], (C, ffn_dim), dtype=jnp.float32) * 0.02, 'b2': jnp.zeros((C,), dtype=jnp.float32), 'gamma1': jnp.ones((C,), dtype=jnp.float32), 'beta1': jnp.zeros((C,), dtype=jnp.float32), 'gamma2': jnp.ones((C,), dtype=jnp.float32), 'beta2': jnp.zeros((C,), dtype=jnp.float32)}
    _L0_attn_a_in = _L0_attn_a_setup()

    def _L0_attn_b_setup():
        import math
        import jax, jax.numpy as jnp
        import numpy as np
        N_HEADS = 16

        def _phi(x, rf, m):
            norms_sq = jnp.sum(x * x, axis=-1, keepdims=True)
            proj = jnp.einsum('bhtd,md->bhtm', x, rf)
            scale = jnp.exp(-norms_sq * 0.5) / math.sqrt(m)
            return jnp.concatenate([jnp.cos(proj), jnp.sin(proj)], axis=-1) * scale
        key = jax.random.key(seed)
        ks = jax.random.split(key, 6)
        B, T, D = (2, 512, 128)
        m, dh = (32, D // N_HEADS)
        x = jax.random.normal(ks[0], (B, T, D), dtype=jnp.float32)
        s = 1.0 / math.sqrt(D)
        wq = jax.random.normal(ks[1], (D, D), dtype=jnp.float32) * s
        wk = jax.random.normal(ks[2], (D, D), dtype=jnp.float32) * s
        wv = jax.random.normal(ks[3], (D, D), dtype=jnp.float32) * s
        wo = jax.random.normal(ks[4], (D, D), dtype=jnp.float32) * s
        rf = jax.random.normal(ks[5], (m, dh), dtype=jnp.float32) / math.sqrt(dh)
        return {'x': x, 'wq': wq, 'wk': wk, 'wv': wv, 'wo': wo, 'rf': rf}
    _L0_attn_b_in = _L0_attn_b_setup()

    def _L0_ffn_setup():
        import jax, jax.numpy as jnp
        import numpy as np
        B, T, D, FF, E, TOP_K = (8, 256, 128, 512, 8, 2)
        key = jax.random.key(seed)
        kx, kr, k1, k2 = jax.random.split(key, 4)
        x = jax.random.normal(kx, (B, T, D), dtype=jnp.float32)
        Wr = jax.random.normal(kr, (E, D), dtype=jnp.float32) * 0.02
        W1 = jax.random.normal(k1, (E, D, FF), dtype=jnp.float32) * 0.02
        W2 = jax.random.normal(k2, (E, FF, D), dtype=jnp.float32) * 0.02
        return {'x': x, 'Wr': Wr, 'W1': W1, 'W2': W2}
    _L0_ffn_in = _L0_ffn_setup()
    _d = {'L0_attn_a_x': _L0_attn_a_in['x'], 'L0_attn_a_attn_circuit_params': _L0_attn_a_in['attn_circuit_params'], 'L0_attn_a_ffn_circuit_params': _L0_attn_a_in['ffn_circuit_params'], 'L0_attn_a_w1': _L0_attn_a_in['w1'], 'L0_attn_a_b1': _L0_attn_a_in['b1'], 'L0_attn_a_w2': _L0_attn_a_in['w2'], 'L0_attn_a_b2': _L0_attn_a_in['b2'], 'L0_attn_a_gamma1': _L0_attn_a_in['gamma1'], 'L0_attn_a_beta1': _L0_attn_a_in['beta1'], 'L0_attn_a_gamma2': _L0_attn_a_in['gamma2'], 'L0_attn_a_beta2': _L0_attn_a_in['beta2'], 'L0_attn_b_wq': _L0_attn_b_in['wq'], 'L0_attn_b_wk': _L0_attn_b_in['wk'], 'L0_attn_b_wv': _L0_attn_b_in['wv'], 'L0_attn_b_wo': _L0_attn_b_in['wo'], 'L0_attn_b_rf': _L0_attn_b_in['rf'], 'L0_ffn_Wr': _L0_ffn_in['Wr'], 'L0_ffn_W1': _L0_ffn_in['W1'], 'L0_ffn_W2': _L0_ffn_in['W2']}
    _x0 = _d['L0_attn_a_x']
    _d['L0_attn_a_x'] = jax.random.normal(jax.random.fold_in(jax.random.key(seed), 1), (8, 512, 128), dtype=_x0.dtype)
    del _x0
    return _d

def reference(L0_attn_a_x, L0_attn_a_attn_circuit_params, L0_attn_a_ffn_circuit_params, L0_attn_a_w1, L0_attn_a_b1, L0_attn_a_w2, L0_attn_a_b2, L0_attn_a_gamma1, L0_attn_a_beta1, L0_attn_a_gamma2, L0_attn_a_beta2, L0_attn_b_wq, L0_attn_b_wk, L0_attn_b_wv, L0_attn_b_wo, L0_attn_b_rf, L0_ffn_Wr, L0_ffn_W1, L0_ffn_W2):

    def _L0_attn_a_ref(x, attn_circuit_params, ffn_circuit_params, w1, b1, w2, b2, gamma1, beta1, gamma2, beta2):
        import jax, jax.numpy as jnp
        import numpy as np
        EPS = 1e-05

        def layer_norm(x, g, b):
            mu = jnp.mean(x, axis=-1, keepdims=True)
            var = jnp.mean((x - mu) ** 2, axis=-1, keepdims=True)
            return (x - mu) * jax.lax.rsqrt(var + EPS) * g + b

        def quantum_circuit(v):
            return jnp.cumprod(jnp.cos(v), axis=-1)
        B, T, C = x.shape
        H, dk = attn_circuit_params.shape
        nq = ffn_circuit_params.shape[0]
        xh = x.reshape(B, T, H, dk)
        attn_out = quantum_circuit(xh).reshape(B, T, C)
        x1 = layer_norm(x + attn_out, gamma1, beta1)
        q = quantum_circuit(x1[..., :nq])
        h = jnp.einsum('btq,fq->btf', q, w1) + b1
        ffn_out = jnp.einsum('btf,cf->btc', jax.nn.relu(h), w2) + b2
        return layer_norm(x1 + ffn_out, gamma2, beta2)

    def _L0_attn_b_ref(x, wq, wk, wv, wo, rf):
        import math
        import jax, jax.numpy as jnp
        import numpy as np
        N_HEADS = 16

        def _phi(x, rf, m):
            norms_sq = jnp.sum(x * x, axis=-1, keepdims=True)
            proj = jnp.einsum('bhtd,md->bhtm', x, rf)
            scale = jnp.exp(-norms_sq * 0.5) / math.sqrt(m)
            return jnp.concatenate([jnp.cos(proj), jnp.sin(proj)], axis=-1) * scale
        B, T, D = x.shape
        H = N_HEADS
        Dh = D // H
        m = rf.shape[0]

        def heads(w):
            return (x @ w.T).reshape(B, T, H, Dh).transpose(0, 2, 1, 3)
        Q, K, V = (heads(wq), heads(wk), heads(wv))
        Qf = _phi(Q, rf, m)
        Kf = _phi(K, rf, m)
        KV = jnp.einsum('bhnd,bhnv->bhdv', Kf, V)
        QKV = jnp.einsum('bhnd,bhdv->bhnv', Qf, KV)
        K_sum = jnp.sum(Kf, axis=2)
        Z = jnp.maximum(jnp.einsum('bhnd,bhd->bhn', Qf, K_sum)[..., None], 1e-06)
        out = (QKV / Z).transpose(0, 2, 1, 3).reshape(B, T, D)
        return out @ wo.T

    def _L0_ffn_ref(x, Wr, W1, W2):
        import jax, jax.numpy as jnp
        import numpy as np
        B, T, D, FF, E, TOP_K = (8, 256, 128, 512, 8, 2)
        Bs, Ts, Ds = x.shape
        Ne = Wr.shape[0]
        xf = x.reshape(-1, Ds)
        N = xf.shape[0]
        logits = xf @ Wr.T
        topk_vals, topk_idx = jax.lax.top_k(logits, TOP_K)
        w = jax.nn.softmax(topk_vals.astype(jnp.float32), axis=-1).astype(x.dtype)
        idx_flat = topk_idx.reshape(-1)
        w_flat = w.reshape(-1)
        sort_idx = jnp.argsort(idx_flat)
        rev = sort_idx // TOP_K
        sw = w_flat[sort_idx]
        perm = xf[rev]
        S = perm.shape[0]
        chunks = perm.reshape(Ne, S // Ne, Ds)
        h = jax.nn.gelu(jnp.einsum('ecd,edf->ecf', chunks, W1), approximate=False)
        eo = jnp.einsum('ecf,efd->ecd', h, W2).reshape(S, Ds)
        out = jnp.zeros((N, Ds), dtype=x.dtype).at[rev].add(eo * sw[:, None])
        return out.reshape(Bs, Ts, Ds)
    x = L0_attn_a_x
    x = x + _L0_attn_a_ref(_layernorm(x, axis=-1), L0_attn_a_attn_circuit_params, L0_attn_a_ffn_circuit_params, L0_attn_a_w1, L0_attn_a_b1, L0_attn_a_w2, L0_attn_a_b2, L0_attn_a_gamma1, L0_attn_a_beta1, L0_attn_a_gamma2, L0_attn_a_beta2)
    x = x + _L0_ffn_ref(_layernorm(x, axis=-1), L0_ffn_Wr, L0_ffn_W1, L0_ffn_W2)
    x = x + _L0_attn_b_ref(_layernorm(x, axis=-1), L0_attn_b_wq, L0_attn_b_wk, L0_attn_b_wv, L0_attn_b_wo, L0_attn_b_rf)
    x = x + _L0_ffn_ref(_layernorm(x, axis=-1), L0_ffn_Wr, L0_ffn_W1, L0_ffn_W2)
    return x

_drawn_inputs = setup_inputs


def setup_inputs(seed=0):
    import zlib

    import numpy as np

    out = dict(_drawn_inputs(seed))
    spreads = {'L0_attn_a_b1': (0.0, 0.452),
     'L0_attn_a_b2': (0.0, 0.1),
     'L0_attn_a_gamma1': (1.0, 0.2),
     'L0_attn_a_beta1': (0.0, 0.1),
     'L0_attn_a_gamma2': (1.0, 0.2),
     'L0_attn_a_beta2': (0.0, 0.1)}
    factors = {'L0_attn_a_w1': 3.759}
    for name, (base, spread) in spreads.items():
        noise = np.random.default_rng([zlib.crc32(name.encode()), seed]).standard_normal(out[name].shape)
        drawn = base * np.exp(spread * noise) if base else spread * noise
        out[name] = jnp.asarray(drawn.astype(out[name].dtype))
    for name, factor in factors.items():
        out[name] = (out[name] * factor).astype(out[name].dtype)
    return out
```

```python
import math
from contextlib import ExitStack

import concourse.bass as bass
from concourse import mybir

ALU = mybir.AluOpType
ACT = mybir.ActivationFunctionType
AX = mybir.AxisListType
F32 = mybir.dt.float32
BF16 = mybir.dt.bfloat16
I32 = mybir.dt.int32

P = 128
GT = 4
GN = GT * P
EPS = 1e-5
ROUND = 1.5 * 2.0 ** 23
TURN = 1.0 / (2.0 * math.pi)
TWO_PI = 6.283185005187988
HALF_PI = math.pi / 2


def nth(i, q, k=0, K=1, base=0):
    return i * (2 * K) + (2 * k + q + 1 + base)


class Steps:

    def __init__(self, eng, sem):
        self.eng, self.sem, self.base, self.n, self.i, self.per = eng, sem, 0, 0, 0, 0

    def loop(self, i, per, first=0):
        self.base += self.n - first * per
        self.i, self.per, self.n = i, per, 0

    def end(self, end):
        assert self.n == self.per, ("marks in this loop", self.n, self.per)
        self.base += self.per * end
        self.i, self.per, self.n = 0, 0, 0

    def mark(self, instruction):
        instruction.then_inc(self.sem, 1)
        self.n += 1
        return self.n

    def after(self, token):
        self.eng.wait_ge(self.sem, self.i * self.per + (self.base + token))


def build(nc, x_in, fw1, fb1, fw2, fb2, gamma1, beta1, gamma2, beta2, wq, wk, wv, wo, rf, wr, ew1, ew2, out):
    NTOK, C = x_in.shape
    NT = NTOK // P
    NG = NTOK // GN
    NI = NG // 2
    FF, NQ = fw1.shape
    FC = FF // P
    M, DH = rf.shape
    H = C // DH
    NE = wr.shape[0]
    EF = ew1.shape[2]
    EC = EF // P
    SLOTS = 2
    NPOS = SLOTS * NTOK
    NB = NPOS // GN
    BPE = NB // NE
    NTS = SLOTS * NT
    NHI = NPOS // P
    HPC = P // M
    NJ = H // HPC
    assert C == P and FC == 4 and EC == 4 and NJ == 4 and BPE == 2 and NI == 4 and NTS == 64 and NQ == 16

    xf_dram = nc.dram_tensor("xf_dram", [NTOK, C], F32).ap()
    y_dram = nc.dram_tensor("y_dram", [NPOS, C], F32).ap()

    def rows(ap, first_tile, tiles=GT):
        return ap[bass.ds(first_tile * P, tiles * P), :].rearrange("(t p) c -> p t c", p=P)

    with ExitStack() as ctx:
        def sb(name, shape, dt=F32):
            return ctx.enter_context(nc.sbuf_tensor(name, shape, dt))

        def ps(name, shape, dt=F32):
            return ctx.enter_context(nc.psum_tensor(name, shape, dt))

        def sem(name):
            return ctx.enter_context(nc.semaphore(name))

        ident = sb("ident", [P, P])
        identb = sb("identb", [P, P], BF16)
        after_tri = sb("after_tri", [P, 3 * P], BF16)
        ones_row = sb("ones_row", [P, P], BF16)
        iota_lo = sb("iota_lo", [P, P], BF16)
        iota_i = sb("iota_i", [P, P], I32)
        pcol_i = sb("pcol_i", [P, 1], I32)
        pcol = sb("pcol", [P, 1])
        half_pi = sb("half_pi", [P, 1])
        neg_half = sb("neg_half", [P, GT])
        kv_mask = sb("kv_mask", [P, HPC, DH])
        head_mask = sb("head_mask", [P, H])
        gb = sb("gb", [P, 5, C])
        G1, BE1, G2, BE2, B2 = range(5)
        w1_nat = sb("w1_nat", [P, FC, NQ + 1])
        w1_split = sb("w1_split", [P, FC, P], BF16)
        w1k = sb("w1k", [P, FF], BF16)
        w2t = sb("w2t", [P, FC, C])
        wr_nat = sb("wr_nat", [NE, C])
        wrt = sb("wrt", [C, NE])
        wqkv_t = sb("wqkv_t", [P, 3, C])
        wot = sb("wot", [P, C])
        rf_nat = sb("rf_nat", [M, DH])
        rf_rep = sb("rf_rep", [M, H, DH])
        rf_block = sb("rf_block", [P, H, M])
        wqf = sb("wqf", [P, H * M])
        wkf = sb("wkf", [P, H * M])
        ew1_sb = [sb(f"ew1_{s}", [P, EF]) for s in range(2)]
        ew2_sb = [sb(f"ew2_{s}", [P, EC, C]) for s in range(2)]

        x_all = sb("x_all", [P, NT, C])
        logits = sb("logits", [P, NE, NT])

        def two(name, shape, dt=F32):
            return [sb(f"{name}{q}", shape, dt) for q in range(2)]
        pairs = [two(f"pair{n}_", [P, 2, GT, C]) for n in range(3)]

        def halves(n):
            return [[pairs[n][q][:, h, :, :] for q in range(2)] for h in range(2)]
        (xw, xb), (yt, rt), (x1, x1b) = halves(0), halves(1), halves(2)
        stats = two("stats", [P, GT, 6])
        mv = two("mv", [P, GT, 2])
        var = two("var", [P, GT])
        rstd = two("rstd", [P, GT])
        ct = two("ct", [P, GT, C])
        sm = two("sm", [P, GT, C])
        q_ang = two("q_ang", [P, 2, GT, NQ])
        qc = two("qc", [P, GT, NQ])
        q_rest = two("q_rest", [P, 2, GT, NQ])
        q_split = two("q_split", [P, GT, P], BF16)
        q_t = two("q_t", [P, GN], BF16)
        hid = two("hid", [P, FC, GN])
        w2_nat, w_nat = hid[1][:, 0, :], hid[1][:, 1, :].rearrange("p (n c) -> p n c", n=4)
        xn = two("xn", [P, GT, C])
        xf = two("xf", [P, GT, C])
        xft = two("xft", [P, GN])
        gathered, expert_out = yt, rt
        gather_idx = two("gather_idx", [P, GT], I32)
        scatter_idx = two("scatter_idx", [P, GT], I32)
        y_in = two("y_in", [P, SLOTS, GT, C])
        w_stage = two("w_stage", [P, SLOTS, GT])
        top = sb("top", [P, SLOTS, NT])
        eq = sb("eq", [P, NE, NT])
        order_key = sb("order_key", [P, NE, NT])
        key_max = sb("key_max", [P, NT])
        masked = sb("masked", [P, NE, NT])
        pick = sb("pick", [P, SLOTS, NE, NT])
        picked = sb("picked", [P, NE, NT], BF16)
        first_bonus = sb("first_bonus", [P, NE, NT])
        count_b = sb("count_b", [P, 2, P], BF16)
        posf = sb("posf", [P, NTS])
        posi = sb("posi", [P, 3, NTS], I32)
        hilo = sb("hilo", [P, 2, NTS])
        gate = sb("gate", [P, 3, NT])
        w_slot = sb("w_slot", [P, SLOTS, NT])
        at_pos = sb("at_pos", [P, 2, NHI])
        row_f = sb("row_f", [P, 2, NHI])
        scatter_all = sb("scatter_all", [P, NHI], I32)
        gather_all = sb("gather_all", [P, NHI], I32)
        kfeat = two("kfeat", [P, GT, 2, H * M])
        qfeat = two("qfeat", [P, 2, NJ, GN])
        lo_hot = kfeat[0][:].rearrange("p a b c -> p (a b c)").bitcast(BF16).rearrange("p (s c) -> p s c", c=P)
        hi_hot = qfeat[0][:].rearrange("p a b c -> p (a b c)").bitcast(BF16).rearrange("p (s k c) -> p s k c", k=2, c=NHI)
        ang = [pairs[1][q][:, :, :, :].rearrange("p a b c -> p (a b c)") for q in range(2)]
        ang_abs = [pairs[2][q][:, :, :, :].rearrange("p a b c -> p (a b c)") for q in range(2)]
        vk = pairs[0]
        sq = [hid[q][:, 0:2, :].rearrange("p a (b c) -> p (a b) c", c=2 * C) for q in range(2)]
        v_sb = [hid[q][:, 2, :].rearrange("p (t c) -> p t c", t=GT) for q in range(2)]
        kvt = [hid[q][:, 3, :].rearrange("p (a c) -> p a c", a=4) for q in range(2)]
        nrm = two("nrm", [P, GT, 2 * H])
        scl = two("scl", [P, GT, 2 * H])
        att_t = [hid[q][:, 0, :] for q in range(2)]
        kvm = two("kvm", [P, 4, NJ, HPC * DH])
        zq = two("zq", [P, 3, GT, H])

        F = ps("F", [P, 4, GN])
        TA = [ps(f"TA{q}", [P, GN]) for q in range(2)]
        TB = [ps(f"TB{q}", [P, GN]) for q in range(2)]

        weights_in = sem("weights_in")
        consts_ready = sem("consts_ready")
        pool_steps = sem("pool_steps")
        dve_steps = sem("dve_steps")
        pool_held, dve_held = sem("pool_held"), sem("dve_held")
        setup_dve = sem("setup_dve")
        setup_pe = sem("setup_pe")
        w_split_ready = sem("w_split_ready")
        weights_ready = sem("weights_ready")
        x_loaded = [sem(f"x_loaded{q}") for q in range(2)]
        x_stats_used = sem("x_stats_used")
        var_ready, rstd_ready = sem("var_ready"), sem("rstd_ready")
        angle_ready, cos_ready = sem("angle_ready"), sem("cos_ready")
        x1_ready, x1b_ready, xb_ready = sem("x1_ready"), sem("x1b_ready"), sem("xb_ready")
        qangle_ready, qcos_ready, qsplit_ready = sem("qangle_ready"), sem("qcos_ready"), sem("qsplit_ready")
        qt_psum, qt_ready = sem("qt_psum"), sem("qt_ready")
        h_psum, h_ready = sem("h_psum"), sem("h_ready")
        ffn_psum = sem("ffn_psum")
        xn_ready, x_kept = sem("xn_ready"), sem("x_kept")
        xf_ready = sem("xf_ready")
        xf_stored = [sem(f"xf_stored{q}") for q in range(2)]
        xf_free = [sem(f"xf_free{q}") for q in range(2)]
        xft_psum, xft_ready, logit_psum, logit_ready = sem("xft_psum"), sem("xft_ready"), sem("logit_psum"), sem("logit_ready")
        gap_ready, gap_exp = sem("gap_ready"), sem("gap_exp")
        picked_ready, count_psum, count_ready, pos_psum = sem("picked_ready"), sem("count_psum"), sem("count_ready"), sem("pos_psum")
        hot_ready, inv_psum, index_ready = sem("hot_ready"), sem("inv_psum"), sem("index_ready")
        ew_loaded = [sem(f"ew_loaded{s}") for s in range(2)]
        gathered_in = [sem(f"gathered_in{s}") for s in range(2)]
        gt_psum, gt_ready, eh_psum, eh_ready, eo_psum, eo_ready = (
            sem("gt_psum"), sem("gt_ready"), sem("eh_psum"), sem("eh_ready"), sem("eo_psum"), sem("eo_ready"))
        scattered = [sem(f"scattered{s}") for s in range(2)]
        y_loaded = [sem(f"y_loaded{q}") for q in range(2)]
        y_used = sem("y_used")
        out_ready = sem("out_ready")
        out_stored = [sem(f"out_stored{q}") for q in range(2)]
        ax_ready, axt_psum, axt_ready = sem("ax_ready"), sem("axt_psum"), sem("axt_ready")
        qkv_psum, qkv_used, nrm_ready, scale_ready = sem("qkv_psum"), sem("qkv_used"), sem("nrm_ready"), sem("scale_ready")
        sq_ready, vk_ready, krep_ready = sem("sq_ready"), sem("vk_ready"), sem("krep_ready")
        proj_psum, ang_ready, abs_ready, sin_done, feat_ready = (
            sem("proj_psum"), sem("ang_ready"), sem("abs_ready"), sem("sin_done"), sem("feat_ready"))
        kvt_psum, kvt_ready, kv_psum, kvm_ready = sem("kvt_psum"), sem("kvt_ready"), sem("kv_psum"), sem("kvm_ready")
        num_psum, num_ready, numt_psum, att_ready = sem("num_psum"), sem("num_ready"), sem("numt_psum"), sem("att_ready")
        att_t_psum, att_t_ready, proj_out = sem("att_t_psum"), sem("att_t_ready"), sem("proj_out")

        A_STEPS, B_STEPS, C_STEPS = 64, 32, 6
        A_LN, B_LN = 4, 2
        LN_A0 = 0
        LN_B0 = LN_A0 + A_LN * NG
        PREP = (0, NG)
        XN = (0, 2 * NG)

        block = ctx.enter_context(nc.Block())

        @block.sync
        def _(sp):
            loads = [(w1_nat[:, :, 0:NQ], fw1.rearrange("(c p) k -> p c k", p=P)),
                     (w2_nat[:, :], fw2), (wr_nat[:, :], wr), (rf_nat[:, :], rf)]
            loads += [(gb[:, n, :], v.partition_broadcast(P)) for n, v in enumerate((gamma1, beta1, gamma2, beta2, fb2))]
            loads += [(w_nat[:, n, :], w) for n, w in enumerate((wq, wk, wv, wo))]
            for q in range(2):
                sp.dma_start(xw[q][:, :, :], rows(x_in, q * GT)).then_inc(x_loaded[q], 16)
            for dst, src in loads:
                sp.dma_start(dst, src).then_inc(weights_in, 16)
            with nc.allow_non_contiguous_dma("b1 lies along the partitions once"):
                sp.dma_start(w1_nat[:, :, NQ:NQ + 1], fb1.rearrange("(c p k) -> p c k", p=P, k=1)).then_inc(weights_in, 16)

            def load_expert(e, s):
                sp.dma_start(ew1_sb[s][:, :], ew1[bass.ds(e, 1), :, :].rearrange("a c f -> c (a f)")).then_inc(ew_loaded[s], 16)
                sp.dma_start(ew2_sb[s][:, :, :], ew2[bass.ds(e, 1), :, :].rearrange("a (k p) c -> p (a k) c", p=P))\
                    .then_inc(ew_loaded[s], 16)

            for s in range(2):
                load_expert(s, s)
            for q in range(2):
                sp.sem_inc(xf_free[q], 1)

            def store_xf(i, q, run):
                sp.wait_ge(xf_ready, nth(i, q, base=PREP[run]))
                sp.dma_start(rows(xf_dram, (i * 2 + q) * GT), xf[q][:, :, :]).then_inc(xf_stored[q], 16)

            def free_xf(i, q, run):
                sp.wait_ge(xf_stored[q], i * 16 + (16 + run * 16 * NI))
                sp.sem_inc(xf_free[q], 1)

            with sp.Fori(0, NI - 1) as i:
                for q in range(2):
                    sp.wait_ge(x_stats_used, nth(i, q))
                    sp.wait_ge(xb_ready, nth(i, q))
                    sp.dma_start(xw[q][:, :, :], rows(x_in, (i * 2 + q) * GT + 2 * GT)).then_inc(x_loaded[q], 16)
                for q in range(2):
                    store_xf(i, q, 0)
                for q in range(2):
                    free_xf(i, q, 0)
            for q in range(2):
                store_xf(NI - 1, q, 0)
            for q in range(2):
                free_xf(NI - 1, q, 0)

            def experts(run):
                with sp.Fori(0, NE // 2 - 1) as i:
                    for s in range(2):
                        sp.wait_ge(eo_psum, i * 4 + (2 * s + 2 + run * NB))
                        load_expert(i * 2 + (s + 2), s)
                if run == 0:
                    for s in range(2):
                        sp.wait_ge(eo_psum, NB - 2 + 2 * s)
                        load_expert(s, s)
                for s in range(2):
                    sp.wait_ge(scattered[s], 16 * GT * (NB // 2) * (run + 1))

            def load_y(i, q):
                first = (i * 2 + q) * GT
                for s in range(SLOTS):
                    sp.dma_start(y_in[q][:, s, :, :], rows(y_dram, first + s * NT)).then_inc(y_loaded[q], 16)

            experts(0)
            for q in range(2):
                load_y(0, q)
            with sp.Fori(0, NI - 1) as i:
                for q in range(2):
                    sp.wait_ge(y_used, nth(i, q))
                    load_y(i + 1, q)
                for q in range(2):
                    store_xf(i, q, 1)
                for q in range(2):
                    free_xf(i, q, 1)
            for q in range(2):
                store_xf(NI - 1, q, 1)

            experts(1)
            for q in range(2):
                load_y(0, q)
            with sp.Fori(0, NI - 1) as i:
                for q in range(2):
                    sp.wait_ge(out_ready, nth(i, q))
                    sp.dma_start(rows(out, (i * 2 + q) * GT), xn[q][:, :, :]).then_inc(out_stored[q], 16)
                    load_y(i + 1, q)
            for q in range(2):
                sp.wait_ge(out_ready, nth(NI - 1, q))
                sp.dma_start(rows(out, (2 * NI - 2 + q) * GT), xn[q][:, :, :]).then_inc(out_stored[q], 16)
            for q in range(2):
                sp.wait_ge(out_stored[q], 16 * NI)

        @block.gpsimd
        def _(pool):
            g = nc.gpsimd
            step = Steps(pool, pool_steps)
            m = [step.mark(g.memset(ident[:, :], 0.0)), step.mark(g.memset(after_tri[:, :], 1.0)),
                 step.mark(g.memset(kv_mask[:, :, :], 1.0)), step.mark(g.memset(head_mask[:, :], 1.0)),
                 step.mark(g.iota(iota_i[:, :], pattern=[[1, P]], base=0, channel_multiplier=0)),
                 step.mark(g.iota(pcol_i[:, :], pattern=[[0, 1]], base=0, channel_multiplier=1))]
            g.memset(ones_row[:, :], 1.0)
            g.memset(half_pi[:, :], HALF_PI)
            g.memset(neg_half[:, :], -0.5)
            for e in range(NE):
                g.memset(first_bonus[:, e, :], float(NE - e))
            for q in range(2):
                g.memset(q_split[q][:, :, 6 * NQ:], 0.0)
            last = g.memset(w1_split[:, :, 6 * NQ:], 0.0)
            m.append(step.mark(last))
            step.after(m[-1])
            g.affine_select(out=ident[:, :], in_=ident[:, :], compare_op=ALU.not_equal, fill=1.0, base=0,
                            pattern=[[-1, P]], channel_multiplier=1)
            for q in range(2):
                g.memset(q_split[q][:, :, 6 * NQ:6 * NQ + 3], 1.0)
            g.affine_select(out=after_tri[:, :], in_=after_tri[:, :], compare_op=ALU.is_gt, fill=0.0, base=-P,
                            pattern=[[1, 3 * P]], channel_multiplier=-1)
            lower_kv = g.affine_select(out=kv_mask[:, :, :], in_=kv_mask[:, :, :], compare_op=ALU.is_ge, fill=0.0, base=0,
                                       pattern=[[-M, HPC], [0, DH]], channel_multiplier=1)
            step.mark(lower_kv)
            t = step.mark(g.affine_select(out=head_mask[:, :], in_=head_mask[:, :], compare_op=ALU.is_ge, fill=0.0, base=0,
                                          pattern=[[-DH, H]], channel_multiplier=1))
            step.after(t)
            g.affine_select(out=kv_mask[:, :, :], in_=kv_mask[:, :, :], compare_op=ALU.is_ge, fill=0.0, base=M - 1,
                            pattern=[[M, HPC], [0, DH]], channel_multiplier=-1)
            g.affine_select(out=head_mask[:, :], in_=head_mask[:, :], compare_op=ALU.is_ge, fill=0.0, base=DH - 1,
                            pattern=[[DH, H]], channel_multiplier=-1).then_inc(consts_ready, 1)

            def inverse_root(value):
                for q in range(2):
                    pool.wait_ge(var_ready, value(q))
                    g.tensor_tensor(rstd[q][:, :], var[q][:, :], neg_half[:, :], ALU.pow).then_inc(rstd_ready, 1)

            def tile_bcast(row):
                return gb[:, row, :].unsqueeze(1).broadcast_to([P, GT, C])

            pool.wait_ge(weights_in, 16 * 14)
            with pool.Fori(0, NI) as i:
                inverse_root(lambda q: nth(i, q, 0, A_LN))
                for q in range(2):
                    pool.wait_ge(x_loaded[q], i * 16 + 16)
                    g.tensor_tensor(xb[q][:, :, :], xw[q][:, :, :], tile_bcast(BE2), ALU.add).then_inc(xb_ready, 1)
                inverse_root(lambda q: nth(i, q, 1, A_LN))
                for q in range(2):
                    pool.wait_ge(x1_ready, nth(i, q))
                    g.tensor_tensor(x1b[q][:, :, :], x1[q][:, :, :], tile_bcast(B2), ALU.add).then_inc(x1b_ready, 1)
                inverse_root(lambda q: nth(i, q, 2, A_LN))
                inverse_root(lambda q: nth(i, q, 3, A_LN))

            def experts(run):
                def issue_gather(s):
                    pool.sem_inc(pool_held, 1)
                    for t in range(GT):
                        g.indirect_dma_start(gathered[s][:, t, :], None, xf_dram[:, :],
                                             bass.IndirectOffsetOnAxis(gather_idx[s][:, t:t + 1], 0))\
                            .then_inc(gathered_in[s], 16)

                def issue_scatter(s):
                    pool.sem_inc(pool_held, 1)
                    for t in range(GT):
                        g.indirect_dma_start(y_dram[:, :], bass.IndirectOffsetOnAxis(scatter_idx[s][:, t:t + 1], 0),
                                             expert_out[s][:, t, :], None).then_inc(scattered[s], 16)

                pool.wait_ge(index_ready, run + 1)
                for q in range(2):
                    pool.wait_ge(xf_stored[q], 16 * NI * (run + 1))
                for s in range(2):
                    g_tok = step.mark(g.tensor_copy(gather_idx[s][:, :], gather_all[:, s * GT:(s + 1) * GT]))
                    step.after(g_tok)
                    issue_gather(s)

                def work(i, s, ahead):
                    if ahead:
                        pool.wait_ge(gt_psum, nth(i, s, base=run * NB))
                        pool.wait_ge(gathered_in[s], i * (16 * GT) + (16 * GT + run * 16 * GT * (NB // 2)))
                        pool.sem_inc(pool_held, 1)
                        tok = step.mark(g.tensor_copy(gather_idx[s][:, :], gather_all[:, bass.ds(i * (2 * GT) + (s + 2) * GT, GT)]))
                        step.after(tok)
                        issue_gather(s)
                    if run == 0:
                        if ahead != "first":
                            pool.wait_ge(scattered[s], i * (16 * GT))
                    else:
                        pool.wait_ge(scattered[s], i * (16 * GT) + 16 * GT * (NB // 2))
                    pool.sem_inc(pool_held, 1)
                    tok = step.mark(g.tensor_copy(scatter_idx[s][:, :], scatter_all[:, bass.ds(i * (2 * GT) + s * GT, GT)]))
                    step.after(tok)
                    pool.wait_ge(eo_ready, nth(i, s, base=run * NB))
                    issue_scatter(s)

                for s in range(2):
                    work(0, s, "first")
                with pool.Fori(1, NB // 2 - 1) as i:
                    step.loop(i, 4, 1)
                    for s in range(2):
                        work(i, s, True)
                step.end(NB // 2 - 1)
                for s in range(2):
                    work(NB // 2 - 1, s, False)

            experts(0)

            with pool.Fori(0, NI) as i:
                inverse_root(lambda q: nth(i, q, 0, B_LN, LN_B0))
                for q in range(2):
                    pool.wait_ge(scale_ready, nth(i, q))
                    pool.sem_inc(pool_held, 1)
                    g.tensor_copy(vk[q][:, 1, :, :].rearrange("p t (h d) -> p t h d", h=H),
                                  scl[q][:, :, H:2 * H].unsqueeze(3).broadcast_to([P, GT, H, DH])).then_inc(krep_ready, 1)
                inverse_root(lambda q: nth(i, q, 1, B_LN, LN_B0))
            experts(1)

        @block.scalar
        def _(act):
            a = nc.scalar.activation
            act.wait_ge(consts_ready, 1)

            def transpose_out(i, q, ready, signal, value, psum, dst):
                act.wait_ge(ready, value)
                a(dst, psum, ACT.Copy).then_inc(signal, 1)

            def prepare(i, q, run):
                act.wait_ge(xft_psum, nth(i, q, base=PREP[run]))
                a(xft[q][:, :], TA[q][:, :], ACT.Copy).then_inc(xft_ready, 1)

            def keep(i, q, value):
                act.wait_ge(xn_ready, value)
                a(x_all[:, bass.ds(i * (2 * GT) + q * GT, GT), :], xn[q][:, :, :], ACT.Copy).then_inc(x_kept, 1)

            with act.Fori(0, NI) as i:
                for q in range(2):
                    act.wait_ge(angle_ready, nth(i, q))
                    a(ct[q][:, :, :], rt[q][:, :, :], ACT.Sin, bias=half_pi[:, 0:1], scale=-TWO_PI).then_inc(cos_ready, 1)
                for q in range(2):
                    act.wait_ge(qangle_ready, nth(i, q))
                    a(qc[q][:, :, :], q_ang[q][:, 1, :, :], ACT.Sin, bias=half_pi[:, 0:1], scale=-TWO_PI).then_inc(qcos_ready, 1)
                for q in range(2):
                    act.wait_ge(qt_psum, nth(i, q))
                    a(q_t[q][:, :], TA[q][:, :].bitcast(BF16)[:, 0:GN], ACT.Copy).then_inc(qt_ready, 1)
                for q in range(2):
                    for half in range(2):
                        act.wait_ge(h_psum, i * 4 + (2 * q + half + 1))
                        a(hid[q][:, 2 * half:2 * half + 2, :], F[:, 2 * half:2 * half + 2, :], ACT.Relu).then_inc(h_ready, 1)
                for q in range(2):
                    keep(i, q, nth(i, q, base=XN[0]))
                for q in range(2):
                    prepare(i, q, 0)

            def route(run):
                act.wait_ge(gap_ready, run + 1)
                a(gate[:, 1, :], gate[:, 0, :], ACT.Exp).then_inc(gap_exp, 1)

            def experts(run):
                def work(i, s):
                    for half in range(2):
                        act.wait_ge(eh_psum, i * 4 + (2 * s + half + 1 + run * 2 * NB))
                        a(hid[s][:, 2 * half:2 * half + 2, :], F[:, 2 * half:2 * half + 2, :], ACT.Gelu).then_inc(eh_ready, 1)

                with act.Fori(0, NB // 2) as i:
                    for s in range(2):
                        work(i, s)

            route(0)
            experts(0)
            with act.Fori(0, NI) as i:
                for q in range(2):
                    transpose_out(i, q, axt_psum, axt_ready, nth(i, q), TA[q][:, :], xft[q][:, :])
                for q in range(2):
                    act.wait_ge(qkv_psum, nth(i, q))
                    a(sq[q][:, :, :], F[:, :, 0:2 * C], ACT.Square).then_inc(sq_ready, 1)
                    a(v_sb[q][:, :, :], F[:, :, 2 * C:3 * C], ACT.Copy).then_inc(qkv_used, 1)
                for q in range(2):
                    act.wait_ge(nrm_ready, nth(i, q))
                    a(scl[q][:, :, :], nrm[q][:, :, :], ACT.Exp, scale=-0.5).then_inc(scale_ready, 1)
                for q in range(2):
                    for kind in range(2):
                        for u in range(2):
                            r = u
                            k = q * 4 + kind * 2 + u + 1
                            if kind == 0:
                                sin_dst = kfeat[q][:, 2 * u:2 * u + 2, 0, :]
                                cos_dst = kfeat[q][:, 2 * u:2 * u + 2, 1, :]
                            else:
                                sin_dst = qfeat[q][:, 0, 2 * u:2 * u + 2, :]
                                cos_dst = qfeat[q][:, 1, 2 * u:2 * u + 2, :]
                            src = ang[r][:, :].rearrange("p (a b) -> p a b", a=2)
                            src_abs = ang_abs[r][:, :].rearrange("p (a b) -> p a b", a=2)
                            act.wait_ge(ang_ready, i * 8 + k)
                            a(sin_dst, src, ACT.Sin, scale=TWO_PI).then_inc(sin_done, 1)
                            act.wait_ge(abs_ready, i * 8 + k)
                            a(cos_dst, src_abs, ACT.Sin, bias=half_pi[:, 0:1], scale=-TWO_PI).then_inc(feat_ready, 1)
                for q in range(2):
                    transpose_out(i, q, kvt_psum, kvt_ready, nth(i, q), TA[q][:, :], kvt[q][:, :, :].rearrange("p a b -> p (a b)"))
                for q in range(2):
                    act.wait_ge(num_psum, nth(i, q))
                    a(sm[q][:, :, :].rearrange("p a b -> p (a b)"), TA[q][:, :], ACT.Copy)
                    a(ct[q][:, :, :].rearrange("p a b -> p (a b)"), TB[q][:, :], ACT.Copy).then_inc(num_ready, 1)
                for q in range(2):
                    transpose_out(i, q, att_t_psum, att_t_ready, nth(i, q), TA[q][:, :], att_t[q][:, :])
                for q in range(2):
                    keep(i, q, nth(i, q, base=NG))
                for q in range(2):
                    prepare(i, q, 1)
            route(1)
            experts(1)

        @block.vector
        def _(dve):
            v = nc.vector
            step = Steps(dve, dve_steps)
            MARK = step.mark

            dve.wait_ge(consts_ready, 1)
            v.tensor_copy(identb[:, :], ident[:, :]).then_inc(setup_dve, 1)
            v.tensor_copy(iota_lo[:, :], iota_i[:, :])
            v.tensor_copy(pcol[:, :], pcol_i[:, :])
            dve.wait_ge(weights_in, 16 * 14)
            v.tensor_copy(rf_rep[:, :, :], rf_nat[:, :].unsqueeze(1).broadcast_to([M, H, DH])).then_inc(setup_dve, 1)
            split = w1_split
            rest = q_rest[0][:, 0, :, :].rearrange("p a b -> p (a b)")
            rest = rest.rearrange("p (c k) -> p c k", c=FC)
            rest_b = posf[:, 0:FC].unsqueeze(2)
            wn, bn = w1_nat[:, :, 0:NQ], w1_nat[:, :, NQ:NQ + 1]
            k6 = 6 * NQ

            def cols(part, n=NQ):
                return split[:, :, part * NQ:part * NQ + n]
            t = MARK(v.tensor_copy(cols(0), wn))
            MARK(v.tensor_copy(cols(3), wn))
            MARK(v.tensor_copy(cols(5), wn))
            t = MARK(v.tensor_copy(split[:, :, k6:k6 + 1], bn))
            step.after(t)
            MARK(v.tensor_tensor(rest, wn, cols(0), ALU.subtract))
            t = MARK(v.tensor_tensor(rest_b, bn, split[:, :, k6:k6 + 1], ALU.subtract))
            step.after(t)
            MARK(v.tensor_copy(cols(1), rest))
            MARK(v.tensor_copy(cols(4), rest))
            t = MARK(v.tensor_copy(split[:, :, k6 + 1:k6 + 2], rest_b))
            step.after(t)
            MARK(v.tensor_tensor(rest, rest, cols(1), ALU.subtract))
            t = MARK(v.tensor_tensor(rest_b, rest_b, split[:, :, k6 + 1:k6 + 2], ALU.subtract))
            step.after(t)
            v.tensor_copy(cols(2), rest)
            v.tensor_copy(split[:, :, k6 + 2:k6 + 3], rest_b).then_inc(w_split_ready, 1)
            dve.wait_ge(setup_pe, 1)
            v.tensor_copy(w1k[:, :], F[:, 0, :].bitcast(BF16)[:, 0:FF])
            v.tensor_copy(w2t[:, :, :].rearrange("p a b -> p (a b)"), F[:, 1, :])
            v.tensor_copy(wqkv_t[:, :, :].rearrange("p a b -> p (a b)"), F[:, 2, 0:3 * C])
            v.tensor_copy(wot[:, :], F[:, 2, 3 * C:4 * C])
            v.tensor_copy(wrt[:, :], F[:, 3, 0:NE])
            v.scalar_tensor_tensor(rf_block[:, :, :], F[:, 3, P:P + M].unsqueeze(1).broadcast_to([P, H, M]), TURN,
                                   head_mask[:, :].unsqueeze(2).broadcast_to([P, H, M]), ALU.mult, ALU.mult)\
                .then_inc(setup_dve, 1)
            dve.wait_ge(setup_pe, 2)
            v.tensor_copy(wqf[:, :], TA[0][:, :])
            v.tensor_copy(wkf[:, :], TA[1][:, :]).then_inc(weights_ready, 1)

            def magnitude(dst, src):
                return v.tensor_scalar(dst.bitcast(I32), src.bitcast(I32), 0x7FFFFFFF, None, ALU.bitwise_and)

            def ln_stats(src, scale):
                tok = [0, 0]
                for q in range(2):
                    for t in range(GT):
                        ins = v.bn_stats(stats[q][:, t, :], src(q)[:, t, :])
                    tok[q] = MARK(ins)
                tok2 = [0, 0]
                for q in range(2):
                    step.after(tok[q])
                    dve.sem_inc(dve_held, 1)
                    for t in range(GT):
                        ins = v.bn_aggr(mv[q][:, t, :], stats[q][:, t, :])
                    tok2[q] = MARK(ins)
                for q in range(2):
                    step.after(tok2[q])
                    v.tensor_scalar(var[q][:, :], mv[q][:, :, 1], EPS, scale, ALU.add, ALU.mult).then_inc(var_ready, 1)

            def normalise(dst, src, rstd_value):
                last = []
                for q in range(2):
                    dve.wait_ge(rstd_ready, rstd_value(q))
                    for t in range(GT):
                        ins = v.tensor_scalar(dst(q)[:, t, :], src(q)[:, t, :], mv[q][:, t, 0:1], rstd[q][:, t:t + 1],
                                              ALU.subtract, ALU.mult)
                    last.append(ins)
                return last

            def scale_shift(mid, dst, src, gamma_row, shift, rstd_value):
                toks, last = [], []
                for q in range(2):
                    for t in range(GT):
                        ins = v.scalar_tensor_tensor(mid[q][:, t, :], src[q][:, t, :], mv[q][:, t, 0:1], gb[:, gamma_row, :],
                                                     ALU.subtract, ALU.mult)
                    toks.append(MARK(ins))
                for q in range(2):
                    step.after(toks[q])
                    dve.wait_ge(rstd_ready, rstd_value(q))
                    for t in range(GT):
                        ins = v.scalar_tensor_tensor(dst[q][:, t, :], mid[q][:, t, :], rstd[q][:, t:t + 1], shift(q, t),
                                                     ALU.mult, ALU.add)
                    last.append(ins)
                return last

            def prepare(i, run, rstd_value):
                ln_stats(lambda q: xn[q], 1.0)
                for q in range(2):
                    dve.wait_ge(xf_free[q], i + (1 + run * NI))
                last = normalise(lambda q: xf[q], lambda q: xn[q], rstd_value)
                for q in range(2):
                    last[q].then_inc(xf_ready, 1)
                for q in range(2):
                    dve.wait_ge(logit_psum, nth(i, q, base=PREP[run]))
                    v.tensor_copy(logits[:, :, bass.ds(i * (2 * GT) + q * GT, GT)].rearrange("p e t -> p t e"),
                                  TB[q][:, 0:GT * NE].rearrange("p (t e) -> p t e", e=NE)).then_inc(logit_ready, 1)

            with dve.Fori(0, NI) as i:
                step.loop(i, A_STEPS)
                for q in range(2):
                    dve.wait_ge(x_loaded[q], i * 16 + 16)
                ln_stats(lambda q: xw[q], (2 * math.pi) ** 2)
                last = normalise(lambda q: yt[q], lambda q: xw[q], lambda q: nth(i, q, 0, A_LN))
                for q in range(2):
                    last[q].then_inc(x_stats_used, 1)
                tok = [0, 0]
                for q in range(2):
                    dve.wait_ge(x_stats_used, nth(i, q))
                    tok[q] = MARK(v.tensor_scalar(rt[q][:, :, :], yt[q][:, :, :], ROUND, ROUND, ALU.add, ALU.subtract))
                for q in range(2):
                    step.after(tok[q])
                    tok[q] = MARK(v.tensor_tensor(rt[q][:, :, :], yt[q][:, :, :], rt[q][:, :, :], ALU.subtract))
                for q in range(2):
                    step.after(tok[q])
                    magnitude(rt[q][:, :, :], rt[q][:, :, :]).then_inc(angle_ready, 1)
                cv = [ct[q][:, :, :].rearrange("p t (h d) -> p (t h) d", d=DH) for q in range(2)]
                for q in range(2):
                    dve.wait_ge(cos_ready, nth(i, q))
                for d in range(1, DH):
                    for q in range(2):
                        if d > 1:
                            step.after(tok[q])
                        tok[q] = MARK(v.tensor_tensor(cv[q][:, :, d], cv[q][:, :, d], cv[q][:, :, d - 1], ALU.mult))
                for q in range(2):
                    step.after(tok[q])
                    tok[q] = MARK(v.scalar_tensor_tensor(sm[q][:, :, :], yt[q][:, :, :], 2 * math.pi, ct[q][:, :, :],
                                                         ALU.mult, ALU.add))
                for q in range(2):
                    step.after(tok[q])
                ln_stats(lambda q: sm[q], 1.0)
                last = scale_shift(yt, x1, sm, G1, lambda q, t: gb[:, BE1, :], lambda q: nth(i, q, 1, A_LN))
                for q in range(2):
                    last[q].then_inc(x1_ready, 1)
                qy = [q_rest[q][:, 0, :, :] for q in range(2)]
                for q in range(2):
                    dve.wait_ge(x1_ready, nth(i, q))
                    tok[q] = MARK(v.tensor_scalar(qy[q], x1[q][:, :, 0:NQ], TURN, None, ALU.mult))
                for q in range(2):
                    step.after(tok[q])
                    tok[q] = MARK(v.tensor_scalar(q_ang[q][:, 0, :, :], qy[q], ROUND, ROUND, ALU.add, ALU.subtract))
                for q in range(2):
                    step.after(tok[q])
                    tok[q] = MARK(v.tensor_tensor(q_ang[q][:, 0, :, :], qy[q], q_ang[q][:, 0, :, :], ALU.subtract))
                for q in range(2):
                    step.after(tok[q])
                    magnitude(q_ang[q][:, 1, :, :], q_ang[q][:, 0, :, :]).then_inc(qangle_ready, 1)
                for q in range(2):
                    dve.wait_ge(qcos_ready, nth(i, q))
                k = 1
                while k < NQ:
                    for q in range(2):
                        b = qc[q][:, :, :].rearrange("p t (n two k) -> p (t n) two k", two=2, k=k)
                        if k > 1:
                            step.after(tok[q])
                        nb = GT * NQ // (2 * k)
                        tok[q] = MARK(v.tensor_tensor(b[:, :, 1, :], b[:, :, 1, :],
                                                      b[:, :, 0, k - 1:k].broadcast_to([P, nb, k]), ALU.mult))
                    k *= 2
                def part(q, first, n):
                    return q_split[q][:, :, first * NQ:(first + n) * NQ].rearrange("p t (n k) -> p t n k", n=n)

                def spread(src, n):
                    return src.unsqueeze(2).broadcast_to([P, GT, n, NQ])
                for q in range(2):
                    step.after(tok[q])
                    tok[q] = MARK(v.tensor_copy(part(q, 0, 3), spread(qc[q][:, :, :], 3)))
                for q in range(2):
                    step.after(tok[q])
                    tok[q] = MARK(v.tensor_tensor(q_rest[q][:, 0, :, :], qc[q][:, :, :], q_split[q][:, :, 0:NQ], ALU.subtract))
                for q in range(2):
                    step.after(tok[q])
                    tok[q] = MARK(v.tensor_copy(part(q, 3, 2), spread(q_rest[q][:, 0, :, :], 2)))
                for q in range(2):
                    step.after(tok[q])
                    tok[q] = MARK(v.tensor_tensor(q_rest[q][:, 1, :, :], q_rest[q][:, 0, :, :],
                                                  q_split[q][:, :, 3 * NQ:4 * NQ], ALU.subtract))
                for q in range(2):
                    step.after(tok[q])
                    v.tensor_copy(q_split[q][:, :, 5 * NQ:6 * NQ], q_rest[q][:, 1, :, :]).then_inc(qsplit_ready, 1)
                for q in range(2):
                    dve.wait_ge(ffn_psum, nth(i, q))
                    dve.wait_ge(x1b_ready, nth(i, q))
                    tok[q] = MARK(v.tensor_tensor(sm[q][:, :, :].rearrange("p a b -> p (a b)"), TB[q][:, :],
                                                  x1b[q][:, :, :].rearrange("p a b -> p (a b)"), ALU.add))
                for q in range(2):
                    step.after(tok[q])
                ln_stats(lambda q: sm[q], 1.0)
                for q in range(2):
                    dve.wait_ge(xb_ready, nth(i, q))
                last = scale_shift(yt, xn, sm, G2, lambda q, t: xb[q][:, t, :], lambda q: nth(i, q, 2, A_LN))
                for q in range(2):
                    last[q].then_inc(xn_ready, 1)
                for q in range(2):
                    dve.wait_ge(xn_ready, nth(i, q, base=XN[0]))
                prepare(i, 0, lambda q: nth(i, q, 3, A_LN))
            step.end(NI)

            def route(run):
                def chain(ins):
                    step.after(MARK(ins))

                def over_e(ap):
                    return ap.rearrange("p e t -> p t e")

                def tb(ap):
                    return ap.unsqueeze(1).broadcast_to([P, NE, NT])
                for q in range(2):
                    dve.wait_ge(logit_ready, nth(NI - 1, q, base=PREP[run]))
                src = logits
                for s in range(SLOTS):
                    chain(v.tensor_reduce(top[:, s, :], over_e(src[:, :, :]), AX.X, ALU.max))
                    chain(v.tensor_tensor(eq[:, :, :], src[:, :, :], tb(top[:, s, :]), ALU.is_equal))
                    chain(v.tensor_tensor(order_key[:, :, :], eq[:, :, :], first_bonus[:, :, :], ALU.mult))
                    chain(v.tensor_reduce(key_max[:, :], over_e(order_key[:, :, :]), AX.X, ALU.max))
                    chain(v.tensor_tensor(pick[:, s, :, :], order_key[:, :, :], tb(key_max[:, :]), ALU.is_equal))
                    if s == 0:
                        chain(v.scalar_tensor_tensor(masked[:, :, :], pick[:, 0, :, :], -3.0e38, logits[:, :, :],
                                                     ALU.mult, ALU.add))
                        src = masked
                v.tensor_tensor(picked[:, :, :], pick[:, 0, :, :], pick[:, 1, :, :], ALU.add).then_inc(picked_ready, 1)
                v.tensor_tensor(gate[:, 0, :], top[:, 1, :], top[:, 0, :], ALU.subtract).then_inc(gap_ready, 1)
                dve.wait_ge(gap_exp, run + 1)
                chain(v.tensor_scalar(gate[:, 2, :], gate[:, 1, :], 1.0, None, ALU.add))
                chain(v.reciprocal(w_slot[:, 0, :], gate[:, 2, :]))
                MARK(v.tensor_tensor(w_slot[:, 1, :], gate[:, 1, :], w_slot[:, 0, :], ALU.mult))
                dve.wait_ge(count_psum, run + 1)
                for h in range(2):
                    ins = v.tensor_scalar(count_b[:, h, :], ones_row[:, :], TB[0][:, h:h + 1], None, ALU.mult)
                ins.then_inc(count_ready, 1)
                dve.wait_ge(pos_psum, run + 1)
                pos = TA[0][:, 0:NE * NT].rearrange("p (e t) -> p e t", e=NE)
                for s in range(SLOTS):
                    dst = (eq, order_key)[s]
                    chain(v.tensor_tensor(dst[:, :, :], pick[:, s, :, :], pos, ALU.mult))
                    chain(v.tensor_reduce(posf[:, s * NT:(s + 1) * NT], over_e(dst[:, :, :]), AX.X, ALU.add))
                chain(v.tensor_copy(posi[:, 0, :], posf[:, :]))
                MARK(v.tensor_scalar(posi[:, 1, :], posi[:, 0, :], 7, None, ALU.logical_shift_right))
                chain(v.tensor_scalar(posi[:, 2, :], posi[:, 0, :], P - 1, None, ALU.bitwise_and))
                chain(v.tensor_copy(hilo[:, :, :], posi[:, 1:3, :]))
                for s in range(NTS):
                    v.tensor_scalar(lo_hot[:, s, :], iota_lo[:, :], hilo[:, 1, s:s + 1], None, ALU.is_equal)
                    v.tensor_scalar(hi_hot[:, s, 0, :], iota_lo[:, 0:NHI], hilo[:, 0, s:s + 1], pcol[:, 0:1],
                                    ALU.is_equal, ALU.mult)
                    v.tensor_scalar(hi_hot[:, s, 1, :], iota_lo[:, 0:NHI], hilo[:, 0, s:s + 1], float(s),
                                    ALU.is_equal, ALU.mult).then_inc(hot_ready, 1)
                dve.wait_ge(inv_psum, run + 1)
                chain(v.tensor_copy(at_pos[:, :, :].rearrange("p k c -> p (k c)"), TB[1][:, 0:2 * NHI]))
                chain(v.scalar_tensor_tensor(row_f[:, 0, :], at_pos[:, 1, :], float(P), at_pos[:, 0, :], ALU.mult, ALU.add))
                chain(v.tensor_scalar(row_f[:, 1, :], row_f[:, 0, :], float(NTOK), -float(NTOK), ALU.is_ge, ALU.mult))
                v.tensor_copy(scatter_all[:, :], row_f[:, 0, :])
                v.tensor_tensor(gather_all[:, :], row_f[:, 0, :], row_f[:, 1, :], ALU.add).then_inc(index_ready, 1)

            def experts(run):
                def take_rows(i, s):
                    dve.wait_ge(gt_psum, nth(i, s, base=run * NB))
                    v.tensor_copy(xft[s][:, :], TA[s][:, :]).then_inc(gt_ready, 1)

                def give_rows(i, s, first):
                    dve.wait_ge(eo_psum, nth(i, s, base=run * NB))
                    if not first:
                        dve.wait_ge(scattered[s], i * (16 * GT) + run * 16 * GT * (NB // 2))
                    v.tensor_copy(expert_out[s][:, :, :].rearrange("p a b -> p (a b)"), TB[s][:, :]).then_inc(eo_ready, 1)

                take_rows(0, 0)
                take_rows(0, 1)
                give_rows(0, 0, True)
                take_rows(1, 0)
                give_rows(0, 1, True)
                with dve.Fori(1, NB // 2 - 1) as i:
                    take_rows(i, 1)
                    give_rows(i, 0, False)
                    take_rows(i + 1, 0)
                    give_rows(i, 1, False)
                take_rows(NB // 2 - 1, 1)
                give_rows(NB // 2 - 1, 0, False)
                give_rows(NB // 2 - 1, 1, False)

            def combine(i, run, finish):
                tok = [0, 0]
                for q in range(2):
                    tok[q] = MARK(v.tensor_copy(w_stage[q][:, :, :], w_slot[:, :, bass.ds(i * (2 * GT) + q * GT, GT)]))
                    MARK(v.tensor_copy(xw[q][:, :, :], x_all[:, bass.ds(i * (2 * GT) + q * GT, GT), :]))
                for q in range(2):
                    tok[q] = step.n
                step.after(tok[1])
                for s in range(SLOTS):
                    for q in range(2):
                        if s == 0:
                            dve.wait_ge(y_loaded[q], i * 32 + (32 + run * 32 * NI))
                        else:
                            step.after(tok[q])
                        dst, add = (sm, xw) if s == 0 else (xn, sm)
                        for t in range(GT):
                            ins = v.scalar_tensor_tensor(dst[q][:, t, :], y_in[q][:, s, t, :], w_stage[q][:, s, t:t + 1],
                                                         add[q][:, t, :], ALU.mult, ALU.add)
                        if s == 0:
                            tok[q] = MARK(ins)
                        else:
                            ins.then_inc(finish, 1)

            route(0)
            experts(0)

            with dve.Fori(0, NI) as i:
                step.loop(i, B_STEPS)
                combine(i, 0, y_used)
                for q in range(2):
                    dve.wait_ge(y_used, nth(i, q))
                ln_stats(lambda q: xn[q], 1.0)
                last = normalise(lambda q: x1[q], lambda q: xn[q], lambda q: nth(i, q, 0, B_LN, LN_B0))
                for q in range(2):
                    last[q].then_inc(ax_ready, 1)
                for q in range(2):
                    dve.wait_ge(sq_ready, nth(i, q))
                    v.tensor_reduce(nrm[q][:, :, :], sq[q][:, :, :].rearrange("p t (h d) -> p t h d", d=DH), AX.X, ALU.add)\
                        .then_inc(nrm_ready, 1)
                for q in range(2):
                    dve.wait_ge(scale_ready, nth(i, q))
                    v.tensor_tensor(vk[q][:, 0, :, :].rearrange("p t (h d) -> p t h d", h=H),
                                    v_sb[q][:, :, :].rearrange("p t (h d) -> p t h d", h=H),
                                    scl[q][:, :, H:2 * H].unsqueeze(3).broadcast_to([P, GT, H, DH]), ALU.mult)\
                        .then_inc(vk_ready, 1)
                for n in range(8):
                    r = n % 2
                    dve.wait_ge(proj_psum, i * 8 + (n + 1))
                    if n >= 2:
                        dve.wait_ge(feat_ready, i * 8 + (n - 1))
                    src = F[:, 2 * r:2 * r + 2, :]
                    dst = ang[r][:, :].rearrange("p (a b) -> p a b", a=2)
                    tok = MARK(v.tensor_scalar(dst, src, ROUND, ROUND, ALU.add, ALU.subtract))
                    step.after(tok)
                    v.tensor_tensor(dst, src, dst, ALU.subtract).then_inc(ang_ready, 1)
                    dve.wait_ge(ang_ready, i * 8 + (n + 1))
                    magnitude(ang_abs[r][:, :], ang[r][:, :]).then_inc(abs_ready, 1)
                for q in range(2):
                    dve.wait_ge(kv_psum, nth(i, q))
                    v.tensor_tensor(kvm[q][:, :, :, :].rearrange("p a j v -> p (a j) v"),
                                    TB[q][:, :].rearrange("p (a v) -> p a v", v=HPC * DH),
                                    kv_mask[:, :, :].rearrange("p a b -> p (a b)").unsqueeze(1)
                                    .broadcast_to([P, 4 * NJ, HPC * DH]), ALU.mult).then_inc(kvm_ready, 1)
                tok = [0, 0]
                for q in range(2):
                    tok[q] = MARK(v.tensor_scalar(scl[q][:, :, 0:H], scl[q][:, :, 0:H], 1.0 / M, None, ALU.mult))
                for q in range(2):
                    step.after(tok[q])
                    dve.wait_ge(numt_psum, nth(i, q))
                    zz = TB[q][:, :].rearrange("p (t h d) -> p t h d", t=GT, h=H)[:, :, :, 0]
                    tok[q] = MARK(v.tensor_tensor(zq[q][:, 0, :, :], zz, scl[q][:, :, 0:H], ALU.mult))
                for q in range(2):
                    step.after(tok[q])
                    tok[q] = MARK(v.tensor_scalar(zq[q][:, 1, :, :], zq[q][:, 0, :, :], 1e-6, None, ALU.max))
                for q in range(2):
                    step.after(tok[q])
                    tok[q] = MARK(v.reciprocal(zq[q][:, 2, :, :], zq[q][:, 1, :, :]))
                for q in range(2):
                    step.after(tok[q])
                    tok[q] = MARK(v.tensor_tensor(zq[q][:, 0, :, :], zq[q][:, 2, :, :], scl[q][:, :, 0:H], ALU.mult))
                for q in range(2):
                    step.after(tok[q])
                    v.tensor_tensor(x1b[q][:, :, :].rearrange("p t (h d) -> p t h d", h=H),
                                    TA[q][:, :].rearrange("p (t h d) -> p t h d", t=GT, h=H),
                                    zq[q][:, 0, :, :].unsqueeze(3).broadcast_to([P, GT, H, DH]), ALU.mult)\
                        .then_inc(att_ready, 1)
                for q in range(2):
                    dve.wait_ge(proj_out, nth(i, q))
                    v.tensor_tensor(xn[q][:, :, :].rearrange("p a b -> p (a b)"), xn[q][:, :, :].rearrange("p a b -> p (a b)"),
                                    TB[q][:, :], ALU.add).then_inc(xn_ready, 1)
                for q in range(2):
                    dve.wait_ge(xn_ready, nth(i, q, base=NG))
                prepare(i, 1, lambda q: nth(i, q, 1, B_LN, LN_B0))
            step.end(NI)

            route(1)
            experts(1)
            combine(0, 1, out_ready)
            with dve.Fori(1, NI) as i:
                step.loop(i, C_STEPS, 1)
                for q in range(2):
                    dve.wait_ge(out_stored[q], i * 16)
                combine(i, 1, out_ready)
            step.end(NI)

        @block.tensor
        def _(pe):
            mm = nc.tensor.matmul
            tr = nc.tensor.transpose

            pe.wait_ge(weights_in, 16 * 14)
            pe.wait_ge(consts_ready, 1)
            pe.wait_ge(setup_dve, 2)
            pe.wait_ge(w_split_ready, 1)
            for c in range(FC):
                tr(F[:, 0, :].bitcast(BF16)[:, c * P:(c + 1) * P], w1_split[:, c, :], identb[:, :])
                tr(F[:, 1, c * P:(c + 1) * P], w2_nat[:, c * P:(c + 1) * P], ident[:, :])
                tr(F[:, 2, c * P:(c + 1) * P], w_nat[:, c, :], ident[:, :])
            tr(F[:, 3, 0:NE], wr_nat[:, :], ident[0:NE, 0:NE])
            mm(F[:, 3, P:P + M], rf_rep[:, :, :].rearrange("m h d -> m (h d)"), ident[0:M, 0:M], start=True, stop=True)\
                .then_inc(setup_pe, 1)
            pe.wait_ge(setup_dve, 3)
            rfb = rf_block[:, :, :].rearrange("p h m -> p (h m)")
            mm(TA[0][:, :], w_nat[:, 0, :], rfb, start=True, stop=True)
            mm(TA[1][:, :], w_nat[:, 1, :], rfb, start=True, stop=True).then_inc(setup_pe, 1)
            pe.wait_ge(weights_ready, 1)

            def four_transposes(dst, src, signal):
                for t in range(GT):
                    ins = tr(dst[:, t * P:(t + 1) * P], src(t), ident[:, :])
                ins.then_inc(signal, 1)

            def prepare(i, run):
                for q in range(2):
                    pe.wait_ge(xf_ready, nth(i, q, base=PREP[run]))
                    four_transposes(TA[q], lambda t: xf[q][:, t, :], xft_psum)
                for q in range(2):
                    pe.wait_ge(xft_ready, nth(i, q, base=PREP[run]))
                    for t in range(GT):
                        ins = mm(TB[q][:, t * NE:(t + 1) * NE], xft[q][:, t * P:(t + 1) * P], wrt[:, :], start=True, stop=True)
                    ins.then_inc(logit_psum, 1)

            with pe.Fori(0, NI) as i:
                for q in range(2):
                    pe.wait_ge(qsplit_ready, nth(i, q))
                    for t in range(GT):
                        ins = tr(TA[q][:, :].bitcast(BF16)[:, t * P:(t + 1) * P], q_split[q][:, t, :], identb[:, :])
                    ins.then_inc(qt_psum, 1)
                for q in range(2):
                    pe.wait_ge(qt_ready, nth(i, q))
                    for c in range(FC):
                        if q == 1:
                            if c % 2 == 0:
                                pe.wait_ge(h_ready, i * 4 + (c // 2 + 1))
                        ins = mm(F[:, c, :], w1k[:, c * P:(c + 1) * P], q_t[q][:, :], start=True, stop=True)
                        if c % 2:
                            ins.then_inc(h_psum, 1)
                for q in range(2):
                    pe.wait_ge(h_ready, i * 4 + (2 * q + 2))
                    for t in range(GT):
                        for c in range(FC):
                            ins = mm(TB[q][:, t * P:(t + 1) * P], hid[q][:, c, t * P:(t + 1) * P], w2t[:, c, :],
                                     start=(c == 0), stop=(c == FC - 1))
                    ins.then_inc(ffn_psum, 1)
                prepare(i, 0)

            def route(run):
                pe.wait_ge(picked_ready, run + 1)
                chosen = picked[:, :, :].rearrange("p e t -> p (e t)")
                for h in range(2):
                    ins = mm(TB[0][:, h:h + 1], chosen[:, h * P:(h + 1) * P], ones_row[:, 0:1], start=True, stop=True)
                ins.then_inc(count_psum, 1)
                pe.wait_ge(count_ready, run + 1)
                n = NE * NT
                mm(TA[0][:, 0:n], after_tri[:, P:2 * P], chosen, start=True, stop=False)
                mm(TA[0][:, 0:n], count_b[:, 0, :], after_tri[:, P:3 * P], start=False, stop=False)
                mm(TA[0][:, 0:n], count_b[:, 1, :], after_tri[:, 0:2 * P], start=False, stop=True).then_inc(pos_psum, 1)
                for s in range(NTS):
                    pe.wait_ge(hot_ready, run * NTS + s + 1)
                    ins = mm(TB[1][:, 0:2 * NHI], lo_hot[:, s, :], hi_hot[:, s, :, :].rearrange("p k c -> p (k c)"),
                             start=(s == 0), stop=(s == NTS - 1))
                ins.then_inc(inv_psum, 1)

            def experts(run):
                gathers = run * 16 * GT * (NB // 2)
                pe.wait_ge(index_ready, run + 1)

                def turn(i, s):
                    pe.wait_ge(gathered_in[s], i * (16 * GT) + (16 * GT + gathers))
                    four_transposes(TA[s], lambda t: gathered[s][:, t, :], gt_psum)

                def up(i, s, e):
                    pe.wait_ge(gt_ready, nth(i, s, base=run * NB))
                    for c in range(EC):
                        ins = mm(F[:, c, :], ew1_sb[e][:, c * P:(c + 1) * P], xft[s][:, :], start=True, stop=True)
                        if c % 2:
                            ins.then_inc(eh_psum, 1)

                def down(i, s, e):
                    pe.wait_ge(eh_ready, i * 4 + (2 * s + 2 + run * 2 * NB))
                    for t in range(GT):
                        for c in range(EC):
                            ins = mm(TB[s][:, t * P:(t + 1) * P], hid[s][:, c, t * P:(t + 1) * P], ew2_sb[e][:, c, :],
                                     start=(c == 0), stop=(c == EC - 1))
                    ins.then_inc(eo_psum, 1)

                def pair(k):
                    for e in range(2):
                        i = k * 2 + e
                        pe.wait_ge(ew_loaded[e], k * 32 + (32 + run * 32 * (NE // 2)))
                        for s in range(2):
                            if e == 0 and s == 0:
                                turn(i, s)
                            up(i, s, e)
                            if not (e == 1 and s == 1):
                                turn(i + s, 1 - s)
                            down(i, s, e)
                with pe.Fori(0, NE // 2) as k:
                    pair(k)

            route(0)
            experts(0)

            with pe.Fori(0, NI) as i:
                for q in range(2):
                    pe.wait_ge(ax_ready, nth(i, q))
                    four_transposes(TA[q], lambda t: x1[q][:, t, :], axt_psum)
                wqkv = wqkv_t[:, :, :].rearrange("p a b -> p (a b)")
                for q in range(2):
                    pe.wait_ge(axt_ready, nth(i, q))
                    if q == 1:
                        pe.wait_ge(qkv_used, nth(i, 0))
                    for t in range(GT):
                        ins = mm(F[:, t, 0:3 * C], xft[q][:, t * P:(t + 1) * P], wqkv, start=True, stop=True)
                    ins.then_inc(qkv_psum, 1)
                pe.wait_ge(qkv_used, nth(i, 1))
                for q in range(2):
                    for kind in range(2):
                        for u in range(2):
                            n = q * 4 + kind * 2 + u
                            if n >= 2:
                                pe.wait_ge(ang_ready, i * 8 + (n - 1))
                            for b in range(2):
                                if kind == 0:
                                    t = 2 * u + b
                                    ins = mm(F[:, 2 * u + b, :], xft[q][:, t * P:(t + 1) * P], wkf[:, :], start=True, stop=True)
                                else:
                                    j = 2 * u + b
                                    ins = mm(F[:, 2 * u + b, :], wqf[:, j * P:(j + 1) * P], xft[q][:, :], start=True, stop=True)
                            ins.then_inc(proj_psum, 1)
                for q in range(2):
                    pe.wait_ge(feat_ready, i * 8 + (q * 4 + 2))
                    pe.wait_ge(vk_ready, nth(i, q))
                    pe.wait_ge(krep_ready, nth(i, q))
                    VW = HPC * DH
                    for a in range(2):
                        for t in range(GT):
                            for j in range(NJ):
                                ins = mm(TA[q][j * VW:(j + 1) * VW, a * 2 * P:(a + 1) * 2 * P].rearrange("p (s c) -> p s c", s=2),
                                         vk[q][:, a, t, j * VW:(j + 1) * VW],
                                         kfeat[q][:, t, :, j * P:(j + 1) * P],
                                         start=(t == 0), stop=(t == GT - 1), tile_position=(0, j * VW))
                    ins.then_inc(kvt_psum, 1)
                for q in range(2):
                    pe.wait_ge(kvt_ready, nth(i, q))
                    four_transposes(TB[q], lambda t: kvt[q][:, t, :], kv_psum)
                for q in range(2):
                    pe.wait_ge(kvm_ready, nth(i, q))
                    pe.wait_ge(feat_ready, i * 8 + (q * 4 + 4))
                    VW = HPC * DH
                    for a, dst in ((0, TA[q]), (1, TB[q])):
                        for sc in range(2):
                            for j in range(NJ):
                                ins = mm(dst[j * VW:(j + 1) * VW, :], kvm[q][:, 2 * a + sc, j, :], qfeat[q][:, sc, j, :],
                                         start=(sc == 0), stop=(sc == 1), tile_position=(0, j * VW))
                    ins.then_inc(num_psum, 1)
                for q in range(2):
                    pe.wait_ge(num_ready, nth(i, q))
                    for t in range(GT):
                        tr(TA[q][:, t * P:(t + 1) * P], sm[q][:, t, :], ident[:, :])
                    four_transposes(TB[q], lambda t: ct[q][:, t, :], numt_psum)
                for q in range(2):
                    pe.wait_ge(att_ready, nth(i, q))
                    four_transposes(TA[q], lambda t: x1b[q][:, t, :], att_t_psum)
                for q in range(2):
                    pe.wait_ge(att_t_ready, nth(i, q))
                    for t in range(GT):
                        ins = mm(TB[q][:, t * P:(t + 1) * P], att_t[q][:, t * P:(t + 1) * P], wot[:, :], start=True, stop=True)
                    ins.then_inc(proj_out, 1)
                prepare(i, 1)
            route(1)
            experts(1)


_INS = ["L0_attn_a_x", "L0_attn_a_w1", "L0_attn_a_b1", "L0_attn_a_w2", "L0_attn_a_b2", "L0_attn_a_gamma1", "L0_attn_a_beta1",
        "L0_attn_a_gamma2", "L0_attn_a_beta2", "L0_attn_b_wq", "L0_attn_b_wk", "L0_attn_b_wv", "L0_attn_b_wo",
        "L0_attn_b_rf", "L0_ffn_Wr", "L0_ffn_W1", "L0_ffn_W2"]


def kernel(**inputs):
    import numpy as np
    import concourse.bacc as bacc
    from concourse.bass_utils import run_bass_kernel_spmd

    nc = bacc.Bacc("TRN2", target_bir_lowering=False, num_devices=1)
    arrays, args = {}, []
    for name in _INS:
        a = np.ascontiguousarray(inputs[name])
        if name == "L0_attn_a_x":
            shape = a.shape
            a = a.reshape(-1, a.shape[-1])
        arrays[f"in_{name}"] = a
        args.append(nc.dram_tensor(f"in_{name}", a.shape, mybir.dt.from_np(a.dtype), kind="ExternalInput").ap())
    rows_out = (shape[0] * shape[1], shape[2])
    args.append(nc.dram_tensor("out_dram", rows_out, F32, kind="ExternalOutput").ap())
    build(nc, *args)
    r = run_bass_kernel_spmd(nc, [arrays], core_ids=[0])
    return r.results[0]["out_dram"].reshape(shape)
```

```python
import math
from contextlib import ExitStack

import concourse.bass as bass
from concourse import mybir

ALU = mybir.AluOpType
ACT = mybir.ActivationFunctionType
AX = mybir.AxisListType
F32 = mybir.dt.float32
BF16 = mybir.dt.bfloat16
I32 = mybir.dt.int32

P = 128
GT = 4
GN = GT * P
EPS = 1e-5
ROUND = 1.5 * 2.0 ** 23
TURN = 1.0 / (2.0 * math.pi)
TWO_PI = 6.283185005187988
HALF_PI = math.pi / 2


def nth(i, q, base=0):
    return i * 2 + (q + 1 + base)


class Batch:

    def __init__(self, i, off):
        self.i, self.off, self.q = i, off, off % 2

    def plus(self, d):
        return Batch(self.i, self.off + d)

    def n(self, base=0):
        return self.i * 2 + (self.off + 1 + base)

    def k(self, k, per):
        return self.i * (2 * per) + (self.off * per + k + 1)

    def turns(self, each=1, base=0):
        return self.i * each + ((self.off // 2 + 1) * each + base)

    def tile(self):
        return self.i * (2 * GT) + self.off * GT


class Steps:

    def __init__(self, eng, sem):
        self.eng, self.sem, self.base, self.n, self.i, self.per = eng, sem, 0, 0, 0, 0

    def loop(self, i, per, first=0):
        self.base += self.n - first * per
        self.i, self.per, self.n = i, per, 0

    def end(self, end):
        assert self.n == self.per, ("marks in this loop", self.n, self.per)
        self.base += self.per * end
        self.i, self.per, self.n = 0, 0, 0

    def mark(self, instruction):
        instruction.then_inc(self.sem, 1)
        self.n += 1
        return self.n

    def after(self, token):
        self.eng.wait_ge(self.sem, self.i * self.per + (self.base + token))


def build(nc, x_in, fw1, fb1, fw2, fb2, gamma1, beta1, gamma2, beta2, wq, wk, wv, wo, rf, wr, ew1, ew2, out):
    NTOK, C = x_in.shape
    NT = NTOK // P
    NG = NTOK // GN
    NI = NG // 2
    FF, NQ = fw1.shape
    FC = FF // P
    M, DH = rf.shape
    H = C // DH
    NE = wr.shape[0]
    EF = ew1.shape[2]
    EC = EF // P
    SLOTS = 2
    NPOS = SLOTS * NTOK
    NB = NPOS // GN
    BPE = NB // NE
    NTS = SLOTS * NT
    NHI = NPOS // P
    HPC = P // M
    NJ = H // HPC
    assert C == P and FC == 4 and EC == 4 and NJ == 4 and BPE == 2 and NI == 4 and NTS == 64 and NQ == 16

    xf_dram = nc.dram_tensor("xf_dram", [NTOK, C], F32).ap()
    y_dram = nc.dram_tensor("y_dram", [NPOS, C], F32).ap()

    def rows(ap, first_tile, tiles=GT):
        return ap[bass.ds(first_tile * P, tiles * P), :].rearrange("(t p) c -> p t c", p=P)

    with ExitStack() as ctx:
        def sb(name, shape, dt=F32):
            return ctx.enter_context(nc.sbuf_tensor(name, shape, dt))

        def ps(name, shape, dt=F32):
            return ctx.enter_context(nc.psum_tensor(name, shape, dt))

        def sem(name):
            return ctx.enter_context(nc.semaphore(name))

        ident = sb("ident", [P, P])
        identb = sb("identb", [P, P], BF16)
        after_tri = sb("after_tri", [P, 3 * P], BF16)
        ones_row = sb("ones_row", [P, P], BF16)
        iota_lo = sb("iota_lo", [P, P], BF16)
        iota_i = sb("iota_i", [P, P], I32)
        pcol_i = sb("pcol_i", [P, 1], I32)
        pcol = sb("pcol", [P, 1])
        half_pi = sb("half_pi", [P, 1])
        neg_half = sb("neg_half", [P, GT])
        kv_mask = sb("kv_mask", [P, HPC, DH])
        head_mask = sb("head_mask", [P, H])
        gb = sb("gb", [P, 5, C])
        G1, BE1, G2, BE2, B2 = range(5)
        w1_nat = sb("w1_nat", [P, FC, NQ + 1])
        w1_split = sb("w1_split", [P, FC, P], BF16)
        w1k = sb("w1k", [P, FF], BF16)
        w2t = sb("w2t", [P, FC, C])
        wr_nat = sb("wr_nat", [NE, C])
        wrt = sb("wrt", [C, NE])
        wqkv_t = sb("wqkv_t", [P, 3, C])
        wot = sb("wot", [P, C])
        rf_nat = sb("rf_nat", [M, DH])
        rf_rep = sb("rf_rep", [M, H, DH])
        rf_block = sb("rf_block", [P, H, M])
        wqf = sb("wqf", [P, H * M])
        wkf = sb("wkf", [P, H * M])
        ew1_sb = [sb(f"ew1_{s}", [P, EF]) for s in range(2)]
        ew2_sb = [sb(f"ew2_{s}", [P, EC, C]) for s in range(2)]

        x_all = sb("x_all", [P, NT, C])
        logits = sb("logits", [P, NE, NT])

        def two(name, shape, dt=F32):
            return [sb(f"{name}{q}", shape, dt) for q in range(2)]
        pairs = [two(f"pair{n}_", [P, 2, GT, C]) for n in range(3)]

        def halves(n):
            return [[pairs[n][q][:, h, :, :] for q in range(2)] for h in range(2)]
        (yt, rt), (x1, x1b) = halves(1), halves(2)
        norms = {k: {name: two(f"{name}_{k}", shape) for name, shape in (
            ("stats", [P, GT, 6]), ("mv", [P, GT, 2]), ("var", [P, GT]), ("rstd", [P, GT]), ("neg_mean", [P, GT]), ("shift", [P, GT]))}
            for k in "xasn"}
        ct = two("ct", [P, GT, C])
        sm = two("sm", [P, GT, C])
        q_ang = two("q_ang", [P, 2, GT, NQ])
        qc = two("qc", [P, GT, NQ])
        q_rest = two("q_rest", [P, 2, GT, NQ])
        q_split = two("q_split", [P, GT, P], BF16)
        q_t = two("q_t", [P, GN], BF16)
        hid = two("hid", [P, FC, GN])
        w2_nat, w_nat = hid[1][:, 0, :], hid[1][:, 1, :].rearrange("p (n c) -> p n c", n=4)
        xn = two("xn", [P, GT, C])
        xf = two("xf", [P, GT, C])
        xft = two("xft", [P, GN])
        gathered, expert_out = yt, rt
        gather_idx = two("gather_idx", [P, GT], I32)
        scatter_idx = two("scatter_idx", [P, GT], I32)
        y_idx = two("y_idx", [P, SLOTS, GT], I32)
        y_in = two("y_in", [P, SLOTS, GT, C])
        w_stage = two("w_stage", [P, SLOTS, GT])
        top = sb("top", [P, SLOTS, NT])
        eq = sb("eq", [P, NE, NT])
        order_key = sb("order_key", [P, NE, NT])
        key_max = sb("key_max", [P, NT])
        masked = sb("masked", [P, NE, NT])
        pick = sb("pick", [P, SLOTS, NE, NT])
        picked = sb("picked", [P, NE, NT], BF16)
        first_bonus = sb("first_bonus", [P, NE, NT])
        count_b = sb("count_b", [P, 2, P], BF16)
        posf = sb("posf", [P, NTS])
        posi = sb("posi", [P, 3, NTS], I32)
        hilo = sb("hilo", [P, 2, NTS])
        gate = sb("gate", [P, 3, NT])
        w_slot = sb("w_slot", [P, SLOTS, NT])
        at_pos = sb("at_pos", [P, 2, NHI])
        row_f = sb("row_f", [P, 2, NHI])
        scatter_all = sb("scatter_all", [P, NHI], I32)
        gather_all = sb("gather_all", [P, NHI], I32)
        kfeat = two("kfeat", [P, GT, 2, H * M])
        qfeat = two("qfeat", [P, 2, NJ, GN])
        lo_hot = kfeat[0][:].rearrange("p a b c -> p (a b c)").bitcast(BF16).rearrange("p (s c) -> p s c", c=P)
        hi_hot = qfeat[0][:].rearrange("p a b c -> p (a b c)").bitcast(BF16).rearrange("p (s k c) -> p s k c", k=2, c=NHI)
        hi_one = kfeat[1][:].rearrange("p a b c -> p (a b c)").bitcast(BF16)[:, 0:NTS * NHI].rearrange("p (s c) -> p s c", c=NHI)
        xb_all = kfeat[0][:].rearrange("p a b c -> p (a b c)").rearrange("p (t c) -> p t c", c=C)
        y_all = [kfeat[q][:].rearrange("p t s (i c) -> p (t s i c)", c=C)
                 .rearrange("p (s i t c) -> p s i t c", s=SLOTS, t=GT, c=C) for q in range(2)]
        ang = [pairs[1][q][:, :, :, :].rearrange("p a b c -> p (a b c)") for q in range(2)]
        ang_abs = [pairs[2][q][:, :, :, :].rearrange("p a b c -> p (a b c)") for q in range(2)]
        vk = pairs[0]
        sum0, xh, ax = ct[0], sm, ct[1]
        xt = xft
        sq = hid[0][:, 0:2, :].rearrange("p a (b c) -> p (a b) c", c=2 * C)
        v_sb = hid[0][:, 2, :].rearrange("p (t c) -> p t c", t=GT)
        kvt = [hid[0][:, 3, :].rearrange("p (a c) -> p a c", a=4), hid[1][:, 0, :].rearrange("p (a c) -> p a c", a=4)]
        num_s, den_s, att = [hid[1][:, n, :].rearrange("p (t c) -> p t c", t=GT) for n in (1, 2, 3)]
        att_t = sb("att_t", [P, GN])
        xrt = sb("xrt", [P, GN])
        nrm = sb("nrm", [P, GT, 2 * H])
        scl = sb("scl", [P, GT, 2 * H])
        q_scale = two("q_scale", [P, GT, H])
        kvm = sb("kvm", [P, 4, NJ, HPC * DH])
        zq = sb("zq", [P, 3, GT, H])
        ln = {w: (sb(f"stats_{w}", [P, GT, 6]), sb(f"mv_{w}", [P, GT, 2]), sb(f"var_{w}", [P, GT]), sb(f"neg_mean_{w}", [P, GT]),
                  sb(f"rstd_{w}", [P, GT]), sb(f"shift_{w}", [P, GT])) for w in "ht"}

        F = ps("F", [P, 4, GN])
        TA = [ps(f"TA{q}", [P, GN]) for q in range(2)]
        TB = [ps(f"TB{q}", [P, GN]) for q in range(2)]
        (T_A, H_A), (T_B, H_B) = TA, TB

        weights_in = sem("weights_in")
        consts_ready = sem("consts_ready")
        pool_steps = sem("pool_steps")
        dve_steps = sem("dve_steps")
        pool_held, dve_held = sem("pool_held"), sem("dve_held")
        setup_dve = sem("setup_dve")
        setup_pe = sem("setup_pe")
        w_split_ready = sem("w_split_ready")
        weights_ready = sem("weights_ready")
        x_loaded = [sem(f"x_loaded{n}") for n in range(2)]
        N = {f"{name}_{k}": sem(f"{name}_{k}") for k in "xasn" for name in ("var", "rstd")}
        turns_ready, angle_ready, cos_ready = sem("turns_ready"), sem("angle_ready"), sem("cos_ready")
        x1_ready, x1b_ready, xb_ready, x1b_used = sem("x1_ready"), sem("x1b_ready"), sem("xb_ready"), sem("x1b_used")
        qangle_ready, qcos_ready, qsplit_ready = sem("qangle_ready"), sem("qcos_ready"), sem("qsplit_ready")
        qt_psum, qt_ready = sem("qt_psum"), sem("qt_ready")
        h_psum, h_ready = sem("h_psum"), sem("h_ready")
        ffn_psum = sem("ffn_psum")
        xn_ready, x_kept = sem("xn_ready"), sem("x_kept")
        xf_ready = sem("xf_ready")
        xf_stored = [sem(f"xf_stored{q}") for q in range(2)]
        xf_free = [sem(f"xf_free{q}") for q in range(2)]
        xft_psum, xft_ready, logit_psum, logit_ready = sem("xft_psum"), sem("xft_ready"), sem("logit_psum"), sem("logit_ready")
        gap_ready, gap_exp = sem("gap_ready"), sem("gap_exp")
        picked_ready, count_psum, count_ready, pos_psum = sem("picked_ready"), sem("count_psum"), sem("count_ready"), sem("pos_psum")
        hilo_ready, lo_ready, hi_one_ready, hi_row_ready, hi_col_ready = (
            sem(n) for n in ("hilo_ready", "lo_ready", "hi_one_ready", "hi_row_ready", "hi_col_ready"))
        inv_psum, index_ready = sem("inv_psum"), sem("index_ready")
        ew_loaded = [sem(f"ew_loaded{s}") for s in range(2)]
        gathered_in = [sem(f"gathered_in{s}") for s in range(2)]
        gt_psum, gt_ready, eh_psum, eh_ready, eo_psum, eo_ready = (
            sem("gt_psum"), sem("gt_ready"), sem("eh_psum"), sem("eh_ready"), sem("eo_psum"), sem("eo_ready"))
        scattered = [sem(f"scattered{s}") for s in range(2)]
        y_loaded = [sem(f"y_loaded{b}") for b in range(NG)]
        y_gathered = [sem(f"y_gathered{q}") for q in range(2)]
        out_ready = sem("out_ready")
        out_stored = sem("out_stored")
        S = {name: sem("att_" + name) for name in (
            "var_h", "rstd_h", "var_t", "rstd_t", "ax", "axt_psum", "axt", "qkv_psum", "qkv_used", "nrm", "scale", "vk", "krep",
            "proj_psum", "ang", "abs", "sin", "feat", "kvt_psum", "kvt", "kv_psum", "kvm", "num_psum", "num", "numt_psum", "att",
            "attt_psum", "attt", "wo_psum", "xn", "xf", "xft_psum", "xft", "logit_psum", "logit_read", "kept_h", "kept_t", "wo_used")}
        b_xf_stored = [sem(f"att_xf_stored{q}") for q in range(2)]
        b_xf_free = [sem(f"att_xf_free{q}") for q in range(2)]
        eo_stored = [sem(f"eo_stored{s}") for s in range(2)]

        def run_pipeline(eng, work, steps=None, marks=0):
            work(Batch(0, -1), head=True, feat=False, tail=False, late=False)
            work(Batch(0, 0), head=True, feat=True, tail=False, late=False)
            work(Batch(0, 1), head=True, feat=True, tail=True, late=False)
            with eng.Fori(0, (NG - 4) // 2) as i:
                if steps:
                    steps.loop(i, marks)
                for off in (2, 3):
                    work(Batch(i, off), head=True, feat=True, tail=True, late=True)
            if steps:
                steps.end((NG - 4) // 2)
            work(Batch(0, NG - 2), head=True, feat=True, tail=True, late=True)
            work(Batch(0, NG - 1), head=False, feat=True, tail=True, late=True)
            work(Batch(0, NG), head=False, feat=False, tail=True, late=True)
            work(Batch(0, NG + 1), head=False, feat=False, tail=False, late=True)

        ATT_POOL, ATT_DVE = 6, 30
        A_DVE, A_POOL = 62, 4

        def run_pairs(eng, work, steps=None, marks=0):
            work(-1, head=True, tail=False, late=False)
            work(0, head=True, tail=True, late=False)
            with eng.Fori(1, NI - 1) as i:
                if steps:
                    steps.loop(i, marks, 1)
                work(i, head=True, tail=True, late=True)
            if steps:
                steps.end(NI - 1)
            work(NI - 1, head=False, tail=True, late=True)
            work(NI, head=False, tail=False, late=True)

        def pair_tiles(i, d, q):
            return bass.ds(i * (2 * GT) + (d * 2 * GT + q * GT), GT)

        HS = 4
        CPS = NTS // HS

        def hot_part(n):
            return slice(n * CPS, (n + 1) * CPS)

        block = ctx.enter_context(nc.Block())

        @block.sync
        def _(sp):
            loads = [(w1_nat[:, :, 0:NQ], fw1.rearrange("(c p) k -> p c k", p=P)),
                     (w2_nat[:, :], fw2), (wr_nat[:, :], wr), (rf_nat[:, :], rf)]
            loads += [(gb[:, n, :], v.partition_broadcast(P)) for n, v in enumerate((gamma1, beta1, gamma2, beta2, fb2))]
            loads += [(w_nat[:, n, :], w) for n, w in enumerate((wq, wk, wv, wo))]
            for q in range(2):
                sp.dma_start(x_all[:, q * GT:(q + 1) * GT, :], rows(x_in, q * GT)).then_inc(x_loaded[0], 16)
            for dst, src in loads:
                sp.dma_start(dst, src).then_inc(weights_in, 16)
            with nc.allow_non_contiguous_dma("b1 lies along the partitions once"):
                sp.dma_start(w1_nat[:, :, NQ:NQ + 1], fb1.rearrange("(c p k) -> p c k", p=P, k=1)).then_inc(weights_in, 16)

            for b in range(2, NG):
                sp.dma_start(x_all[:, b * GT:(b + 1) * GT, :], rows(x_in, b * GT)).then_inc(x_loaded[1], 16)

            def load_expert(e, s):
                sp.dma_start(ew1_sb[s][:, :], ew1[bass.ds(e, 1), :, :].rearrange("a c f -> c (a f)")).then_inc(ew_loaded[s], 16)
                sp.dma_start(ew2_sb[s][:, :, :], ew2[bass.ds(e, 1), :, :].rearrange("a (k p) c -> p (a k) c", p=P))\
                    .then_inc(ew_loaded[s], 16)

            for s in range(2):
                load_expert(s, s)
            for q in range(2):
                sp.sem_inc(xf_free[q], 1)

            with sp.Fori(0, NI) as i:
                for q in range(2):
                    sp.wait_ge(xf_ready, nth(i, q))
                    sp.dma_start(rows(xf_dram, (i * 2 + q) * GT), xf[q][:, :, :]).then_inc(xf_stored[q], 16)
                for q in range(2):
                    sp.wait_ge(xf_stored[q], i * 16 + 16)
                    sp.sem_inc(xf_free[q], 1)

            def experts(run):
                def store_sorted(i, s):
                    sp.wait_ge(eo_ready, nth(i, s))
                    sp.dma_start(rows(y_dram, i * (2 * GT) + s * GT), expert_out[s][:, :, :]).then_inc(eo_stored[s], 16)

                with sp.Fori(0, NE // 2 - 1) as i:
                    for e in range(2):
                        if run == 0:
                            for s in range(2):
                                store_sorted(i * 2 + e, s)
                        sp.wait_ge(eo_psum, i * 4 + (2 * e + 2 + run * NB))
                        load_expert(i * 2 + (e + 2), e)
                if run == 0:
                    for i in range(NE - 2, NE):
                        for s in range(2):
                            store_sorted(i, s)
                if run == 0:
                    for s in range(2):
                        sp.wait_ge(eo_psum, NB - 2 + 2 * s)
                        load_expert(s, s)
                if run == 1:
                    for s in range(2):
                        sp.wait_ge(scattered[s], 16 * GT * (NB // 2))

            experts(0)
            for q in range(2):
                sp.sem_inc(b_xf_free[q], 1)
            with sp.Fori(0, NI) as i:
                for q in range(2):
                    b = Batch(i, q)
                    sp.wait_ge(S["xf"], b.n())
                    sp.dma_start(rows(xf_dram, b.tile()), xf[q][:, :, :]).then_inc(b_xf_stored[q], 16)
                    sp.wait_ge(b_xf_stored[q], b.turns(16))
                    sp.sem_inc(b_xf_free[q], 1)

            experts(1)
            for b in range(NG):
                for s in range(SLOTS):
                    sp.dma_start(y_all[b % 2][:, s, b // 2, :, :], rows(y_dram, b * GT + s * NT)).then_inc(y_loaded[b], 16)
            with sp.Fori(0, NI) as i:
                for q in range(2):
                    sp.wait_ge(out_ready, nth(i, q))
                    sp.dma_start(rows(out, (i * 2 + q) * GT), x_all[:, bass.ds(i * (2 * GT) + q * GT, GT), :])\
                        .then_inc(out_stored, 16)
            sp.wait_ge(out_stored, 16 * NG)

        @block.gpsimd
        def _(pool):
            g = nc.gpsimd
            step = Steps(pool, pool_steps)
            m = [step.mark(g.memset(ident[:, :], 0.0)), step.mark(g.memset(after_tri[:, :], 1.0)),
                 step.mark(g.memset(kv_mask[:, :, :], 1.0)), step.mark(g.memset(head_mask[:, :], 1.0)),
                 step.mark(g.iota(iota_i[:, :], pattern=[[1, P]], base=0, channel_multiplier=0)),
                 step.mark(g.iota(pcol_i[:, :], pattern=[[0, 1]], base=0, channel_multiplier=1))]
            g.memset(ones_row[:, :], 1.0)
            g.memset(half_pi[:, :], HALF_PI)
            g.memset(neg_half[:, :], -0.5)
            for e in range(NE):
                g.memset(first_bonus[:, e, :], float(NE - e))
            for q in range(2):
                g.memset(q_split[q][:, :, 6 * NQ:], 0.0)
            last = g.memset(w1_split[:, :, 6 * NQ:], 0.0)
            m.append(step.mark(last))
            step.after(m[-1])
            g.affine_select(out=ident[:, :], in_=ident[:, :], compare_op=ALU.not_equal, fill=1.0, base=0,
                            pattern=[[-1, P]], channel_multiplier=1)
            for q in range(2):
                g.memset(q_split[q][:, :, 6 * NQ:6 * NQ + 3], 1.0)
            g.affine_select(out=after_tri[:, :], in_=after_tri[:, :], compare_op=ALU.is_gt, fill=0.0, base=-P,
                            pattern=[[1, 3 * P]], channel_multiplier=-1)
            lower_kv = g.affine_select(out=kv_mask[:, :, :], in_=kv_mask[:, :, :], compare_op=ALU.is_ge, fill=0.0, base=0,
                                       pattern=[[-M, HPC], [0, DH]], channel_multiplier=1)
            step.mark(lower_kv)
            t = step.mark(g.affine_select(out=head_mask[:, :], in_=head_mask[:, :], compare_op=ALU.is_ge, fill=0.0, base=0,
                                          pattern=[[-DH, H]], channel_multiplier=1))
            step.after(t)
            g.affine_select(out=kv_mask[:, :, :], in_=kv_mask[:, :, :], compare_op=ALU.is_ge, fill=0.0, base=M - 1,
                            pattern=[[M, HPC], [0, DH]], channel_multiplier=-1)
            g.affine_select(out=head_mask[:, :], in_=head_mask[:, :], compare_op=ALU.is_ge, fill=0.0, base=DH - 1,
                            pattern=[[DH, H]], channel_multiplier=-1).then_inc(consts_ready, 1)

            def first_block(i, head, tail, late):
                def root(k, d, shift=False):
                    n = norms[k]
                    toks = []
                    for q in range(2):
                        pool.wait_ge(N["var_" + k], nth(i, q, 2 * d))
                        ins = g.tensor_tensor(n["rstd"][q][:, :], n["var"][q][:, :], neg_half[:, :], ALU.pow)
                        if not shift:
                            ins.then_inc(N["rstd_" + k], 1)
                        else:
                            step.after(step.mark(ins))
                            g.tensor_tensor(n["shift"][q][:, :], n["neg_mean"][q][:, :], n["rstd"][q][:, :], ALU.mult)\
                                .then_inc(N["rstd_" + k], 1)

                if head:
                    root("x", 1, True)
                if late:
                    root("n", -1, True)
                if head:
                    root("a", 1)
                if tail:
                    root("s", 0)
                if head:
                    if not tail:
                        pool.wait_ge(weights_in, 16 * 14)
                    for q in range(2):
                        pool.wait_ge(x1_ready, nth(i, q, 2))
                        if tail:
                            pool.wait_ge(x1b_used, nth(i, q))
                        g.tensor_tensor(x1b[q][:, :, :], x1[q][:, :, :], gb[:, B2, :].unsqueeze(1).broadcast_to([P, GT, C]),
                                        ALU.add).then_inc(x1b_ready, 1)
                if head and not tail:
                    pool.wait_ge(x_loaded[1], 16 * (NG - 2))
                    for b in range(NG):
                        t = slice(b * GT, (b + 1) * GT)
                        ins = g.tensor_tensor(xb_all[:, t, :], x_all[:, t, :], gb[:, BE2, :].unsqueeze(1).broadcast_to([P, GT, C]), ALU.add)
                    ins.then_inc(xb_ready, 1)

            run_pairs(pool, first_block, step, A_POOL)

            def experts(run):
                def issue_gather(s):
                    pool.sem_inc(pool_held, 1)
                    for t in range(GT):
                        g.indirect_dma_start(gathered[s][:, t, :], None, xf_dram[:, :],
                                             bass.IndirectOffsetOnAxis(gather_idx[s][:, t:t + 1], 0))\
                            .then_inc(gathered_in[s], 16)

                def issue_scatter(s):
                    pool.sem_inc(pool_held, 1)
                    for t in range(GT):
                        g.indirect_dma_start(y_dram[:, :], bass.IndirectOffsetOnAxis(scatter_idx[s][:, t:t + 1], 0),
                                             expert_out[s][:, t, :], None).then_inc(scattered[s], 16)

                for n in range(HS):
                    pool.wait_ge(hi_one_ready, run * HS + n + 1)
                    g.tensor_tensor(hi_hot[:, hot_part(n), 1, :], hi_one[:, hot_part(n), :],
                                    iota_lo[:, hot_part(n)].unsqueeze(2).broadcast_to([P, CPS, NHI]), ALU.mult).then_inc(hi_col_ready, 1)
                pool.wait_ge(index_ready, run + 1)
                for q in range(2):
                    pool.wait_ge((xf_stored, b_xf_stored)[run][q], 16 * NI)
                for s in range(2):
                    g_tok = step.mark(g.tensor_copy(gather_idx[s][:, :], gather_all[:, s * GT:(s + 1) * GT]))
                    step.after(g_tok)
                    issue_gather(s)

                def work(i, s, ahead):
                    if ahead:
                        pool.wait_ge(gt_psum, nth(i, s, base=run * NB))
                        pool.wait_ge(gathered_in[s], i * (16 * GT) + (16 * GT + run * 16 * GT * (NB // 2)))
                        pool.sem_inc(pool_held, 1)
                        tok = step.mark(g.tensor_copy(gather_idx[s][:, :], gather_all[:, bass.ds(i * (2 * GT) + (s + 2) * GT, GT)]))
                        step.after(tok)
                        issue_gather(s)
                    if run == 0:
                        return
                    if ahead != "first":
                        pool.wait_ge(scattered[s], i * (16 * GT))
                    pool.sem_inc(pool_held, 1)
                    tok = step.mark(g.tensor_copy(scatter_idx[s][:, :], scatter_all[:, bass.ds(i * (2 * GT) + s * GT, GT)]))
                    step.after(tok)
                    pool.wait_ge(eo_ready, nth(i, s, base=run * NB))
                    issue_scatter(s)

                for s in range(2):
                    work(0, s, "first")
                with pool.Fori(1, NB // 2 - 1) as i:
                    step.loop(i, 2 + 2 * run, 1)
                    for s in range(2):
                        work(i, s, True)
                step.end(NB // 2 - 1)
                for s in range(2):
                    work(NB // 2 - 1, s, False)

            experts(0)

            position = posi[:, 0, :].rearrange("p (s t) -> p s t", s=SLOTS)

            def y_indices(b):
                pool.sem_inc(pool_held, 1)
                return step.mark(g.tensor_copy(y_idx[b.q][:, :, :], position[:, :, bass.ds(b.tile(), GT)]))

            def y_gather(b, s):
                for t in range(GT):
                    g.indirect_dma_start(y_in[b.q][:, s, t, :], None, y_dram[:, :],
                                         bass.IndirectOffsetOnAxis(y_idx[b.q][:, s, t:t + 1], 0)).then_inc(y_gathered[b.q], 16)

            def inverse_root_of(w, b):
                _, _, var_w, neg_w, rstd_w, shift_w = ln[w]
                pool.wait_ge(S["var_" + w], b.n())
                tok = step.mark(g.tensor_tensor(rstd_w[:, :], var_w[:, :], neg_half[:, :], ALU.pow))
                step.after(tok)
                g.tensor_tensor(shift_w[:, :], neg_w[:, :], rstd_w[:, :], ALU.mult).then_inc(S["rstd_" + w], 1)

            for q in range(2):
                pool.wait_ge(eo_stored[q], 16 * (NB // 2))
            step.after(y_indices(Batch(0, 0)))
            for s in range(SLOTS):
                y_gather(Batch(0, 0), s)

            def attention_step(b, head, feat, tail, late):
                more = head and not (isinstance(b.i, int) and b.off == NG - 2)
                if late:
                    inverse_root_of("t", b.plus(-2))
                if more:
                    y = b.plus(2)
                    if feat:
                        pool.wait_ge(S["kept_h"], b.n())
                    tok = y_indices(y)
                    step.after(tok)
                    pool.sem_inc(pool_held, 1)
                    y_gather(y, 0)
                if feat:
                    pool.wait_ge(S["scale"], b.n())
                    pool.sem_inc(pool_held, 1)
                    g.tensor_copy(vk[b.q][:, 1, :, :].rearrange("p t (h d) -> p t h d", h=H),
                                  scl[:, :, H:2 * H].unsqueeze(3).broadcast_to([P, GT, H, DH])).then_inc(S["krep"], 1)
                if head:
                    inverse_root_of("h", b.plus(1))
                if more:
                    y_gather(y, 1)

            run_pipeline(pool, attention_step, step, ATT_POOL)
            experts(1)

        @block.scalar
        def _(act):
            a = nc.scalar.activation
            act.wait_ge(consts_ready, 1)

            def first_block(i, head, tail, late):
                def normalised(k, d, dst, src, signal):
                    for q in range(2):
                        act.wait_ge(N["rstd_" + k], nth(i, q, 2 * d))
                        if k == "n":
                            act.wait_ge(xf_free[q], i)
                        for t in range(GT):
                            ins = a(dst[q][:, t:t + 1, :], src(q, t), ACT.Identity, bias=norms[k]["shift"][q][:, t:t + 1],
                                    scale=norms[k]["rstd"][q][:, t:t + 1])
                        ins.then_inc(signal, 1)

                def relu(q):
                    for half in range(2):
                        act.wait_ge(h_psum, i * 4 + (2 * q + half + 1))
                        a(hid[q][:, 2 * half:2 * half + 2, :], F[:, 2 * half:2 * half + 2, :], ACT.Relu).then_inc(h_ready, 1)

                if tail:
                    for q in range(2):
                        act.wait_ge(qt_psum, nth(i, q))
                        a(q_t[q][:, :], TA[q][:, :].bitcast(BF16)[:, 0:GN], ACT.Copy).then_inc(qt_ready, 1)
                if tail:
                    relu(0)
                if head:
                    normalised("x", 1, yt, lambda q, t: x_all[:, bass.ds(i * (2 * GT) + (2 * GT + q * GT + t), 1), :], turns_ready)
                if tail:
                    relu(1)
                if head:
                    for q in range(2):
                        act.wait_ge(angle_ready, nth(i, q, 2))
                        a(ct[q][:, :, :], rt[q][:, :, :], ACT.Sin, bias=half_pi[:, 0:1], scale=-TWO_PI).then_inc(cos_ready, 1)
                if late:
                    normalised("n", -1, xf, lambda q, t: xn[q][:, t:t + 1, :], xf_ready)
                    for q in range(2):
                        a(x_all[:, pair_tiles(i, -1, q), :], xn[q][:, :, :], ACT.Copy).then_inc(x_kept, 1)
                    for q in range(2):
                        act.wait_ge(xft_psum, nth(i, q, -2))
                        a(xft[q][:, :], TA[q][:, :], ACT.Copy).then_inc(xft_ready, 1)
                if head:
                    for q in range(2):
                        act.wait_ge(qangle_ready, nth(i, q, 2))
                        a(qc[q][:, :, :], q_ang[q][:, 1, :, :], ACT.Sin, bias=half_pi[:, 0:1], scale=-TWO_PI).then_inc(qcos_ready, 1)

            act.wait_ge(x_loaded[0], 32)
            run_pairs(act, first_block)

            def route(run):
                act.wait_ge(gap_ready, run + 1)
                a(gate[:, 1, :], gate[:, 0, :], ACT.Exp).then_inc(gap_exp, 1)
                for n in range(HS):
                    act.wait_ge(hi_one_ready, run * HS + n + 1)
                    a(hi_hot[:, hot_part(n), 0, :], hi_one[:, hot_part(n), :], ACT.Copy, scale=pcol[:, 0:1]).then_inc(hi_row_ready, 1)

            def experts(run):
                def work(i, s):
                    for half in range(2):
                        act.wait_ge(eh_psum, i * 4 + (2 * s + half + 1 + run * 2 * NB))
                        a(hid[s][:, 2 * half:2 * half + 2, :], F[:, 2 * half:2 * half + 2, :], ACT.Gelu).then_inc(eh_ready, 1)

                with act.Fori(0, NB // 2) as i:
                    for s in range(2):
                        work(i, s)

            route(0)
            experts(0)
            def out_of_psum(ready, value, dst, src, signal):
                act.wait_ge(S[ready], value)
                a(dst, src, ACT.Copy).then_inc(S[signal], 1)

            def normalise(w, b, dst, src, signal):
                rstd_w, shift_w = ln[w][4:]
                act.wait_ge(S["rstd_" + w], b.n())
                for t in range(GT):
                    ins = a(dst[:, t, :], src[:, t, :], ACT.Identity, bias=shift_w[:, t:t + 1], scale=rstd_w[:, t:t + 1])
                ins.then_inc(S[signal], 1)

            def attention_step(b, head, feat, tail, late):
                h, t_, l_ = b.plus(1), b.plus(-1), b.plus(-2)

                def unit(bb, u):
                    kind, half, r = u // 2, u % 2, u % 2
                    if kind == 0:
                        dst = [kfeat[bb.q][:, 2 * half:2 * half + 2, sc, :] for sc in range(2)]
                    else:
                        dst = [qfeat[bb.q][:, sc, 2 * half:2 * half + 2, :] for sc in range(2)]
                    act.wait_ge(S["ang"], bb.k(u, 4))
                    a(dst[0], ang[r].rearrange("p (a b) -> p a b", a=2), ACT.Sin, scale=TWO_PI).then_inc(S["sin"], 1)
                    act.wait_ge(S["abs"], bb.k(u, 4))
                    a(dst[1], ang_abs[r].rearrange("p (a b) -> p a b", a=2), ACT.Sin, bias=half_pi[:, 0:1], scale=-TWO_PI)\
                        .then_inc(S["feat"], 1)

                if late:
                    normalise("t", l_, xf[l_.q], xn[l_.q], "xf")
                if feat:
                    act.wait_ge(S["nrm"], b.n())
                    a(scl[:, :, :], nrm[:, :, :], ACT.Exp, scale=-0.5).then_inc(S["scale"], 1)
                if tail:
                    act.wait_ge(S["num_psum"], t_.n())
                    a(num_s, T_A[:, :].rearrange("p (t c) -> p t c", t=GT), ACT.Copy)
                    a(den_s, T_B[:, :].rearrange("p (t c) -> p t c", t=GT), ACT.Copy).then_inc(S["num"], 1)
                if late:
                    out_of_psum("xft_psum", l_.n(), xrt[:, :], H_B[:, :], "xft")
                if feat:
                    unit(b, 1)
                    unit(b, 2)
                if head:
                    normalise("h", h, ax, xh[h.q], "ax")
                if feat:
                    out_of_psum("kvt_psum", b.n(), kvt[b.q], H_A[:, :].rearrange("p (a c) -> p a c", a=4), "kvt")
                if head:
                    out_of_psum("axt_psum", h.n(), xt[h.q][:, :], H_B[:, :], "axt")
                if feat:
                    unit(b, 3)
                if tail:
                    out_of_psum("attt_psum", t_.n(), att_t[:, :], T_A[:, :], "attt")
                if head:
                    for t in range(GT):
                        bank = (H_A, H_B)[t % 2]
                        act.wait_ge(S["qkv_psum"], h.k(t, 4))
                        a(sq[:, t, :], bank[:, 0:2 * C], ACT.Square)
                        a(v_sb[:, t, :], bank[:, 2 * C:3 * C], ACT.Copy).then_inc(S["qkv_used"], 1)
                    unit(h, 0)
                    a(x_all[:, bass.ds(h.tile(), GT), :], xh[h.q][:, :, :], ACT.Copy).then_inc(S["kept_h"], 1)
                if late:
                    a(x_all[:, bass.ds(l_.tile(), GT), :], xn[l_.q][:, :, :], ACT.Copy).then_inc(S["kept_t"], 1)

            run_pipeline(act, attention_step)
            route(1)
            experts(1)

        @block.vector
        def _(dve):
            v = nc.vector
            step = Steps(dve, dve_steps)
            MARK = step.mark

            dve.wait_ge(consts_ready, 1)
            v.tensor_copy(identb[:, :], ident[:, :]).then_inc(setup_dve, 1)
            v.tensor_copy(iota_lo[:, :], iota_i[:, :])
            v.tensor_copy(pcol[:, :], pcol_i[:, :])
            def split_weights():
                dve.wait_ge(weights_in, 16 * 14)
                v.tensor_copy(rf_rep[:, :, :], rf_nat[:, :].unsqueeze(1).broadcast_to([M, H, DH])).then_inc(setup_dve, 1)
                split = w1_split
                rest = q_rest[0][:, 0, :, :].rearrange("p a b -> p (a b)")
                rest = rest.rearrange("p (c k) -> p c k", c=FC)
                rest_b = posf[:, 0:FC].unsqueeze(2)
                wn, bn = w1_nat[:, :, 0:NQ], w1_nat[:, :, NQ:NQ + 1]
                k6 = 6 * NQ

                def cols(part, n=NQ):
                    return split[:, :, part * NQ:part * NQ + n]
                t = MARK(v.tensor_copy(cols(0), wn))
                MARK(v.tensor_copy(cols(3), wn))
                MARK(v.tensor_copy(cols(5), wn))
                t = MARK(v.tensor_copy(split[:, :, k6:k6 + 1], bn))
                step.after(t)
                MARK(v.tensor_tensor(rest, wn, cols(0), ALU.subtract))
                t = MARK(v.tensor_tensor(rest_b, bn, split[:, :, k6:k6 + 1], ALU.subtract))
                step.after(t)
                MARK(v.tensor_copy(cols(1), rest))
                MARK(v.tensor_copy(cols(4), rest))
                t = MARK(v.tensor_copy(split[:, :, k6 + 1:k6 + 2], rest_b))
                step.after(t)
                MARK(v.tensor_tensor(rest, rest, cols(1), ALU.subtract))
                t = MARK(v.tensor_tensor(rest_b, rest_b, split[:, :, k6 + 1:k6 + 2], ALU.subtract))
                step.after(t)
                v.tensor_copy(cols(2), rest)
                v.tensor_copy(split[:, :, k6 + 2:k6 + 3], rest_b).then_inc(w_split_ready, 1)

            def finish_weights():
                dve.wait_ge(setup_pe, 1)
                v.tensor_copy(w1k[:, :], F[:, 0, :].bitcast(BF16)[:, 0:FF])
                v.tensor_copy(w2t[:, :, :].rearrange("p a b -> p (a b)"), F[:, 1, :])
                v.tensor_copy(wqkv_t[:, :, :].rearrange("p a b -> p (a b)"), F[:, 2, 0:3 * C])
                v.tensor_copy(wot[:, :], F[:, 2, 3 * C:4 * C])
                v.tensor_copy(wrt[:, :], F[:, 3, 0:NE])
                v.scalar_tensor_tensor(rf_block[:, :, :], F[:, 3, P:P + M].unsqueeze(1).broadcast_to([P, H, M]), TURN,
                                       head_mask[:, :].unsqueeze(2).broadcast_to([P, H, M]), ALU.mult, ALU.mult)\
                    .then_inc(setup_dve, 1)
                dve.wait_ge(setup_pe, 2)
                v.tensor_copy(wqf[:, :], TA[0][:, :])
                v.tensor_copy(wkf[:, :], TA[1][:, :]).then_inc(weights_ready, 1)

            def magnitude(dst, src):
                return v.tensor_scalar(dst.bitcast(I32), src.bitcast(I32), 0x7FFFFFFF, None, ALU.bitwise_and)

            def first_block(i, head, tail, late):
                def ln_stats(k, src, scale, neg=False):
                    n = norms[k]
                    tok = []
                    for q in range(2):
                        for t in range(GT):
                            ins = v.bn_stats(n["stats"][q][:, t, :], src(q, t))
                        tok.append(MARK(ins))
                    for q in range(2):
                        step.after(tok[q])
                        dve.sem_inc(dve_held, 1)
                        for t in range(GT):
                            ins = v.bn_aggr(n["mv"][q][:, t, :], n["stats"][q][:, t, :])
                        tok[q] = MARK(ins)
                    for q in range(2):
                        step.after(tok[q])
                        if neg:
                            v.tensor_scalar(n["neg_mean"][q][:, :], n["mv"][q][:, :, 0], -1.0, None, ALU.mult)
                        v.tensor_scalar(n["var"][q][:, :], n["mv"][q][:, :, 1], EPS, scale, ALU.add, ALU.mult)\
                            .then_inc(N["var_" + k], 1)

                def scaled(k, mid, src, gamma_row, signal=None):
                    toks = []
                    for q in range(2):
                        for t in range(GT):
                            ins = v.scalar_tensor_tensor(mid[q][:, t, :], src[q][:, t, :], norms[k]["mv"][q][:, t, 0:1],
                                                         gb[:, gamma_row, :], ALU.subtract, ALU.mult)
                        if signal:
                            ins.then_inc(signal, 1)
                        else:
                            toks.append(MARK(ins))
                    return toks

                tok = [0, 0]
                if head and tail and not late:
                    dve.wait_ge(x_loaded[1], 16 * (NG - 2))
                if head:
                    ln_stats("x", lambda q, t: x_all[:, bass.ds(i * (2 * GT) + (2 * GT + q * GT + t), 1), :].rearrange("p a c -> p (a c)"),
                             (2 * math.pi) ** 2, True)
                if head and not tail:
                    split_weights()
                if late:
                    for q in range(2):
                        dve.wait_ge(xn_ready, nth(i, q, -2))
                    ln_stats("n", lambda q, t: xn[q][:, t, :], 1.0, True)
                if head:
                    for q in range(2):
                        dve.wait_ge(turns_ready, nth(i, q, 2))
                        tok[q] = MARK(v.tensor_scalar(rt[q][:, :, :], yt[q][:, :, :], ROUND, ROUND, ALU.add, ALU.subtract))
                    for q in range(2):
                        step.after(tok[q])
                        tok[q] = MARK(v.tensor_tensor(rt[q][:, :, :], yt[q][:, :, :], rt[q][:, :, :], ALU.subtract))
                    for q in range(2):
                        step.after(tok[q])
                        magnitude(rt[q][:, :, :], rt[q][:, :, :]).then_inc(angle_ready, 1)
                    cv = [ct[q][:, :, :].rearrange("p t (h d) -> p (t h) d", d=DH) for q in range(2)]
                    for q in range(2):
                        dve.wait_ge(cos_ready, nth(i, q, 2))
                    for d in range(1, DH):
                        for q in range(2):
                            if d > 1:
                                step.after(tok[q])
                            tok[q] = MARK(v.tensor_tensor(cv[q][:, :, d], cv[q][:, :, d], cv[q][:, :, d - 1], ALU.mult))
                    for q in range(2):
                        step.after(tok[q])
                        tok[q] = MARK(v.scalar_tensor_tensor(sm[q][:, :, :], yt[q][:, :, :], 2 * math.pi, ct[q][:, :, :],
                                                             ALU.mult, ALU.add))
                    for q in range(2):
                        step.after(tok[q])
                    ln_stats("a", lambda q, t: sm[q][:, t, :], 1.0)
                if tail:
                    for q in range(2):
                        dve.wait_ge(ffn_psum, nth(i, q))
                        dve.wait_ge(x1b_ready, nth(i, q))
                        tok[q] = MARK(v.tensor_tensor(x1b[q][:, :, :].rearrange("p a b -> p (a b)"), TB[q][:, :],
                                                      x1b[q][:, :, :].rearrange("p a b -> p (a b)"), ALU.add))
                    for q in range(2):
                        step.after(tok[q])
                    ln_stats("s", lambda q, t: x1b[q][:, t, :], 1.0)
                if head:
                    toks = scaled("a", sm, sm, G1)
                    for q in range(2):
                        step.after(toks[q])
                        dve.wait_ge(N["rstd_a"], nth(i, q, 2))
                        for t in range(GT):
                            ins = v.scalar_tensor_tensor(x1[q][:, t, :], sm[q][:, t, :], norms["a"]["rstd"][q][:, t:t + 1],
                                                         gb[:, BE1, :], ALU.mult, ALU.add)
                        ins.then_inc(x1_ready, 1)
                    qy = [q_rest[q][:, 0, :, :] for q in range(2)]
                    for q in range(2):
                        dve.wait_ge(x1_ready, nth(i, q, 2))
                        tok[q] = MARK(v.tensor_scalar(qy[q], x1[q][:, :, 0:NQ], TURN, None, ALU.mult))
                    for q in range(2):
                        step.after(tok[q])
                        tok[q] = MARK(v.tensor_scalar(q_ang[q][:, 0, :, :], qy[q], ROUND, ROUND, ALU.add, ALU.subtract))
                    for q in range(2):
                        step.after(tok[q])
                        tok[q] = MARK(v.tensor_tensor(q_ang[q][:, 0, :, :], qy[q], q_ang[q][:, 0, :, :], ALU.subtract))
                    for q in range(2):
                        step.after(tok[q])
                        magnitude(q_ang[q][:, 1, :, :], q_ang[q][:, 0, :, :]).then_inc(qangle_ready, 1)
                if late:
                    for q in range(2):
                        dve.wait_ge(logit_psum, nth(i, q, -2))
                        v.tensor_copy(logits[:, :, pair_tiles(i, -1, q)].rearrange("p e t -> p t e"),
                                      TA[q][:, 0:GT * NE].rearrange("p (t e) -> p t e", e=NE)).then_inc(logit_ready, 1)
                if tail:
                    if late:
                        for q in range(2):
                            dve.wait_ge(x_kept, nth(i, q, -2))
                    scaled("s", xn, x1b, G2, x1b_used)
                    if not late:
                        dve.wait_ge(xb_ready, 1)
                    for q in range(2):
                        dve.wait_ge(x1b_used, nth(i, q))
                        dve.wait_ge(N["rstd_s"], nth(i, q))
                        for t in range(GT):
                            xb = xb_all[:, bass.ds(i * (2 * GT) + (q * GT + t), 1), :]
                            ins = v.scalar_tensor_tensor(xn[q][:, t:t + 1, :], xn[q][:, t:t + 1, :], norms["s"]["rstd"][q][:, t:t + 1],
                                                         xb, ALU.mult, ALU.add)
                        ins.then_inc(xn_ready, 1)
                if head:
                    for q in range(2):
                        dve.wait_ge(qcos_ready, nth(i, q, 2))
                    k = 1
                    while k < NQ:
                        for q in range(2):
                            b = qc[q][:, :, :].rearrange("p t (n two k) -> p (t n) two k", two=2, k=k)
                            if k > 1:
                                step.after(tok[q])
                            nb = GT * NQ // (2 * k)
                            tok[q] = MARK(v.tensor_tensor(b[:, :, 1, :], b[:, :, 1, :],
                                                          b[:, :, 0, k - 1:k].broadcast_to([P, nb, k]), ALU.mult))
                        k *= 2

                    def part(q, first, n):
                        return q_split[q][:, :, first * NQ:(first + n) * NQ].rearrange("p t (n k) -> p t n k", n=n)

                    def spread(src, n):
                        return src.unsqueeze(2).broadcast_to([P, GT, n, NQ])
                    for q in range(2):
                        step.after(tok[q])
                        tok[q] = MARK(v.tensor_copy(part(q, 0, 3), spread(qc[q][:, :, :], 3)))
                    for q in range(2):
                        step.after(tok[q])
                        tok[q] = MARK(v.tensor_tensor(q_rest[q][:, 0, :, :], qc[q][:, :, :], q_split[q][:, :, 0:NQ], ALU.subtract))
                    for q in range(2):
                        step.after(tok[q])
                        tok[q] = MARK(v.tensor_copy(part(q, 3, 2), spread(q_rest[q][:, 0, :, :], 2)))
                    for q in range(2):
                        step.after(tok[q])
                        tok[q] = MARK(v.tensor_tensor(q_rest[q][:, 1, :, :], q_rest[q][:, 0, :, :],
                                                      q_split[q][:, :, 3 * NQ:4 * NQ], ALU.subtract))
                    for q in range(2):
                        step.after(tok[q])
                        v.tensor_copy(q_split[q][:, :, 5 * NQ:6 * NQ], q_rest[q][:, 1, :, :]).then_inc(qsplit_ready, 1)
                if head and not tail:
                    finish_weights()

            dve.wait_ge(x_loaded[0], 32)
            run_pairs(dve, first_block, step, A_DVE)

            def route(run):
                def chain(ins):
                    step.after(MARK(ins))

                def over_e(ap):
                    return ap.rearrange("p e t -> p t e")

                def tb(ap):
                    return ap.unsqueeze(1).broadcast_to([P, NE, NT])
                if run == 0:
                    dve.wait_ge(logit_ready, nth(NI - 1, 1))
                else:
                    dve.wait_ge(S["logit_read"], NG)
                src = logits
                for s in range(SLOTS):
                    chain(v.tensor_reduce(top[:, s, :], over_e(src[:, :, :]), AX.X, ALU.max))
                    chain(v.tensor_tensor(eq[:, :, :], src[:, :, :], tb(top[:, s, :]), ALU.is_equal))
                    chain(v.tensor_tensor(order_key[:, :, :], eq[:, :, :], first_bonus[:, :, :], ALU.mult))
                    chain(v.tensor_reduce(key_max[:, :], over_e(order_key[:, :, :]), AX.X, ALU.max))
                    chain(v.tensor_tensor(pick[:, s, :, :], order_key[:, :, :], tb(key_max[:, :]), ALU.is_equal))
                    if s == 0:
                        chain(v.scalar_tensor_tensor(masked[:, :, :], pick[:, 0, :, :], -3.0e38, logits[:, :, :],
                                                     ALU.mult, ALU.add))
                        src = masked
                v.tensor_tensor(picked[:, :, :], pick[:, 0, :, :], pick[:, 1, :, :], ALU.add).then_inc(picked_ready, 1)
                v.tensor_tensor(gate[:, 0, :], top[:, 1, :], top[:, 0, :], ALU.subtract).then_inc(gap_ready, 1)
                dve.wait_ge(gap_exp, run + 1)
                chain(v.tensor_scalar(gate[:, 2, :], gate[:, 1, :], 1.0, None, ALU.add))
                chain(v.reciprocal(w_slot[:, 0, :], gate[:, 2, :]))
                MARK(v.tensor_tensor(w_slot[:, 1, :], gate[:, 1, :], w_slot[:, 0, :], ALU.mult))
                dve.wait_ge(count_psum, run + 1)
                for h in range(2):
                    ins = v.tensor_scalar(count_b[:, h, :], ones_row[:, :], TB[0][:, h:h + 1], None, ALU.mult)
                ins.then_inc(count_ready, 1)
                dve.wait_ge(pos_psum, run + 1)
                pos = TA[0][:, 0:NE * NT].rearrange("p (e t) -> p e t", e=NE)
                for s in range(SLOTS):
                    dst = (eq, order_key)[s]
                    chain(v.tensor_tensor(dst[:, :, :], pick[:, s, :, :], pos, ALU.mult))
                    chain(v.tensor_reduce(posf[:, s * NT:(s + 1) * NT], over_e(dst[:, :, :]), AX.X, ALU.add))
                chain(v.tensor_copy(posi[:, 0, :], posf[:, :]))
                MARK(v.tensor_scalar(posi[:, 1, :], posi[:, 0, :], 7, None, ALU.logical_shift_right))
                chain(v.tensor_scalar(posi[:, 2, :], posi[:, 0, :], P - 1, None, ALU.bitwise_and))
                v.tensor_copy(hilo[:, :, :], posi[:, 1:3, :]).then_inc(hilo_ready, 1)
                dve.wait_ge(hilo_ready, run + 1)
                for n in range(HS):
                    v.tensor_tensor(hi_one[:, hot_part(n), :], iota_lo[:, 0:NHI].unsqueeze(1).broadcast_to([P, CPS, NHI]),
                                    hilo[:, 0, hot_part(n)].unsqueeze(2).broadcast_to([P, CPS, NHI]), ALU.is_equal)\
                        .then_inc(hi_one_ready, 1)
                for s in range(NTS):
                    v.tensor_scalar(lo_hot[:, s, :], iota_lo[:, :], hilo[:, 1, s:s + 1], None, ALU.is_equal).then_inc(lo_ready, 1)
                dve.wait_ge(inv_psum, run + 1)
                chain(v.tensor_copy(at_pos[:, :, :].rearrange("p k c -> p (k c)"), TB[1][:, 0:2 * NHI]))
                chain(v.scalar_tensor_tensor(row_f[:, 0, :], at_pos[:, 1, :], float(P), at_pos[:, 0, :], ALU.mult, ALU.add))
                chain(v.tensor_scalar(row_f[:, 1, :], row_f[:, 0, :], float(NTOK), -float(NTOK), ALU.is_ge, ALU.mult))
                v.tensor_copy(scatter_all[:, :], row_f[:, 0, :])
                v.tensor_tensor(gather_all[:, :], row_f[:, 0, :], row_f[:, 1, :], ALU.add).then_inc(index_ready, 1)

            def experts(run):
                def take_rows(i, s):
                    dve.wait_ge(gt_psum, nth(i, s, base=run * NB))
                    v.tensor_copy(xft[s][:, :], TA[s][:, :]).then_inc(gt_ready, 1)

                def give_rows(i, s, first):
                    dve.wait_ge(eo_psum, nth(i, s, base=run * NB))
                    if not first:
                        dve.wait_ge((eo_stored, scattered)[run][s], i * (16, 16 * GT)[run])
                    v.tensor_copy(expert_out[s][:, :, :].rearrange("p a b -> p (a b)"), TB[s][:, :]).then_inc(eo_ready, 1)

                take_rows(0, 0)
                take_rows(0, 1)
                give_rows(0, 0, True)
                take_rows(1, 0)
                give_rows(0, 1, True)
                with dve.Fori(1, NB // 2 - 1) as i:
                    take_rows(i, 1)
                    give_rows(i, 0, False)
                    take_rows(i + 1, 0)
                    give_rows(i, 1, False)
                take_rows(NB // 2 - 1, 1)
                give_rows(NB // 2 - 1, 0, False)
                give_rows(NB // 2 - 1, 1, False)

            def combine(i):
                toks = []
                for s in range(SLOTS):
                    for q in range(2):
                        if s == 0:
                            dve.wait_ge(y_loaded[2 * i + q], 16 * SLOTS)
                            if i:
                                dve.wait_ge(out_ready, nth(i - 1, q))
                        else:
                            step.after(toks[q])
                        for t in range(GT):
                            tile = (2 * i + q) * GT + t
                            src, dst = ((x_all[:, tile, :], sm[q][:, t, :]), (sm[q][:, t, :], x_all[:, tile, :]))[s]
                            ins = v.scalar_tensor_tensor(dst, y_all[q][:, s, i, t, :], w_slot[:, s, tile:tile + 1], src,
                                                         ALU.mult, ALU.add)
                        if s == 0:
                            toks.append(MARK(ins))
                        else:
                            ins.then_inc(out_ready, 1)

            route(0)
            experts(0)

            def attention_step(b, head, feat, tail, late):
                h, t_, l_ = b.plus(1), b.plus(-1), b.plus(-2)

                def stats_of(w, src):
                    st, mv_w = ln[w][0:2]
                    for t in range(GT):
                        ins = v.bn_stats(st[:, t, :], src[:, t, :])
                    return MARK(ins)

                def aggregate(w, tok):
                    st, mv_w = ln[w][0:2]
                    step.after(tok)
                    dve.sem_inc(dve_held, 1)
                    for t in range(GT):
                        ins = v.bn_aggr(mv_w[:, t, :], st[:, t, :])
                    return MARK(ins)

                def finish_stats(w, tok):
                    _, mv_w, var_w, neg_w = ln[w][0:4]
                    step.after(tok)
                    v.tensor_scalar(neg_w[:, :], mv_w[:, :, 0], -1.0, None, ALU.mult)
                    v.tensor_scalar(var_w[:, :], mv_w[:, :, 1], EPS, None, ALU.add).then_inc(S["var_" + w], 1)

                def unit_views(u):
                    r = u % 2
                    return F[:, 2 * r:2 * r + 2, :], ang[r].rearrange("p (a b) -> p a b", a=2), r

                def round_(bb, u, first=False):
                    src, dst, r = unit_views(u)
                    dve.wait_ge(S["proj_psum"], bb.k(u, 4))
                    if not first:
                        dve.wait_ge(S["feat"], bb.k(u - 2, 4))
                    return MARK(v.tensor_scalar(dst, src, ROUND, ROUND, ALU.add, ALU.subtract))

                def less(u, tok):
                    src, dst, r = unit_views(u)
                    step.after(tok)
                    v.tensor_tensor(dst, src, dst, ALU.subtract).then_inc(S["ang"], 1)

                def absolute(bb, u):
                    _, _, r = unit_views(u)
                    dve.wait_ge(S["ang"], bb.k(u, 4))
                    magnitude(ang_abs[r], ang[r]).then_inc(S["abs"], 1)

                def add_expert(s, tok):
                    if s == 0:
                        dve.wait_ge(y_gathered[h.q], h.turns(16 * SLOTS * GT))
                    step.after(tok)
                    for t in range(GT):
                        if s == 0:
                            dst, add = sum0[:, t:t + 1, :], x_all[:, bass.ds(h.tile() + t, 1), :]
                        else:
                            dst, add = xh[h.q][:, t:t + 1, :], sum0[:, t:t + 1, :]
                        ins = v.scalar_tensor_tensor(dst, y_in[h.q][:, s, t:t + 1, :], w_stage[h.q][:, s, t:t + 1], add,
                                                     ALU.mult, ALU.add)
                    return MARK(ins)

                if late:
                    dve.wait_ge(S["wo_psum"], l_.n())
                    dve.wait_ge(S["kept_h"], l_.n())
                    for t in range(GT):
                        ins = v.tensor_tensor(xn[l_.q][:, t:t + 1, :], x_all[:, bass.ds(l_.tile() + t, 1), :],
                                              T_B[:, t * P:(t + 1) * P].unsqueeze(1), ALU.add)
                    ins.then_inc(S["wo_used"], 1)
                if head:
                    w_tok = MARK(v.tensor_copy(w_stage[h.q][:, :, :], w_slot[:, :, bass.ds(h.tile(), GT)]))
                if late:
                    dve.wait_ge(S["wo_used"], l_.n())
                    l_tok = stats_of("t", xn[l_.q])
                if late:
                    l_tok = aggregate("t", l_tok)
                if late:
                    dve.wait_ge(b_xf_free[l_.q], l_.turns())
                    finish_stats("t", l_tok)
                if tail:
                    dve.wait_ge(S["kv_psum"], t_.n())
                    v.tensor_tensor(kvm[:, :, :, :].rearrange("p a j v -> p (a j) v"),
                                    T_B[:, :].rearrange("p (a v) -> p a v", v=HPC * DH),
                                    kv_mask[:, :, :].rearrange("p a b -> p (a b)").unsqueeze(1)
                                    .broadcast_to([P, 4 * NJ, HPC * DH]), ALU.mult).then_inc(S["kvm"], 1)
                if feat:
                    dve.wait_ge(S["qkv_used"], b.k(3, 4))
                    v.tensor_reduce(nrm[:, :, :], sq.rearrange("p t (h d) -> p t h d", d=DH), AX.X, ALU.add)\
                        .then_inc(S["nrm"], 1)
                    tok = round_(b, 1, not tail)
                if head:
                    h_tok = add_expert(0, w_tok)
                if feat:
                    less(1, tok)
                if head:
                    h_tok = add_expert(1, h_tok)
                if feat:
                    absolute(b, 1)
                    dve.wait_ge(S["scale"], b.n())
                    v.tensor_tensor(vk[b.q][:, 0, :, :].rearrange("p t (h d) -> p t h d", h=H),
                                    v_sb.rearrange("p t (h d) -> p t h d", h=H),
                                    scl[:, :, H:2 * H].unsqueeze(3).broadcast_to([P, GT, H, DH]), ALU.mult)\
                        .then_inc(S["vk"], 1)
                if head:
                    step.after(h_tok)
                    h_tok = stats_of("h", xh[h.q])
                if feat:
                    tok = round_(b, 2)
                if head:
                    h_tok = aggregate("h", h_tok)
                if feat:
                    less(2, tok)
                if head:
                    finish_stats("h", h_tok)
                if late:
                    dve.wait_ge(S["logit_psum"], l_.n())
                    v.tensor_copy(logits[:, :, bass.ds(l_.tile(), GT)].rearrange("p e t -> p t e"),
                                  H_B[:, 0:GT * NE].rearrange("p (t e) -> p t e", e=NE)).then_inc(S["logit_read"], 1)
                if feat:
                    absolute(b, 2)
                    tok = round_(b, 3)
                if tail:
                    dve.wait_ge(S["numt_psum"], t_.n())
                    zz = T_B[:, :].rearrange("p (t h d) -> p t h d", t=GT, h=H)[:, :, :, 0]
                    t_tok = MARK(v.tensor_tensor(zq[:, 0, :, :], zz, q_scale[t_.q][:, :, :], ALU.mult))
                    step.after(t_tok)
                    t_tok = MARK(v.tensor_scalar(zq[:, 1, :, :], zq[:, 0, :, :], 1e-6, None, ALU.max))
                    if feat:
                        less(3, tok)
                    step.after(t_tok)
                    t_tok = MARK(v.reciprocal(zq[:, 2, :, :], zq[:, 1, :, :]))
                    if feat:
                        v.tensor_scalar(q_scale[b.q][:, :, :], scl[:, :, 0:H], 1.0 / M, None, ALU.mult)
                    step.after(t_tok)
                    t_tok = MARK(v.tensor_tensor(zq[:, 0, :, :], zq[:, 2, :, :], q_scale[t_.q][:, :, :], ALU.mult))
                    if feat:
                        absolute(b, 3)
                    step.after(t_tok)
                    v.tensor_tensor(att.rearrange("p t (h d) -> p t h d", h=H),
                                    T_A[:, :].rearrange("p (t h d) -> p t h d", t=GT, h=H),
                                    zq[:, 0, :, :].unsqueeze(3).broadcast_to([P, GT, H, DH]), ALU.mult)\
                        .then_inc(S["att"], 1)
                elif feat:
                    less(3, tok)
                    v.tensor_scalar(q_scale[b.q][:, :, :], scl[:, :, 0:H], 1.0 / M, None, ALU.mult)
                    absolute(b, 3)
                if head:
                    tok = round_(h, 0, not feat)
                    less(0, tok)
                    absolute(h, 0)

            run_pipeline(dve, attention_step, step, ATT_DVE)

            route(1)
            experts(1)
            for i in range(NI):
                combine(i)

        @block.tensor
        def _(pe):
            mm = nc.tensor.matmul
            tr = nc.tensor.transpose

            pe.wait_ge(weights_in, 16 * 14)
            pe.wait_ge(consts_ready, 1)
            pe.wait_ge(setup_dve, 2)
            pe.wait_ge(w_split_ready, 1)
            for c in range(FC):
                tr(F[:, 0, :].bitcast(BF16)[:, c * P:(c + 1) * P], w1_split[:, c, :], identb[:, :])
                tr(F[:, 1, c * P:(c + 1) * P], w2_nat[:, c * P:(c + 1) * P], ident[:, :])
                tr(F[:, 2, c * P:(c + 1) * P], w_nat[:, c, :], ident[:, :])
            tr(F[:, 3, 0:NE], wr_nat[:, :], ident[0:NE, 0:NE])
            mm(F[:, 3, P:P + M], rf_rep[:, :, :].rearrange("m h d -> m (h d)"), ident[0:M, 0:M], start=True, stop=True)\
                .then_inc(setup_pe, 1)
            pe.wait_ge(setup_dve, 3)
            rfb = rf_block[:, :, :].rearrange("p h m -> p (h m)")
            mm(TA[0][:, :], w_nat[:, 0, :], rfb, start=True, stop=True)
            mm(TA[1][:, :], w_nat[:, 1, :], rfb, start=True, stop=True).then_inc(setup_pe, 1)
            pe.wait_ge(weights_ready, 1)

            def four_transposes(dst, src, signal):
                for t in range(GT):
                    ins = tr(dst[:, t * P:(t + 1) * P], src(t), ident[:, :])
                ins.then_inc(signal, 1)

            def add_half(dst, half, hidden, w):
                for t in range(GT):
                    for c in (2 * half, 2 * half + 1):
                        ins = mm(dst[:, t * P:(t + 1) * P], hidden(c, t), w(c), start=(t == 0 and c == 0),
                                 stop=(t == GT - 1 and c == 3))
                return ins

            def first_block(i, head, tail, late):
                if tail:
                    for q in range(2):
                        pe.wait_ge(qsplit_ready, nth(i, q))
                        for t in range(GT):
                            ins = tr(TA[q][:, :].bitcast(BF16)[:, t * P:(t + 1) * P], q_split[q][:, t, :], identb[:, :])
                        ins.then_inc(qt_psum, 1)
                    for q in range(2):
                        pe.wait_ge(qt_ready, nth(i, q))
                        for c in range(FC):
                            if q == 1 and c % 2 == 0:
                                pe.wait_ge(h_ready, i * 4 + (c // 2 + 1))
                            ins = mm(F[:, c, :], w1k[:, c * P:(c + 1) * P], q_t[q][:, :], start=True, stop=True)
                            if c % 2:
                                ins.then_inc(h_psum, 1)
                    for q in range(2):
                        for half in range(2):
                            pe.wait_ge(h_ready, i * 4 + (2 * q + half + 1))
                            ins = add_half(TB[q], half, lambda c, t: hid[q][:, c, t * P:(t + 1) * P], lambda c: w2t[:, c, :])
                        ins.then_inc(ffn_psum, 1)
                if late:
                    for q in range(2):
                        pe.wait_ge(xf_ready, nth(i, q, -2))
                        four_transposes(TA[q], lambda t: xf[q][:, t, :], xft_psum)
                    for q in range(2):
                        pe.wait_ge(xft_ready, nth(i, q, -2))
                        for t in range(GT):
                            ins = mm(TA[q][:, t * NE:(t + 1) * NE], xft[q][:, t * P:(t + 1) * P], wrt[:, :], start=True, stop=True)
                        ins.then_inc(logit_psum, 1)

            run_pairs(pe, first_block)

            def route(run):
                pe.wait_ge(picked_ready, run + 1)
                chosen = picked[:, :, :].rearrange("p e t -> p (e t)")
                for h in range(2):
                    ins = mm(TB[0][:, h:h + 1], chosen[:, h * P:(h + 1) * P], ones_row[:, 0:1], start=True, stop=True)
                ins.then_inc(count_psum, 1)
                pe.wait_ge(count_ready, run + 1)
                n = NE * NT
                mm(TA[0][:, 0:n], after_tri[:, P:2 * P], chosen, start=True, stop=False)
                mm(TA[0][:, 0:n], count_b[:, 0, :], after_tri[:, P:3 * P], start=False, stop=False)
                mm(TA[0][:, 0:n], count_b[:, 1, :], after_tri[:, 0:2 * P], start=False, stop=True).then_inc(pos_psum, 1)
                for s in range(NTS):
                    pe.wait_ge(lo_ready, run * NTS + s + 1)
                    if s % CPS == 0:
                        pe.wait_ge(hi_row_ready, run * HS + s // CPS + 1)
                        pe.wait_ge(hi_col_ready, run * HS + s // CPS + 1)
                    ins = mm(TB[1][:, 0:2 * NHI], lo_hot[:, s, :], hi_hot[:, s, :, :].rearrange("p k c -> p (k c)"),
                             start=(s == 0), stop=(s == NTS - 1))
                ins.then_inc(inv_psum, 1)

            def experts(run):
                gathers = run * 16 * GT * (NB // 2)
                pe.wait_ge(index_ready, run + 1)

                def turn(i, s):
                    pe.wait_ge(gathered_in[s], i * (16 * GT) + (16 * GT + gathers))
                    four_transposes(TA[s], lambda t: gathered[s][:, t, :], gt_psum)

                def up(i, s, e):
                    pe.wait_ge(gt_ready, nth(i, s, base=run * NB))
                    for c in range(EC):
                        ins = mm(F[:, c, :], ew1_sb[e][:, c * P:(c + 1) * P], xft[s][:, :], start=True, stop=True)
                        if c % 2:
                            ins.then_inc(eh_psum, 1)

                def down(i, s, e):
                    for half in range(2):
                        pe.wait_ge(eh_ready, i * 4 + (2 * s + half + 1 + run * 2 * NB))
                        ins = add_half(TB[s], half, lambda c, t: hid[s][:, c, t * P:(t + 1) * P], lambda c: ew2_sb[e][:, c, :])
                    ins.then_inc(eo_psum, 1)

                def pair(k):
                    for e in range(2):
                        i = k * 2 + e
                        pe.wait_ge(ew_loaded[e], k * 32 + (32 + run * 32 * (NE // 2)))
                        for s in range(2):
                            if e == 0 and s == 0:
                                turn(i, s)
                            up(i, s, e)
                            if not (e == 1 and s == 1):
                                turn(i + s, 1 - s)
                            down(i, s, e)
                with pe.Fori(0, NE // 2) as k:
                    pair(k)

            route(0)
            experts(0)

            VW = HPC * DH
            wqkv = wqkv_t[:, :, :].rearrange("p a b -> p (a b)")

            def attention_step(b, head, feat, tail, late):
                h, t_, l_ = b.plus(1), b.plus(-1), b.plus(-2)

                def unit(bb, u, first=False):
                    if not first:
                        pe.wait_ge(S["ang"], bb.k(u - 2, 4))
                    for n in range(2):
                        c = 2 * (u % 2) + n
                        if u < 2:
                            ins = mm(F[:, c, :], xt[bb.q][:, c * P:(c + 1) * P], wkf[:, :], start=True, stop=True)
                        else:
                            ins = mm(F[:, c, :], wqf[:, c * P:(c + 1) * P], xt[bb.q][:, :], start=True, stop=True)
                    ins.then_inc(S["proj_psum"], 1)

                if feat:
                    unit(b, 1, not tail)
                if tail:
                    pe.wait_ge(S["kvt"], t_.n())
                    if late:
                        pe.wait_ge(S["wo_used"], l_.n())
                    four_transposes(T_B, lambda t: kvt[t_.q][:, t, :], S["kv_psum"])
                if feat:
                    unit(b, 2)
                if tail:
                    pe.wait_ge(S["kvm"], t_.n())
                    pe.wait_ge(S["feat"], t_.k(3, 4))
                    for a, dst in ((0, T_A), (1, T_B)):
                        for sc in range(2):
                            for j in range(NJ):
                                ins = mm(dst[j * VW:(j + 1) * VW, :], kvm[:, 2 * a + sc, j, :], qfeat[t_.q][:, sc, j, :],
                                         start=(sc == 0), stop=(sc == 1), tile_position=(0, j * VW))
                    ins.then_inc(S["num_psum"], 1)
                if late:
                    pe.wait_ge(S["xf"], l_.n())
                    if feat:
                        pe.wait_ge(S["qkv_used"], b.k(3, 4))
                    four_transposes(H_B, lambda t: xf[l_.q][:, t, :], S["xft_psum"])
                if feat:
                    unit(b, 3)
                if late:
                    pe.wait_ge(S["xft"], l_.n())
                    for t in range(GT):
                        ins = mm(H_B[:, t * NE:(t + 1) * NE], xrt[:, t * P:(t + 1) * P], wrt[:, :], start=True, stop=True)
                    ins.then_inc(S["logit_psum"], 1)
                if tail:
                    pe.wait_ge(S["num"], t_.n())
                    for t in range(GT):
                        tr(T_A[:, t * P:(t + 1) * P], num_s[:, t, :], ident[:, :])
                    four_transposes(T_B, lambda t: den_s[:, t, :], S["numt_psum"])
                if feat:
                    pe.wait_ge(S["feat"], b.k(1, 4))
                    pe.wait_ge(S["qkv_used"], b.k(3, 4))
                    for a in range(2):
                        pe.wait_ge(S[("vk", "krep")[a]], b.n())
                        for t in range(GT):
                            for j in range(NJ):
                                ins = mm(H_A[j * VW:(j + 1) * VW, a * 2 * P:(a + 1) * 2 * P].rearrange("p (s c) -> p s c", s=2),
                                         vk[b.q][:, a, t, j * VW:(j + 1) * VW], kfeat[b.q][:, t, :, j * P:(j + 1) * P],
                                         start=(t == 0), stop=(t == GT - 1), tile_position=(0, j * VW))
                    ins.then_inc(S["kvt_psum"], 1)

                def qkv(t):
                    if t >= 2:
                        pe.wait_ge(S["qkv_used"], h.k(t - 2, 4))
                    mm((H_A, H_B)[t % 2][:, 0:3 * C], xt[h.q][:, t * P:(t + 1) * P], wqkv, start=True, stop=True)\
                        .then_inc(S["qkv_psum"], 1)
                if head:
                    pe.wait_ge(S["ax"], h.n())
                    if late:
                        pe.wait_ge(S["logit_read"], l_.n())
                    four_transposes(H_B, lambda t: ax[:, t, :], S["axt_psum"])
                if head:
                    pe.wait_ge(S["axt"], h.n())
                    unit(h, 0, not feat)
                if tail:
                    pe.wait_ge(S["att"], t_.n())
                    four_transposes(T_A, lambda t: att[:, t, :], S["attt_psum"])
                if head:
                    if feat:
                        pe.wait_ge(S["kvt"], b.n())
                    qkv(0)
                    qkv(1)
                    qkv(2)
                    qkv(3)
                if tail:
                    pe.wait_ge(S["attt"], t_.n())
                    for t in range(GT):
                        ins = mm(T_B[:, t * P:(t + 1) * P], att_t[:, t * P:(t + 1) * P], wot[:, :], start=True, stop=True)
                    ins.then_inc(S["wo_psum"], 1)

            run_pipeline(pe, attention_step)
            route(1)
            experts(1)


_INS = ["L0_attn_a_x", "L0_attn_a_w1", "L0_attn_a_b1", "L0_attn_a_w2", "L0_attn_a_b2", "L0_attn_a_gamma1", "L0_attn_a_beta1",
        "L0_attn_a_gamma2", "L0_attn_a_beta2", "L0_attn_b_wq", "L0_attn_b_wk", "L0_attn_b_wv", "L0_attn_b_wo",
        "L0_attn_b_rf", "L0_ffn_Wr", "L0_ffn_W1", "L0_ffn_W2"]


def kernel(**inputs):
    import numpy as np
    import concourse.bacc as bacc
    from concourse.bass_utils import run_bass_kernel_spmd

    nc = bacc.Bacc("TRN2", target_bir_lowering=False, num_devices=1)
    arrays, args = {}, []
    for name in _INS:
        a = np.ascontiguousarray(inputs[name])
        if name == "L0_attn_a_x":
            shape = a.shape
            a = a.reshape(-1, a.shape[-1])
        arrays[f"in_{name}"] = a
        args.append(nc.dram_tensor(f"in_{name}", a.shape, mybir.dt.from_np(a.dtype), kind="ExternalInput").ap())
    rows_out = (shape[0] * shape[1], shape[2])
    args.append(nc.dram_tensor("out_dram", rows_out, F32, kind="ExternalOutput").ap())
    build(nc, *args)
    r = run_bass_kernel_spmd(nc, [arrays], core_ids=[0])
    return r.results[0]["out_dram"].reshape(shape)
```

```python
import math
from contextlib import ExitStack

import concourse.bass as bass
from concourse import mybir

ALU = mybir.AluOpType
ACT = mybir.ActivationFunctionType
AX = mybir.AxisListType
F32 = mybir.dt.float32
F32R = mybir.dt.float32r
BF16 = mybir.dt.bfloat16
I32 = mybir.dt.int32

P = 128
GT = 4
GN = GT * P
EPS = 1e-5
ROUND = 1.5 * 2.0 ** 23
TURN = 1.0 / (2.0 * math.pi)
TWO_PI = 6.283185005187988
HALF_PI = math.pi / 2


def nth(i, q, base=0):
    return i * 2 + (q + 1 + base)


class Batch:

    def __init__(self, i, off):
        self.i, self.off, self.q = i, off, off % 2

    def plus(self, d):
        return Batch(self.i, self.off + d)

    def n(self, base=0):
        return self.i * 2 + (self.off + 1 + base)

    def k(self, k, per):
        return self.i * (2 * per) + (self.off * per + k + 1)

    def turns(self, each=1, base=0):
        return self.i * each + ((self.off // 2 + 1) * each + base)

    def tile(self):
        return self.i * (2 * GT) + self.off * GT


class Steps:

    def __init__(self, eng, sem):
        self.eng, self.sem, self.base, self.n, self.i, self.per = eng, sem, 0, 0, 0, 0

    def loop(self, i, per, first=0):
        self.base += self.n - first * per
        self.i, self.per, self.n = i, per, 0

    def end(self, end):
        assert self.n == self.per, ("marks in this loop", self.n, self.per)
        self.base += self.per * end
        self.i, self.per, self.n = 0, 0, 0

    def mark(self, instruction):
        instruction.then_inc(self.sem, 1)
        self.n += 1
        return self.n

    def after(self, token):
        self.eng.wait_ge(self.sem, self.i * self.per + (self.base + token))


def build(nc, x_in, fw1, fb1, fw2, fb2, gamma1, beta1, gamma2, beta2, wq, wk, wv, wo, rf, wr, ew1, ew2, out):
    NTOK, C = x_in.shape
    NT = NTOK // P
    NG = NTOK // GN
    NI = NG // 2
    FF, NQ = fw1.shape
    FC = FF // P
    M, DH = rf.shape
    H = C // DH
    NE = wr.shape[0]
    EF = ew1.shape[2]
    EC = EF // P
    SLOTS = 2
    NPOS = SLOTS * NTOK
    NB = NPOS // GN
    BPE = NB // NE
    NTS = SLOTS * NT
    NHI = NPOS // P
    HPC = P // M
    NJ = H // HPC
    assert C == P and FC == 4 and EC == 4 and NJ == 4 and BPE == 2 and NI == 4 and NTS == 64 and NQ == 16

    xf_dram = nc.dram_tensor("xf_dram", [NTOK, C], F32).ap()
    y_dram = nc.dram_tensor("y_dram", [NPOS, C], F32).ap()

    def rows(ap, first_tile, tiles=GT):
        return ap[bass.ds(first_tile * P, tiles * P), :].rearrange("(t p) c -> p t c", p=P)

    with ExitStack() as ctx:
        def sb(name, shape, dt=F32):
            return ctx.enter_context(nc.sbuf_tensor(name, shape, dt))

        def ps(name, shape, dt=F32):
            return ctx.enter_context(nc.psum_tensor(name, shape, dt))

        def sem(name):
            return ctx.enter_context(nc.semaphore(name))

        ident = sb("ident", [P, P])
        identb = sb("identb", [P, P], BF16)
        after_tri = sb("after_tri", [P, 3 * P], BF16)
        ones_row = sb("ones_row", [P, P], BF16)
        iota_lo = sb("iota_lo", [P, P], BF16)
        iota_i = sb("iota_i", [P, P], I32)
        pcol_i = sb("pcol_i", [P, 1], I32)
        pcol = sb("pcol", [P, 1])
        half_pi = sb("half_pi", [P, 1])
        neg_half = sb("neg_half", [P, GT])
        kv_mask = sb("kv_mask", [P, HPC, DH])
        head_mask = sb("head_mask", [P, H])
        gb = sb("gb", [P, 5, C])
        G1, BE1, G2, BE2, B2 = range(5)
        w1_nat = sb("w1_nat", [P, FC, NQ + 1])
        w1k = sb("w1k", [P, FF], BF16)
        w2t = sb("w2t", [P, FC, C])
        wr_nat = sb("wr_nat", [NE, C])
        wrt = sb("wrt", [C, NE])
        wqkv_part = [sb(f"wqkv_part{n}", [P, 3 * C], F32R) for n in range(2)]
        wot = sb("wot", [P, C])
        rf_nat = sb("rf_nat", [M, DH])
        rf_block = sb("rf_block", [P, H, M])
        wqf = sb("wqf", [P, H * M])
        wkf = sb("wkf", [P, H * M])
        ew1_sb = [sb(f"ew1_{s}", [P, EF]) for s in range(2)]
        ew2_sb = [sb(f"ew2_{s}", [P, EC, C]) for s in range(2)]

        x_all = sb("x_all", [P, NT, C])
        logits = sb("logits", [P, NE, NT])

        def two(name, shape, dt=F32):
            return [sb(f"{name}{q}", shape, dt) for q in range(2)]
        pairs = [two(f"pair{n}_", [P, 2, GT, C]) for n in range(3)]

        def halves(n):
            return [[pairs[n][q][:, h, :, :] for q in range(2)] for h in range(2)]
        (yt, rt), x1b = halves(1), halves(2)[1]
        norms = {k: {name: two(f"{name}_{k}", shape) for name, shape in (
            ("stats", [P, GT, 6]), ("mv", [P, GT, 2]), ("var", [P, GT]), ("rstd", [P, GT]), ("neg_mean", [P, GT]), ("shift", [P, GT]))}
            for k in "xasn"}
        ct = two("ct", [P, GT, C])
        sm = two("sm", [P, GT, C])
        q_ang = two("q_ang", [P, 2, GT, NQ])
        qc = two("qc", [P, GT, NQ])
        q_rest = two("q_rest", [P, 2, GT, NQ])
        q_split_mem = sb("q_split_mem", [P, 2, GT, P], BF16)
        q_t_mem = sb("q_t_mem", [P, 2, GN], BF16)
        q_split, q_t = [[mem[:, q] for q in range(2)] for mem in (q_split_mem, q_t_mem)]
        hid = two("hid", [P, FC, GN])
        w2_nat, w_nat = hid[1][:, 0, :], hid[1][:, 1, :].rearrange("p (n c) -> p n c", n=4)
        w1_split = hid[1][:, 2, 0:FF // 2].bitcast(BF16).rearrange("p (c n) -> p c n", c=FC)
        rf_rep = hid[1][0:M, 2, FF // 2:FF // 2 + C].rearrange("m (h d) -> m h d", h=H)
        xn = two("xn", [P, GT, C])
        xf = two("xf", [P, GT, C])
        gathered, expert_out = yt, rt
        ew1_part = [[sb(f"ew1_part{s}{n}", [P, EF], F32R) for n in range(2)] for s in range(2)]
        xt_part = [[sb(f"xt_part{q}{n}", [P, GN], F32R) for n in range(2)] for q in range(2)]
        gather_idx = two("gather_idx", [P, GT], I32)
        scatter_idx = two("scatter_idx", [P, GT], I32)
        y_idx = two("y_idx", [P, SLOTS, GT], I32)
        y_in = two("y_in", [P, SLOTS, GT, C])
        w_stage = two("w_stage", [P, SLOTS, GT])
        top = sb("top", [P, SLOTS, NT])
        eq = sb("eq", [P, NE, NT])
        order_key = sb("order_key", [P, NE, NT])
        key_max = sb("key_max", [P, NT])
        masked = sb("masked", [P, NE, NT])
        pick = sb("pick", [P, SLOTS, NE, NT])
        picked = sb("picked", [P, NE, NT], BF16)
        first_bonus = sb("first_bonus", [P, NE, NT])
        count_b = sb("count_b", [P, 2, P], BF16)
        posf = sb("posf", [P, NTS])
        posi = sb("posi", [P, 3, NTS], I32)
        hilo = sb("hilo", [P, 2, NTS])
        gate = sb("gate", [P, 3, NT])
        w_slot = sb("w_slot", [P, SLOTS, NT])
        at_pos = sb("at_pos", [P, 2, NHI])
        row_f = sb("row_f", [P, 2, NHI])
        scatter_all = sb("scatter_all", [P, NHI], I32)
        gather_all = sb("gather_all", [P, NHI], I32)
        kfeat = two("kfeat", [P, GT, 2, H * M])
        qfeat = two("qfeat", [P, 2, NJ, GN])
        lo_hot = kfeat[0][:].rearrange("p a b c -> p (a b c)").bitcast(BF16).rearrange("p (s c) -> p s c", c=P)
        hi_hot = qfeat[0][:].rearrange("p a b c -> p (a b c)").bitcast(BF16).rearrange("p (s k c) -> p s k c", k=2, c=NHI)
        hi_one = kfeat[1][:].rearrange("p a b c -> p (a b c)").bitcast(BF16)[:, 0:NTS * NHI].rearrange("p (s c) -> p s c", c=NHI)
        xb_all = kfeat[0][:].rearrange("p a b c -> p (a b c)").rearrange("p (t c) -> p t c", c=C)
        y_all = [kfeat[q][:].rearrange("p t s (i c) -> p (t s i c)", c=C)
                 .rearrange("p (s i t c) -> p s i t c", s=SLOTS, t=GT, c=C) for q in range(2)]
        ang = [pairs[1][q][:, :, :, :].rearrange("p a b c -> p (a b c)") for q in range(2)]
        ang_abs = [pairs[2][q][:, :, :, :].rearrange("p a b c -> p (a b c)") for q in range(2)]
        vk = pairs[0]
        sum0, ax = ct[0], ct[1]
        proj_part = ew1_part
        xft = [pick[:, :, :, :].rearrange("p s e t -> p (s e t)"), rf_block[:, :, :].rearrange("p h m -> p (h m)")]
        sq = hid[0][:, 0:2, :].rearrange("p a (b c) -> p (a b) c", c=2 * C)
        v_sb = hid[0][:, 2, :].rearrange("p (t c) -> p t c", t=GT)
        kvt = [hid[0][:, 3, :].rearrange("p (a c) -> p a c", a=4), hid[1][:, 0, :].rearrange("p (a c) -> p a c", a=4)]
        num_s, den_s, att = [hid[1][:, n, :].rearrange("p (t c) -> p t c", t=GT) for n in (1, 2, 3)]
        att_t = w2t[:, :, :].rearrange("p f c -> p (f c)")
        xrt = q_t_mem[:, :, :].rearrange("p q n -> p (q n)").bitcast(F32)
        kvm = q_split_mem[:, :, :, :].rearrange("p q t n -> p (q t n)").bitcast(F32).rearrange("p (a j v) -> p a j v", a=4, j=NJ)
        nrm, scl = [order_key[:, e * NE // 2:(e + 1) * NE // 2, :] for e in range(2)]
        q_scale = [masked[:, e * NE // 4:(e + 1) * NE // 4, :] for e in range(2)]
        nrm, scl = [mem.rearrange("p e (t h) -> p (e t) h", h=2 * H) for mem in (nrm, scl)]
        q_scale = [mem.rearrange("p e (t h) -> p (e t) h", h=H) for mem in q_scale]
        zq = eq[:, 0:3 * GT * H // NT, :].rearrange("p (n e) (t h) -> p n (e t) h", n=3, h=H)
        ln = {w: [norms[k][name][0] for name in ("stats", "mv", "var", "neg_mean", "rstd", "shift")] for w, k in ("hx", "ta")}

        F = ps("F", [P, 4, GN])
        TA = [ps(f"TA{q}", [P, GN]) for q in range(2)]
        TB = [ps(f"TB{q}", [P, GN]) for q in range(2)]
        (T_A, H_A), (T_B, H_B) = TA, TB

        weights_in = sem("weights_in")
        consts_ready = sem("consts_ready")
        pool_steps = sem("pool_steps")
        dve_steps = sem("dve_steps")
        pool_held, dve_held = sem("pool_held"), sem("dve_held")
        setup_dve = sem("setup_dve")
        setup_pe = sem("setup_pe")
        w_split_ready = sem("w_split_ready")
        weights_ready = sem("weights_ready")
        x_loaded = [sem(f"x_loaded{n}") for n in range(2)]
        N = {f"{name}_{k}": sem(f"{name}_{k}") for k in "xasn" for name in ("var", "rstd")}
        turns_ready, angle_ready, cos_ready = sem("turns_ready"), sem("angle_ready"), sem("cos_ready")
        za_ready, zs_ready, x1g_ready, x2g_ready = sem("za_ready"), sem("zs_ready"), sem("x1g_ready"), sem("x2g_ready")
        x1b_ready = sem("x1b_ready")
        qangle_ready, qcos_ready, qsplit_ready = sem("qangle_ready"), sem("qcos_ready"), sem("qsplit_ready")
        qt_psum, qt_ready = sem("qt_psum"), sem("qt_ready")
        h_psum, h_ready = sem("h_psum"), sem("h_ready")
        ffn_psum = sem("ffn_psum")
        xn_ready, x_kept = sem("xn_ready"), sem("x_kept")
        xf_ready = sem("xf_ready")
        xf_stored = [sem(f"xf_stored{q}") for q in range(2)]
        xf_free = [sem(f"xf_free{q}") for q in range(2)]
        xft_psum, xft_ready, logit_psum, logit_ready = sem("xft_psum"), sem("xft_ready"), sem("logit_psum"), sem("logit_ready")
        gap_ready, gap_exp = sem("gap_ready"), sem("gap_exp")
        picked_ready, count_psum, count_ready, pos_psum = sem("picked_ready"), sem("count_psum"), sem("count_ready"), sem("pos_psum")
        hilo_ready, lo_ready, hi_one_ready, hi_row_ready, hi_col_ready = (
            sem(n) for n in ("hilo_ready", "lo_ready", "hi_one_ready", "hi_row_ready", "hi_col_ready"))
        inv_psum, index_ready = sem("inv_psum"), sem("index_ready")
        ew1_split = sem("ew1_split")
        proj_split, gather_idx_ready = sem("proj_split"), sem("gather_idx_ready")
        ew_loaded = [sem(f"ew_loaded{s}") for s in range(2)]
        gathered_in = [sem(f"gathered_in{s}") for s in range(2)]
        gt_psum, gt_ready, eh_psum, eh_ready, eo_psum, eo_ready = (
            sem("gt_psum"), sem("gt_ready"), sem("eh_psum"), sem("eh_ready"), sem("eo_psum"), sem("eo_ready"))
        scattered = [sem(f"scattered{s}") for s in range(2)]
        y_loaded = [sem(f"y_loaded{b}") for b in range(NG)]
        y_gathered = [sem(f"y_gathered{q}") for q in range(2)]
        out_ready, shared_out_ready, weighted = sem("out_ready"), sem("shared_out_ready"), sem("weighted")
        out_stored = sem("out_stored")
        S = {name: sem("att_" + name) for name in (
            "var_h", "rstd_h", "var_t", "rstd_t", "ax", "axt_psum", "axt", "xt_lo", "qkv_psum", "qkv_used", "nrm", "scale", "vk", "krep",
            "proj_psum", "ang", "abs", "feat", "kvt_psum", "kvt", "kv_psum", "kvm", "num_psum", "num", "numt_psum", "att",
            "attt_psum", "attt", "wo_psum", "xf", "xft_psum", "xft", "logit_psum", "logit_read", "wo_used")}
        b_xf_stored = [sem(f"att_xf_stored{q}") for q in range(2)]
        b_xf_free = [sem(f"att_xf_free{q}") for q in range(2)]
        eo_stored = [sem(f"eo_stored{s}") for s in range(2)]

        def run_pipeline(eng, work, steps=None, marks=0):
            work(Batch(0, -1), head=True, feat=False, tail=False, late=False)
            work(Batch(0, 0), head=True, feat=True, tail=False, late=False)
            work(Batch(0, 1), head=True, feat=True, tail=True, late=False)
            with eng.Fori(0, (NG - 4) // 2) as i:
                if steps:
                    steps.loop(i, marks)
                for off in (2, 3):
                    work(Batch(i, off), head=True, feat=True, tail=True, late=True)
            if steps:
                steps.end((NG - 4) // 2)
            work(Batch(0, NG - 2), head=True, feat=True, tail=True, late=True)
            work(Batch(0, NG - 1), head=False, feat=True, tail=True, late=True)
            work(Batch(0, NG), head=False, feat=False, tail=True, late=True)
            work(Batch(0, NG + 1), head=False, feat=False, tail=False, late=True)

        ATT_POOL, ATT_DVE = 6, 30
        A_POOL, A_DVE = 8, 62

        def run_pairs(eng, work, steps=None, marks=0):
            work(-1, head=True, tail=False, late=False)
            work(0, head=True, tail=True, late=False)
            with eng.Fori(1, NI - 1) as i:
                if steps:
                    steps.loop(i, marks, 1)
                work(i, head=True, tail=True, late=True)
            if steps:
                steps.end(NI - 1)
            work(NI - 1, head=False, tail=True, late=True)
            work(NI, head=False, tail=False, late=True)

        def pair_tiles(i, d, q):
            return bass.ds(i * (2 * GT) + (d * 2 * GT + q * GT), GT)

        VECTOR_GROUPS, SHARED_GROUPS = (0, 1, 3, 4, 6, 7), (2, 5)

        HS = 4
        CPS = NTS // HS

        def hot_part(n):
            return slice(n * CPS, (n + 1) * CPS)

        block = ctx.enter_context(nc.Block())

        @block.sync
        def _(sp):
            loads = [(w1_nat[:, :, 0:NQ], fw1.rearrange("(c p) k -> p c k", p=P)),
                     (w2_nat[:, :], fw2), (wr_nat[:, :], wr), (rf_nat[:, :], rf)]
            loads += [(gb[:, n, :], v.partition_broadcast(P)) for n, v in enumerate((gamma1, beta1, gamma2, beta2, fb2))]
            loads += [(w_nat[:, n, :], w) for n, w in enumerate((wq, wk, wv, wo))]
            for q in range(2):
                sp.dma_start(x_all[:, q * GT:(q + 1) * GT, :], rows(x_in, q * GT)).then_inc(x_loaded[0], 16)
            for dst, src in loads:
                sp.dma_start(dst, src).then_inc(weights_in, 16)
            with nc.allow_non_contiguous_dma("b1 lies along the partitions once"):
                sp.dma_start(w1_nat[:, :, NQ:NQ + 1], fb1.rearrange("(c p k) -> p c k", p=P, k=1)).then_inc(weights_in, 16)

            for b in range(2, NG):
                sp.dma_start(x_all[:, b * GT:(b + 1) * GT, :], rows(x_in, b * GT)).then_inc(x_loaded[1], 16)

            def load_expert(e, s):
                sp.dma_start(ew1_sb[s][:, :], ew1[bass.ds(e, 1), :, :].rearrange("a c f -> c (a f)")).then_inc(ew_loaded[s], 16)
                sp.dma_start(ew2_sb[s][:, :, :], ew2[bass.ds(e, 1), :, :].rearrange("a (k p) c -> p (a k) c", p=P))\
                    .then_inc(ew_loaded[s], 16)

            for s in range(2):
                load_expert(s, s)
            for q in range(2):
                sp.sem_inc(xf_free[q], 1)

            with sp.Fori(0, NI) as i:
                for q in range(2):
                    sp.wait_ge(xf_ready, nth(i, q))
                    sp.dma_start(rows(xf_dram, (i * 2 + q) * GT), xf[q][:, :, :]).then_inc(xf_stored[q], 16)
                for q in range(2):
                    sp.wait_ge(xf_stored[q], i * 16 + 16)
                    sp.sem_inc(xf_free[q], 1)

            def experts(run):
                def store_sorted(i, s):
                    sp.wait_ge(eo_ready, nth(i, s))
                    sp.dma_start(rows(y_dram, i * (2 * GT) + s * GT), expert_out[s][:, :, :]).then_inc(eo_stored[s], 16)

                with sp.Fori(0, NE // 2 - 1) as i:
                    for e in range(2):
                        if run == 0:
                            for s in range(2):
                                store_sorted(i * 2 + e, s)
                        sp.wait_ge(eo_psum, i * 4 + (2 * e + 2 + run * NB))
                        load_expert(i * 2 + (e + 2), e)
                if run == 0:
                    for i in range(NE - 2, NE):
                        for s in range(2):
                            store_sorted(i, s)
                if run == 0:
                    for s in range(2):
                        sp.wait_ge(eo_psum, NB - 2 + 2 * s)
                        load_expert(s, s)
                if run == 1:
                    for s in range(2):
                        sp.wait_ge(scattered[s], 16 * GT * (NB // 2))

            experts(0)
            for q in range(2):
                sp.sem_inc(b_xf_free[q], 1)
            with sp.Fori(0, NI) as i:
                for q in range(2):
                    b = Batch(i, q)
                    sp.wait_ge(S["xf"], b.n())
                    sp.dma_start(rows(xf_dram, b.tile()), xf[q][:, :, :]).then_inc(b_xf_stored[q], 16)
                    sp.wait_ge(b_xf_stored[q], b.turns(16))
                    sp.sem_inc(b_xf_free[q], 1)

            experts(1)
            for b in range(NG):
                for s in range(SLOTS):
                    sp.dma_start(y_all[b % 2][:, s, b // 2, :, :], rows(y_dram, b * GT + s * NT)).then_inc(y_loaded[b], 16)
            for b in range(NG):
                if b in SHARED_GROUPS:
                    sp.wait_ge(shared_out_ready, SHARED_GROUPS.index(b) + 1)
                else:
                    sp.wait_ge(out_ready, VECTOR_GROUPS.index(b) + 1)
                sp.dma_start(rows(out, b * GT), x_all[:, b * GT:(b + 1) * GT, :]).then_inc(out_stored, 16)
            sp.wait_ge(out_stored, 16 * NG)

        @block.gpsimd
        def _(pool):
            g = nc.gpsimd
            step = Steps(pool, pool_steps)
            m = [step.mark(g.memset(ident[:, :], 0.0)), step.mark(g.memset(after_tri[:, :], 1.0)),
                 step.mark(g.memset(kv_mask[:, :, :], 1.0)), step.mark(g.memset(head_mask[:, :], 1.0)),
                 step.mark(g.iota(iota_i[:, :], pattern=[[1, P]], base=0, channel_multiplier=0)),
                 step.mark(g.iota(pcol_i[:, :], pattern=[[0, 1]], base=0, channel_multiplier=1))]
            g.memset(ones_row[:, :], 1.0)
            g.memset(half_pi[:, :], HALF_PI)
            g.memset(neg_half[:, :], -0.5)
            for e in range(NE):
                g.memset(first_bonus[:, e, :], float(NE - e))
            for q in range(2):
                g.memset(q_split[q][:, :, 6 * NQ:], 0.0)
            last = g.memset(w1_split[:, :, 6 * NQ:], 0.0)
            m.append(step.mark(last))
            step.after(m[-1])
            g.affine_select(out=ident[:, :], in_=ident[:, :], compare_op=ALU.not_equal, fill=1.0, base=0,
                            pattern=[[-1, P]], channel_multiplier=1)
            for q in range(2):
                g.memset(q_split[q][:, :, 6 * NQ:6 * NQ + 3], 1.0)
            g.affine_select(out=after_tri[:, :], in_=after_tri[:, :], compare_op=ALU.is_gt, fill=0.0, base=-P,
                            pattern=[[1, 3 * P]], channel_multiplier=-1)
            lower_kv = g.affine_select(out=kv_mask[:, :, :], in_=kv_mask[:, :, :], compare_op=ALU.is_ge, fill=0.0, base=0,
                                       pattern=[[-M, HPC], [0, DH]], channel_multiplier=1)
            step.mark(lower_kv)
            t = step.mark(g.affine_select(out=head_mask[:, :], in_=head_mask[:, :], compare_op=ALU.is_ge, fill=0.0, base=0,
                                          pattern=[[-DH, H]], channel_multiplier=1))
            step.after(t)
            g.affine_select(out=kv_mask[:, :, :], in_=kv_mask[:, :, :], compare_op=ALU.is_ge, fill=0.0, base=M - 1,
                            pattern=[[M, HPC], [0, DH]], channel_multiplier=-1)
            g.affine_select(out=head_mask[:, :], in_=head_mask[:, :], compare_op=ALU.is_ge, fill=0.0, base=DH - 1,
                            pattern=[[DH, H]], channel_multiplier=-1).then_inc(consts_ready, 1)

            def first_block(i, head, tail, late):
                def root(k, d):
                    n = norms[k]
                    for q in range(2):
                        pool.wait_ge(N["var_" + k], nth(i, q, 2 * d))
                        step.after(step.mark(g.tensor_tensor(n["rstd"][q][:, :], n["var"][q][:, :], neg_half[:, :], ALU.pow)))
                        g.tensor_tensor(n["shift"][q][:, :], n["neg_mean"][q][:, :], n["rstd"][q][:, :], ALU.mult)\
                            .then_inc(N["rstd_" + k], 1)

                if head:
                    root("x", 1)
                if late:
                    root("n", -1)
                if head:
                    root("a", 1)
                if tail:
                    root("s", 0)
                    for q in range(2):
                        pool.wait_ge(x2g_ready, nth(i, q))
                        if late:
                            pool.wait_ge(x_kept, nth(i, q, -2))
                            pool.wait_ge(xf_ready, nth(i, q, -2))
                        g.tensor_tensor(xn[q][:, :, :], x1b[q][:, :, :], xb_all[:, pair_tiles(i, 0, q), :], ALU.add).then_inc(xn_ready, 1)
                if head:
                    if not tail:
                        pool.wait_ge(weights_in, 16 * 14)
                        step.after(step.mark(g.tensor_tensor(gb[:, B2, :], gb[:, B2, :], gb[:, BE1, :], ALU.add)))
                    for q in range(2):
                        pool.wait_ge(x1g_ready, nth(i, q, 2))
                        if tail:
                            pool.wait_ge(xn_ready, nth(i, q))
                        g.tensor_tensor(x1b[q][:, :, :], sm[q][:, :, :], gb[:, B2, :].unsqueeze(1).broadcast_to([P, GT, C]),
                                        ALU.add).then_inc(x1b_ready, 1)
                if head and not tail:
                    pool.wait_ge(x_loaded[0], 32)
                    pool.wait_ge(x_loaded[1], 16 * (NG - 2))
                    toks = []
                    for b in range(NG):
                        t = slice(b * GT, (b + 1) * GT)
                        toks.append(step.mark(g.tensor_tensor(xb_all[:, t, :], x_all[:, t, :],
                                                              gb[:, BE2, :].unsqueeze(1).broadcast_to([P, GT, C]), ALU.add)))
                    step.after(toks[-1])

            run_pairs(pool, first_block, step, A_POOL)

            def experts(run):
                def issue_gather(s):
                    pool.sem_inc(pool_held, 1)
                    for t in range(GT):
                        g.indirect_dma_start(gathered[s][:, t, :], None, xf_dram[:, :],
                                             bass.IndirectOffsetOnAxis(gather_idx[s][:, t:t + 1], 0))\
                            .then_inc(gathered_in[s], 16)

                def issue_scatter(s):
                    pool.sem_inc(pool_held, 1)
                    for t in range(GT):
                        g.indirect_dma_start(y_dram[:, :], bass.IndirectOffsetOnAxis(scatter_idx[s][:, t:t + 1], 0),
                                             expert_out[s][:, t, :], None).then_inc(scattered[s], 16)

                for n in range(HS):
                    pool.wait_ge(hi_one_ready, run * HS + n + 1)
                    g.tensor_tensor(hi_hot[:, hot_part(n), 1, :], hi_one[:, hot_part(n), :],
                                    iota_lo[:, hot_part(n)].unsqueeze(2).broadcast_to([P, CPS, NHI]), ALU.mult).then_inc(hi_col_ready, 1)
                pool.wait_ge(index_ready, run + 1)
                for q in range(2):
                    pool.wait_ge((xf_stored, b_xf_stored)[run][q], 16 * NI)
                for s in range(2):
                    g_tok = step.mark(g.tensor_copy(gather_idx[s][:, :], gather_all[:, s * GT:(s + 1) * GT]))
                    step.after(g_tok)
                    issue_gather(s)

                def work(i, s, ahead):
                    if ahead:
                        pool.wait_ge(gather_idx_ready, nth(i, s, base=run * (NB - 2)))
                        issue_gather(s)
                    if run == 0:
                        return
                    pool.wait_ge(eo_ready, nth(i, s, base=run * NB))
                    issue_scatter(s)

                for s in range(2):
                    work(0, s, True)
                with pool.Fori(1, NB // 2 - 1) as i:
                    for s in range(2):
                        work(i, s, True)
                for s in range(2):
                    work(NB // 2 - 1, s, False)

            experts(0)

            position = posi[:, 0, :].rearrange("p (s t) -> p s t", s=SLOTS)

            def y_indices(b):
                pool.sem_inc(pool_held, 1)
                return step.mark(g.tensor_copy(y_idx[b.q][:, :, :], position[:, :, bass.ds(b.tile(), GT)]))

            def y_gather(b, s):
                for t in range(GT):
                    g.indirect_dma_start(y_in[b.q][:, s, t, :], None, y_dram[:, :],
                                         bass.IndirectOffsetOnAxis(y_idx[b.q][:, s, t:t + 1], 0)).then_inc(y_gathered[b.q], 16)

            def inverse_root_of(w, b):
                _, _, var_w, neg_w, rstd_w, shift_w = ln[w]
                pool.wait_ge(S["var_" + w], b.n())
                tok = step.mark(g.tensor_tensor(rstd_w[:, :], var_w[:, :], neg_half[:, :], ALU.pow))
                step.after(tok)
                g.tensor_tensor(shift_w[:, :], neg_w[:, :], rstd_w[:, :], ALU.mult).then_inc(S["rstd_" + w], 1)

            for q in range(2):
                pool.wait_ge(eo_stored[q], 16 * (NB // 2))
            step.after(y_indices(Batch(0, 0)))
            for s in range(SLOTS):
                y_gather(Batch(0, 0), s)

            def attention_step(b, head, feat, tail, late):
                more = head and not (isinstance(b.i, int) and b.off == NG - 2)
                if late:
                    inverse_root_of("t", b.plus(-2))
                if more:
                    y = b.plus(2)
                    if feat:
                        pool.wait_ge(S["var_h"], b.n())
                    tok = y_indices(y)
                    step.after(tok)
                    pool.sem_inc(pool_held, 1)
                    y_gather(y, 0)
                if feat:
                    pool.wait_ge(S["scale"], b.n())
                    g.tensor_tensor(vk[b.q][:, 0, :, :].rearrange("p t (h d) -> p t h d", h=H),
                                    v_sb.rearrange("p t (h d) -> p t h d", h=H),
                                    scl[:, :, H:2 * H].unsqueeze(3).broadcast_to([P, GT, H, DH]), ALU.mult)\
                        .then_inc(S["vk"], 1)
                    g.tensor_copy(vk[b.q][:, 1, :, :].rearrange("p t (h d) -> p t h d", h=H),
                                  scl[:, :, H:2 * H].unsqueeze(3).broadcast_to([P, GT, H, DH])).then_inc(S["krep"], 1)
                if head:
                    inverse_root_of("h", b.plus(1))
                if more:
                    y_gather(y, 1)

            run_pipeline(pool, attention_step, step, ATT_POOL)
            experts(1)
            for n, b in enumerate(SHARED_GROUPS):
                y0, y1 = [y_all[b % 2][:, s, b // 2, :, :] for s in range(SLOTS)]
                x_b = x_all[:, b * GT:(b + 1) * GT, :]
                pool.wait_ge(weighted, SLOTS * n + 1)
                step.after(step.mark(g.tensor_tensor(y0, y0, x_b, ALU.add)))
                pool.wait_ge(weighted, SLOTS * n + 2)
                g.tensor_tensor(x_b, y0, y1, ALU.add).then_inc(shared_out_ready, 1)

        @block.scalar
        def _(act):
            a = nc.scalar.activation
            act.wait_ge(consts_ready, 1)

            def first_block(i, head, tail, late):
                def normalised(k, d, dst, src, signal):
                    for q in range(2):
                        act.wait_ge(N["rstd_" + k], nth(i, q, 2 * d))
                        if k == "n":
                            act.wait_ge(xf_free[q], i)
                        for t in range(GT):
                            ins = a(dst[q][:, t:t + 1, :], src(q, t), ACT.Identity, bias=norms[k]["shift"][q][:, t:t + 1],
                                    scale=norms[k]["rstd"][q][:, t:t + 1])
                        ins.then_inc(signal, 1)

                def relu(q):
                    for half in range(2):
                        act.wait_ge(h_psum, i * 4 + (2 * q + half + 1))
                        a(hid[q][:, 2 * half:2 * half + 2, :], F[:, 2 * half:2 * half + 2, :], ACT.Relu).then_inc(h_ready, 1)

                if tail:
                    for q in range(2):
                        act.wait_ge(qt_psum, nth(i, q))
                        a(q_t[q][:, :], TA[q][:, :].bitcast(BF16)[:, 0:GN], ACT.Copy).then_inc(qt_ready, 1)
                if tail:
                    relu(0)
                if head:
                    normalised("x", 1, yt, lambda q, t: x_all[:, bass.ds(i * (2 * GT) + (2 * GT + q * GT + t), 1), :], turns_ready)
                if tail:
                    relu(1)
                if head:
                    for q in range(2):
                        act.wait_ge(angle_ready, nth(i, q, 2))
                        a(ct[q][:, :, :], rt[q][:, :, :], ACT.Sin, bias=half_pi[:, 0:1], scale=-TWO_PI).then_inc(cos_ready, 1)
                if late:
                    normalised("n", -1, xf, lambda q, t: xn[q][:, t:t + 1, :], xf_ready)
                    for q in range(2):
                        a(x_all[:, pair_tiles(i, -1, q), :], xn[q][:, :, :], ACT.Copy).then_inc(x_kept, 1)
                    for q in range(2):
                        act.wait_ge(xft_psum, nth(i, q, -2))
                        a(xft[q][:, :], TA[q][:, :], ACT.Copy).then_inc(xft_ready, 1)
                if head:
                    normalised("a", 1, sm, lambda q, t: sm[q][:, t:t + 1, :], za_ready)
                if tail:
                    normalised("s", 0, x1b, lambda q, t: x1b[q][:, t:t + 1, :], zs_ready)
                if head:
                    for q in range(2):
                        act.wait_ge(qangle_ready, nth(i, q, 2))
                        a(qc[q][:, :, :], q_ang[q][:, 1, :, :], ACT.Sin, bias=half_pi[:, 0:1], scale=-TWO_PI).then_inc(qcos_ready, 1)

            act.wait_ge(x_loaded[0], 32)
            run_pairs(act, first_block)

            def route(run):
                act.wait_ge(gap_ready, run + 1)
                a(gate[:, 1, :], gate[:, 0, :], ACT.Exp).then_inc(gap_exp, 1)
                for n in range(HS):
                    act.wait_ge(hi_one_ready, run * HS + n + 1)
                    a(hi_hot[:, hot_part(n), 0, :], hi_one[:, hot_part(n), :], ACT.Copy, scale=pcol[:, 0:1]).then_inc(hi_row_ready, 1)

            def experts(run):
                def work(i, s):
                    for half in range(2):
                        act.wait_ge(eh_psum, i * 4 + (2 * s + half + 1 + run * 2 * NB))
                        a(hid[s][:, 2 * half:2 * half + 2, :], F[:, 2 * half:2 * half + 2, :], ACT.Gelu).then_inc(eh_ready, 1)

                with act.Fori(0, NB // 2) as i:
                    for s in range(2):
                        work(i, s)

            route(0)
            experts(0)
            def out_of_psum(ready, value, dst, src, signal):
                act.wait_ge(S[ready], value)
                a(dst, src, ACT.Copy).then_inc(S[signal], 1)

            def normalise(w, b, dst, signal):
                rstd_w, shift_w = ln[w][4:]
                act.wait_ge(S["rstd_" + w], b.n())
                for t in range(GT):
                    ins = a(dst[:, t:t + 1, :], x_all[:, bass.ds(b.tile() + t, 1), :], ACT.Identity,
                            bias=shift_w[:, t:t + 1], scale=rstd_w[:, t:t + 1])
                ins.then_inc(S[signal], 1)

            def attention_step(b, head, feat, tail, late):
                h, t_, l_ = b.plus(1), b.plus(-1), b.plus(-2)

                def unit(bb, u):
                    kind, half, r = u // 2, u % 2, u % 2
                    if kind == 0:
                        dst = [kfeat[bb.q][:, 2 * half:2 * half + 2, sc, :] for sc in range(2)]
                    else:
                        dst = [qfeat[bb.q][:, sc, 2 * half:2 * half + 2, :] for sc in range(2)]
                    act.wait_ge(S["ang"], bb.k(u, 4))
                    a(dst[0], ang[r].rearrange("p (a b) -> p a b", a=2), ACT.Sin, scale=TWO_PI)
                    act.wait_ge(S["abs"], bb.k(u, 4))
                    a(dst[1], ang_abs[r].rearrange("p (a b) -> p a b", a=2), ACT.Sin, bias=half_pi[:, 0:1], scale=-TWO_PI)\
                        .then_inc(S["feat"], 1)

                if late:
                    normalise("t", l_, xf[l_.q], "xf")
                if feat:
                    act.wait_ge(S["nrm"], b.n())
                    a(scl[:, :, :], nrm[:, :, :], ACT.Exp, scale=-0.5).then_inc(S["scale"], 1)
                if tail:
                    act.wait_ge(S["num_psum"], t_.n())
                    a(num_s, T_A[:, :].rearrange("p (t c) -> p t c", t=GT), ACT.Copy)
                    a(den_s, T_B[:, :].rearrange("p (t c) -> p t c", t=GT), ACT.Copy).then_inc(S["num"], 1)
                if late:
                    out_of_psum("xft_psum", l_.n(), xrt[:, :], H_B[:, :], "xft")
                if feat:
                    unit(b, 1)
                    unit(b, 2)
                if head:
                    normalise("h", h, ax, "ax")
                if feat:
                    out_of_psum("kvt_psum", b.n(), kvt[b.q], H_A[:, :].rearrange("p (a c) -> p a c", a=4), "kvt")
                if head:
                    out_of_psum("axt_psum", h.n(), xt_part[h.q][0][:, :], H_B[:, :], "axt")
                if feat:
                    unit(b, 3)
                if tail:
                    out_of_psum("attt_psum", t_.n(), att_t[:, :], T_A[:, :], "attt")
                if head:
                    for t in range(GT):
                        bank = (H_A, H_B)[t % 2]
                        act.wait_ge(S["qkv_psum"], h.k(t, 4))
                        a(sq[:, t, :], bank[:, 0:2 * C], ACT.Square)
                        a(v_sb[:, t, :], bank[:, 2 * C:3 * C], ACT.Copy).then_inc(S["qkv_used"], 1)
                    unit(h, 0)

            run_pipeline(act, attention_step)
            route(1)
            experts(1)
            for b in SHARED_GROUPS:
                act.wait_ge(y_loaded[b], 16 * SLOTS)
                for s in range(SLOTS):
                    for t in range(GT):
                        y = y_all[b % 2][:, s, b // 2, t, :]
                        ins = a(y, y, ACT.Copy, scale=w_slot[:, s, b * GT + t:b * GT + t + 1])
                    ins.then_inc(weighted, 1)

        @block.vector
        def _(dve):
            v = nc.vector
            step = Steps(dve, dve_steps)
            MARK = step.mark

            dve.wait_ge(consts_ready, 1)
            v.tensor_copy(identb[:, :], ident[:, :]).then_inc(setup_dve, 1)
            v.tensor_copy(iota_lo[:, :], iota_i[:, :])
            v.tensor_copy(pcol[:, :], pcol_i[:, :])
            def split_weights():
                dve.wait_ge(weights_in, 16 * 14)
                v.tensor_copy(rf_rep[:, :, :], rf_nat[:, :].unsqueeze(1).broadcast_to([M, H, DH])).then_inc(setup_dve, 1)
                split = w1_split
                rest = q_rest[0][:, 0, :, :].rearrange("p a b -> p (a b)")
                rest = rest.rearrange("p (c k) -> p c k", c=FC)
                rest_b = posf[:, 0:FC].unsqueeze(2)
                wn, bn = w1_nat[:, :, 0:NQ], w1_nat[:, :, NQ:NQ + 1]
                k6 = 6 * NQ

                def cols(part, n=NQ):
                    return split[:, :, part * NQ:part * NQ + n]
                t = MARK(v.tensor_copy(cols(0), wn))
                MARK(v.tensor_copy(cols(3), wn))
                MARK(v.tensor_copy(cols(5), wn))
                t = MARK(v.tensor_copy(split[:, :, k6:k6 + 1], bn))
                step.after(t)
                MARK(v.tensor_tensor(rest, wn, cols(0), ALU.subtract))
                t = MARK(v.tensor_tensor(rest_b, bn, split[:, :, k6:k6 + 1], ALU.subtract))
                step.after(t)
                MARK(v.tensor_copy(cols(1), rest))
                MARK(v.tensor_copy(cols(4), rest))
                t = MARK(v.tensor_copy(split[:, :, k6 + 1:k6 + 2], rest_b))
                step.after(t)
                MARK(v.tensor_tensor(rest, rest, cols(1), ALU.subtract))
                t = MARK(v.tensor_tensor(rest_b, rest_b, split[:, :, k6 + 1:k6 + 2], ALU.subtract))
                step.after(t)
                v.tensor_copy(cols(2), rest)
                v.tensor_copy(split[:, :, k6 + 2:k6 + 3], rest_b).then_inc(w_split_ready, 1)

            def finish_weights():
                dve.wait_ge(setup_pe, 1)
                v.tensor_copy(w1k[:, :], F[:, 0, :].bitcast(BF16)[:, 0:FF])
                v.tensor_copy(w2t[:, :, :].rearrange("p a b -> p (a b)"), F[:, 1, :])
                step.after(MARK(v.tensor_copy(wqkv_part[0][:, :], F[:, 2, 0:3 * C])))
                v.tensor_tensor(wqkv_part[1][:, :], F[:, 2, 0:3 * C], wqkv_part[0][:, :].bitcast(F32), ALU.subtract)
                v.tensor_copy(wot[:, :], F[:, 2, 3 * C:4 * C])
                v.tensor_copy(wrt[:, :], F[:, 3, 0:NE])
                v.scalar_tensor_tensor(rf_block[:, :, :], F[:, 3, P:P + M].unsqueeze(1).broadcast_to([P, H, M]), TURN,
                                       head_mask[:, :].unsqueeze(2).broadcast_to([P, H, M]), ALU.mult, ALU.mult)\
                    .then_inc(setup_dve, 1)
                dve.wait_ge(setup_pe, 2)
                v.tensor_copy(wqf[:, :], TA[0][:, :])
                v.tensor_copy(wkf[:, :], TA[1][:, :]).then_inc(weights_ready, 1)

            def split(part, src):
                step.after(MARK(v.tensor_copy(part[0][:, :], src)))
                return v.tensor_tensor(part[1][:, :], src, part[0][:, :].bitcast(F32), ALU.subtract)

            def magnitude(dst, src):
                return v.tensor_scalar(dst.bitcast(I32), src.bitcast(I32), 0x7FFFFFFF, None, ALU.bitwise_and)

            def first_block(i, head, tail, late):
                def ln_stats(k, src, scale=1.0):
                    n = norms[k]
                    tok = []
                    for q in range(2):
                        for t in range(GT):
                            ins = v.bn_stats(n["stats"][q][:, t, :], src(q, t))
                        tok.append(MARK(ins))
                    for q in range(2):
                        step.after(tok[q])
                        dve.sem_inc(dve_held, 1)
                        for t in range(GT):
                            ins = v.bn_aggr(n["mv"][q][:, t, :], n["stats"][q][:, t, :])
                        tok[q] = MARK(ins)
                    for q in range(2):
                        step.after(tok[q])
                        v.tensor_scalar(n["neg_mean"][q][:, :], n["mv"][q][:, :, 0], -1.0, None, ALU.mult)
                        v.tensor_scalar(n["var"][q][:, :], n["mv"][q][:, :, 1], EPS, scale, ALU.add, ALU.mult)\
                            .then_inc(N["var_" + k], 1)

                def times_gamma(ready, d, dst, src, gamma_row, signal):
                    for q in range(2):
                        dve.wait_ge(ready, nth(i, q, 2 * d))
                        v.tensor_tensor(dst[q][:, :, :], src[q][:, :, :], gb[:, gamma_row, :].unsqueeze(1).broadcast_to([P, GT, C]),
                                        ALU.mult).then_inc(signal, 1)

                tok = [0, 0]
                if head and tail and not late:
                    dve.wait_ge(x_loaded[1], 16 * (NG - 2))
                if head:
                    ln_stats("x", lambda q, t: x_all[:, bass.ds(i * (2 * GT) + (2 * GT + q * GT + t), 1), :].rearrange("p a c -> p (a c)"),
                             (2 * math.pi) ** 2)
                if head and not tail:
                    split_weights()
                if late:
                    for q in range(2):
                        dve.wait_ge(xn_ready, nth(i, q, -2))
                    ln_stats("n", lambda q, t: xn[q][:, t, :])
                if head:
                    for q in range(2):
                        dve.wait_ge(turns_ready, nth(i, q, 2))
                        tok[q] = MARK(v.tensor_scalar(rt[q][:, :, :], yt[q][:, :, :], ROUND, ROUND, ALU.add, ALU.subtract))
                    for q in range(2):
                        step.after(tok[q])
                        tok[q] = MARK(v.tensor_tensor(rt[q][:, :, :], yt[q][:, :, :], rt[q][:, :, :], ALU.subtract))
                    for q in range(2):
                        step.after(tok[q])
                        magnitude(rt[q][:, :, :], rt[q][:, :, :]).then_inc(angle_ready, 1)
                    cv = [ct[q][:, :, :].rearrange("p t (h d) -> p (t h) d", d=DH) for q in range(2)]
                    for q in range(2):
                        dve.wait_ge(cos_ready, nth(i, q, 2))
                    for d in range(1, DH):
                        for q in range(2):
                            if d > 1:
                                step.after(tok[q])
                            tok[q] = MARK(v.tensor_tensor(cv[q][:, :, d], cv[q][:, :, d], cv[q][:, :, d - 1], ALU.mult))
                    for q in range(2):
                        if tail:
                            dve.wait_ge(x1b_ready, nth(i, q))
                        step.after(tok[q])
                        tok[q] = MARK(v.scalar_tensor_tensor(sm[q][:, :, :], yt[q][:, :, :], 2 * math.pi, ct[q][:, :, :],
                                                             ALU.mult, ALU.add))
                    for q in range(2):
                        step.after(tok[q])
                    ln_stats("a", lambda q, t: sm[q][:, t, :])
                if tail:
                    for q in range(2):
                        dve.wait_ge(ffn_psum, nth(i, q))
                        dve.wait_ge(x1b_ready, nth(i, q))
                        tok[q] = MARK(v.tensor_tensor(x1b[q][:, :, :].rearrange("p a b -> p (a b)"), TB[q][:, :],
                                                      x1b[q][:, :, :].rearrange("p a b -> p (a b)"), ALU.add))
                    for q in range(2):
                        step.after(tok[q])
                    ln_stats("s", lambda q, t: x1b[q][:, t, :])
                if head:
                    times_gamma(za_ready, 1, sm, sm, G1, x1g_ready)
                    qy = [q_rest[q][:, 0, :, :] for q in range(2)]
                    for q in range(2):
                        dve.wait_ge(x1g_ready, nth(i, q, 2))
                        tok[q] = MARK(v.tensor_tensor(qy[q], sm[q][:, :, 0:NQ],
                                                      gb[:, BE1, 0:NQ].unsqueeze(1).broadcast_to([P, GT, NQ]), ALU.add))
                    for q in range(2):
                        step.after(tok[q])
                        tok[q] = MARK(v.tensor_scalar(qy[q], qy[q], TURN, None, ALU.mult))
                    for q in range(2):
                        step.after(tok[q])
                        tok[q] = MARK(v.tensor_scalar(q_ang[q][:, 0, :, :], qy[q], ROUND, ROUND, ALU.add, ALU.subtract))
                    for q in range(2):
                        step.after(tok[q])
                        tok[q] = MARK(v.tensor_tensor(q_ang[q][:, 0, :, :], qy[q], q_ang[q][:, 0, :, :], ALU.subtract))
                    for q in range(2):
                        step.after(tok[q])
                        magnitude(q_ang[q][:, 1, :, :], q_ang[q][:, 0, :, :]).then_inc(qangle_ready, 1)
                if late:
                    for q in range(2):
                        dve.wait_ge(logit_psum, nth(i, q, -2))
                        v.tensor_copy(logits[:, :, pair_tiles(i, -1, q)].rearrange("p e t -> p t e"),
                                      TA[q][:, 0:GT * NE].rearrange("p (t e) -> p t e", e=NE)).then_inc(logit_ready, 1)
                if tail:
                    times_gamma(zs_ready, 0, x1b, x1b, G2, x2g_ready)
                if head:
                    for q in range(2):
                        dve.wait_ge(qcos_ready, nth(i, q, 2))
                    k = 1
                    while k < NQ:
                        for q in range(2):
                            b = qc[q][:, :, :].rearrange("p t (n two k) -> p (t n) two k", two=2, k=k)
                            if k > 1:
                                step.after(tok[q])
                            nb = GT * NQ // (2 * k)
                            tok[q] = MARK(v.tensor_tensor(b[:, :, 1, :], b[:, :, 1, :],
                                                          b[:, :, 0, k - 1:k].broadcast_to([P, nb, k]), ALU.mult))
                        k *= 2

                    def part(q, first, n):
                        return q_split[q][:, :, first * NQ:(first + n) * NQ].rearrange("p t (n k) -> p t n k", n=n)

                    def spread(src, n):
                        return src.unsqueeze(2).broadcast_to([P, GT, n, NQ])
                    for q in range(2):
                        step.after(tok[q])
                        tok[q] = MARK(v.tensor_copy(part(q, 0, 3), spread(qc[q][:, :, :], 3)))
                    for q in range(2):
                        step.after(tok[q])
                        tok[q] = MARK(v.tensor_tensor(q_rest[q][:, 0, :, :], qc[q][:, :, :], q_split[q][:, :, 0:NQ], ALU.subtract))
                    for q in range(2):
                        step.after(tok[q])
                        tok[q] = MARK(v.tensor_copy(part(q, 3, 2), spread(q_rest[q][:, 0, :, :], 2)))
                    for q in range(2):
                        step.after(tok[q])
                        tok[q] = MARK(v.tensor_tensor(q_rest[q][:, 1, :, :], q_rest[q][:, 0, :, :],
                                                      q_split[q][:, :, 3 * NQ:4 * NQ], ALU.subtract))
                    for q in range(2):
                        step.after(tok[q])
                        v.tensor_copy(q_split[q][:, :, 5 * NQ:6 * NQ], q_rest[q][:, 1, :, :]).then_inc(qsplit_ready, 1)
                if head and not tail:
                    finish_weights()

            dve.wait_ge(x_loaded[0], 32)
            run_pairs(dve, first_block, step, A_DVE)

            def route(run):
                def chain(ins):
                    step.after(MARK(ins))

                def over_e(ap):
                    return ap.rearrange("p e t -> p t e")

                def tb(ap):
                    return ap.unsqueeze(1).broadcast_to([P, NE, NT])
                if run == 0:
                    dve.wait_ge(logit_ready, nth(NI - 1, 1))
                else:
                    dve.wait_ge(S["logit_read"], NG)
                src = logits
                for s in range(SLOTS):
                    chain(v.tensor_reduce(top[:, s, :], over_e(src[:, :, :]), AX.X, ALU.max))
                    chain(v.tensor_tensor(eq[:, :, :], src[:, :, :], tb(top[:, s, :]), ALU.is_equal))
                    chain(v.tensor_tensor(order_key[:, :, :], eq[:, :, :], first_bonus[:, :, :], ALU.mult))
                    chain(v.tensor_reduce(key_max[:, :], over_e(order_key[:, :, :]), AX.X, ALU.max))
                    chain(v.tensor_tensor(pick[:, s, :, :], order_key[:, :, :], tb(key_max[:, :]), ALU.is_equal))
                    if s == 0:
                        chain(v.scalar_tensor_tensor(masked[:, :, :], pick[:, 0, :, :], -3.0e38, logits[:, :, :],
                                                     ALU.mult, ALU.add))
                        src = masked
                v.tensor_tensor(picked[:, :, :], pick[:, 0, :, :], pick[:, 1, :, :], ALU.add).then_inc(picked_ready, 1)
                v.tensor_tensor(gate[:, 0, :], top[:, 1, :], top[:, 0, :], ALU.subtract).then_inc(gap_ready, 1)
                dve.wait_ge(gap_exp, run + 1)
                chain(v.tensor_scalar(gate[:, 2, :], gate[:, 1, :], 1.0, None, ALU.add))
                chain(v.reciprocal(w_slot[:, 0, :], gate[:, 2, :]))
                MARK(v.tensor_tensor(w_slot[:, 1, :], gate[:, 1, :], w_slot[:, 0, :], ALU.mult))
                dve.wait_ge(count_psum, run + 1)
                for h in range(2):
                    ins = v.tensor_scalar(count_b[:, h, :], ones_row[:, :], TB[0][:, h:h + 1], None, ALU.mult)
                ins.then_inc(count_ready, 1)
                dve.wait_ge(pos_psum, run + 1)
                pos = TA[0][:, 0:NE * NT].rearrange("p (e t) -> p e t", e=NE)
                for s in range(SLOTS):
                    dst = (eq, order_key)[s]
                    chain(v.tensor_tensor(dst[:, :, :], pick[:, s, :, :], pos, ALU.mult))
                    chain(v.tensor_reduce(posf[:, s * NT:(s + 1) * NT], over_e(dst[:, :, :]), AX.X, ALU.add))
                chain(v.tensor_copy(posi[:, 0, :], posf[:, :]))
                MARK(v.tensor_scalar(posi[:, 1, :], posi[:, 0, :], 7, None, ALU.logical_shift_right))
                chain(v.tensor_scalar(posi[:, 2, :], posi[:, 0, :], P - 1, None, ALU.bitwise_and))
                v.tensor_copy(hilo[:, :, :], posi[:, 1:3, :]).then_inc(hilo_ready, 1)
                dve.wait_ge(hilo_ready, run + 1)
                for n in range(HS):
                    v.tensor_tensor(hi_one[:, hot_part(n), :], iota_lo[:, 0:NHI].unsqueeze(1).broadcast_to([P, CPS, NHI]),
                                    hilo[:, 0, hot_part(n)].unsqueeze(2).broadcast_to([P, CPS, NHI]), ALU.is_equal)\
                        .then_inc(hi_one_ready, 1)
                for s in range(NTS):
                    v.tensor_scalar(lo_hot[:, s, :], iota_lo[:, :], hilo[:, 1, s:s + 1], None, ALU.is_equal).then_inc(lo_ready, 1)
                dve.wait_ge(inv_psum, run + 1)
                chain(v.tensor_copy(at_pos[:, :, :].rearrange("p k c -> p (k c)"), TB[1][:, 0:2 * NHI]))
                chain(v.scalar_tensor_tensor(row_f[:, 0, :], at_pos[:, 1, :], float(P), at_pos[:, 0, :], ALU.mult, ALU.add))
                chain(v.tensor_scalar(row_f[:, 1, :], row_f[:, 0, :], float(NTOK), -float(NTOK), ALU.is_ge, ALU.mult))
                v.tensor_copy(scatter_all[:, :], row_f[:, 0, :])
                v.tensor_tensor(gather_all[:, :], row_f[:, 0, :], row_f[:, 1, :], ALU.add).then_inc(index_ready, 1)

            def experts(run):
                def split_weights_of(k, e):
                    dve.wait_ge(ew_loaded[e], k * 32 + (32 + run * 32 * (NE // 2)))
                    split(ew1_part[e], ew1_sb[e][:, :]).then_inc(ew1_split, 1)

                def take_rows(i, s, more=True):
                    dve.wait_ge(gt_psum, nth(i, s, base=run * NB))
                    split(xt_part[s], TA[s][:, :]).then_inc(gt_ready, 1)
                    if more:
                        v.tensor_copy(gather_idx[s][:, :], gather_all[:, bass.ds(i * (2 * GT) + (s + 2) * GT, GT)])\
                            .then_inc(gather_idx_ready, 1)

                def give_rows(i, s, first):
                    dve.wait_ge(eo_psum, nth(i, s, base=run * NB))
                    if not first:
                        dve.wait_ge((eo_stored, scattered)[run][s], i * (16, 16 * GT)[run])
                    if run == 1:
                        v.tensor_copy(scatter_idx[s][:, :], scatter_all[:, bass.ds(i * (2 * GT) + s * GT, GT)])
                    v.tensor_copy(expert_out[s][:, :, :].rearrange("p a b -> p (a b)"), TB[s][:, :]).then_inc(eo_ready, 1)

                def expert(k, e, more=True):
                    i = k * 2 + e
                    take_rows(i, 1)
                    give_rows(i, 0, False)
                    take_rows(i + 1, 0, more)
                    split_weights_of(k + e, 1 - e)
                    give_rows(i, 1, False)

                split_weights_of(0, 0)
                split_weights_of(0, 1)
                take_rows(0, 0)
                take_rows(0, 1)
                give_rows(0, 0, True)
                take_rows(1, 0)
                give_rows(0, 1, True)
                expert(0, 1)
                with dve.Fori(1, NE // 2 - 1) as k:
                    step.loop(k, 6, 1)
                    expert(k, 0)
                    expert(k, 1)
                step.end(NE // 2 - 1)
                expert(NE // 2 - 1, 0, more=False)
                take_rows(NE - 1, 1, more=False)
                give_rows(NE - 1, 0, False)
                give_rows(NE - 1, 1, False)

            def combine(n, pair):
                toks = []
                for s in range(SLOTS):
                    for q, b in enumerate(pair):
                        if s == 0:
                            dve.wait_ge(y_loaded[b], 16 * SLOTS)
                            if n:
                                dve.wait_ge(out_ready, 2 * n - 1 + q)
                        else:
                            step.after(toks[q])
                        for t in range(GT):
                            tile = b * GT + t
                            src, dst = ((x_all[:, tile, :], sm[q][:, t, :]), (sm[q][:, t, :], x_all[:, tile, :]))[s]
                            ins = v.scalar_tensor_tensor(dst, y_all[b % 2][:, s, b // 2, t, :], w_slot[:, s, tile:tile + 1], src,
                                                         ALU.mult, ALU.add)
                        if s == 0:
                            toks.append(MARK(ins))
                        else:
                            ins.then_inc(out_ready, 1)

            route(0)
            experts(0)

            def attention_step(b, head, feat, tail, late):
                h, t_, l_ = b.plus(1), b.plus(-1), b.plus(-2)

                def stats_of(w, bb):
                    dve.sem_inc(dve_held, 1)
                    for t in range(GT):
                        ins = v.bn_stats(ln[w][0][:, t, :], x_all[:, bass.ds(bb.tile() + t, 1), :].rearrange("p a c -> p (a c)"))
                    return MARK(ins)

                def aggregate(w, tok):
                    st, mv_w = ln[w][0:2]
                    step.after(tok)
                    dve.sem_inc(dve_held, 1)
                    for t in range(GT):
                        ins = v.bn_aggr(mv_w[:, t, :], st[:, t, :])
                    return MARK(ins)

                def finish_stats(w, tok):
                    _, mv_w, var_w, neg_w = ln[w][0:4]
                    step.after(tok)
                    v.tensor_scalar(neg_w[:, :], mv_w[:, :, 0], -1.0, None, ALU.mult)
                    v.tensor_scalar(var_w[:, :], mv_w[:, :, 1], EPS, None, ALU.add).then_inc(S["var_" + w], 1)

                def unit_views(u):
                    r = u % 2
                    return F[:, 2 * r:2 * r + 2, :], ang[r].rearrange("p (a b) -> p a b", a=2)

                def round_(bb, u, first=False):
                    src, dst = unit_views(u)
                    dve.wait_ge(S["proj_psum"], bb.k(u, 4))
                    if not first:
                        dve.wait_ge(S["feat"], bb.k(u - 2, 4))
                    return MARK(v.tensor_scalar(dst, src, ROUND, ROUND, ALU.add, ALU.subtract))

                def less(u, tok):
                    src, dst = unit_views(u)
                    step.after(tok)
                    v.tensor_tensor(dst, src, dst, ALU.subtract).then_inc(S["ang"], 1)

                def absolute(bb, u):
                    dve.wait_ge(S["ang"], bb.k(u, 4))
                    magnitude(ang_abs[u % 2], ang[u % 2]).then_inc(S["abs"], 1)

                def add_expert(s, tok):
                    if s == 0:
                        dve.wait_ge(y_gathered[h.q], h.turns(16 * SLOTS * GT))
                    step.after(tok)
                    for t in range(GT):
                        if s == 0:
                            dst, add = sum0[:, t:t + 1, :], x_all[:, bass.ds(h.tile() + t, 1), :]
                        else:
                            dst, add = x_all[:, bass.ds(h.tile() + t, 1), :], sum0[:, t:t + 1, :]
                        ins = v.scalar_tensor_tensor(dst, y_in[h.q][:, s, t:t + 1, :], w_stage[h.q][:, s, t:t + 1], add,
                                                     ALU.mult, ALU.add)
                    return MARK(ins)

                if late:
                    dve.wait_ge(S["wo_psum"], l_.n())
                    for t in range(GT):
                        rows_t = x_all[:, bass.ds(l_.tile() + t, 1), :]
                        ins = v.tensor_tensor(rows_t, rows_t, T_B[:, t * P:(t + 1) * P].unsqueeze(1), ALU.add)
                    ins.then_inc(S["wo_used"], 1)
                if head:
                    w_tok = MARK(v.tensor_copy(w_stage[h.q][:, :, :], w_slot[:, :, bass.ds(h.tile(), GT)]))
                if late:
                    dve.wait_ge(S["wo_used"], l_.n())
                    l_tok = aggregate("t", stats_of("t", l_))
                    dve.wait_ge(b_xf_free[l_.q], l_.turns())
                    finish_stats("t", l_tok)
                if tail:
                    dve.wait_ge(S["kv_psum"], t_.n())
                    v.tensor_tensor(kvm[:, :, :, :].rearrange("p a j v -> p (a j) v"),
                                    T_B[:, :].rearrange("p (a v) -> p a v", v=HPC * DH),
                                    kv_mask[:, :, :].rearrange("p a b -> p (a b)").unsqueeze(1)
                                    .broadcast_to([P, 4 * NJ, HPC * DH]), ALU.mult).then_inc(S["kvm"], 1)
                if feat:
                    dve.wait_ge(S["qkv_used"], b.k(3, 4))
                    v.tensor_reduce(nrm[:, :, :], sq.rearrange("p t (h d) -> p t h d", d=DH), AX.X, ALU.add)\
                        .then_inc(S["nrm"], 1)
                    tok = round_(b, 1, not tail)
                if head:
                    h_tok = add_expert(0, w_tok)
                if feat:
                    less(1, tok)
                if head:
                    h_tok = add_expert(1, h_tok)
                if feat:
                    absolute(b, 1)
                if head:
                    step.after(h_tok)
                    h_tok = stats_of("h", h)
                if feat:
                    tok = round_(b, 2)
                if head:
                    h_tok = aggregate("h", h_tok)
                if feat:
                    less(2, tok)
                if head:
                    finish_stats("h", h_tok)
                if late:
                    dve.wait_ge(S["logit_psum"], l_.n())
                    v.tensor_copy(logits[:, :, bass.ds(l_.tile(), GT)].rearrange("p e t -> p t e"),
                                  H_B[:, 0:GT * NE].rearrange("p (t e) -> p t e", e=NE)).then_inc(S["logit_read"], 1)
                if feat:
                    absolute(b, 2)
                    tok = round_(b, 3)
                    dve.wait_ge(S["scale"], b.n())
                if tail:
                    dve.wait_ge(S["numt_psum"], t_.n())
                    zz = T_B[:, :].rearrange("p (t h d) -> p t h d", t=GT, h=H)[:, :, :, 0]
                    t_tok = MARK(v.tensor_tensor(zq[:, 0, :, :], zz, q_scale[t_.q][:, :, :], ALU.mult))
                    step.after(t_tok)
                    t_tok = MARK(v.tensor_scalar(zq[:, 1, :, :], zq[:, 0, :, :], 1e-6, None, ALU.max))
                    if feat:
                        less(3, tok)
                    step.after(t_tok)
                    t_tok = MARK(v.reciprocal(zq[:, 2, :, :], zq[:, 1, :, :]))
                    if feat:
                        v.tensor_scalar(q_scale[b.q][:, :, :], scl[:, :, 0:H], 1.0 / M, None, ALU.mult)
                    step.after(t_tok)
                    t_tok = MARK(v.tensor_tensor(zq[:, 0, :, :], zq[:, 2, :, :], q_scale[t_.q][:, :, :], ALU.mult))
                    if feat:
                        absolute(b, 3)
                    step.after(t_tok)
                    v.tensor_tensor(att.rearrange("p t (h d) -> p t h d", h=H),
                                    T_A[:, :].rearrange("p (t h d) -> p t h d", t=GT, h=H),
                                    zq[:, 0, :, :].unsqueeze(3).broadcast_to([P, GT, H, DH]), ALU.mult)\
                        .then_inc(S["att"], 1)
                elif feat:
                    less(3, tok)
                    v.tensor_scalar(q_scale[b.q][:, :, :], scl[:, :, 0:H], 1.0 / M, None, ALU.mult)
                    absolute(b, 3)
                if head:
                    dve.wait_ge(S["axt"], h.n())
                    v.tensor_tensor(xt_part[h.q][1][:, :], H_B[:, :], xt_part[h.q][0][:, :].bitcast(F32), ALU.subtract)\
                        .then_inc(S["xt_lo"], 1)
                    tok = round_(h, 0, not feat)
                    less(0, tok)
                    absolute(h, 0)

            for part, w in zip(proj_part, (wqf, wkf)):
                split(part, w[:, :]).then_inc(proj_split, 1)
            run_pipeline(dve, attention_step, step, ATT_DVE)

            route(1)
            experts(1)
            for n in range(0, len(VECTOR_GROUPS), 2):
                combine(n // 2, VECTOR_GROUPS[n:n + 2])

        @block.tensor
        def _(pe):
            mm = nc.tensor.matmul
            tr = nc.tensor.transpose

            pe.wait_ge(weights_in, 16 * 14)
            pe.wait_ge(consts_ready, 1)
            pe.wait_ge(setup_dve, 2)
            pe.wait_ge(w_split_ready, 1)
            for c in range(FC):
                tr(F[:, 0, :].bitcast(BF16)[:, c * P:(c + 1) * P], w1_split[:, c, :], identb[:, :])
                tr(F[:, 1, c * P:(c + 1) * P], w2_nat[:, c * P:(c + 1) * P], ident[:, :])
                tr(F[:, 2, c * P:(c + 1) * P], w_nat[:, c, :], ident[:, :])
            tr(F[:, 3, 0:NE], wr_nat[:, :], ident[0:NE, 0:NE])
            mm(F[:, 3, P:P + M], rf_rep[:, :, :].rearrange("m h d -> m (h d)"), ident[0:M, 0:M], start=True, stop=True)\
                .then_inc(setup_pe, 1)
            pe.wait_ge(setup_dve, 3)
            rfb = rf_block[:, :, :].rearrange("p h m -> p (h m)")
            mm(TA[0][:, :], w_nat[:, 0, :], rfb, start=True, stop=True)
            mm(TA[1][:, :], w_nat[:, 1, :], rfb, start=True, stop=True).then_inc(setup_pe, 1)
            pe.wait_ge(weights_ready, 1)

            def four_transposes(dst, src, signal):
                for t in range(GT):
                    ins = tr(dst[:, t * P:(t + 1) * P], src(t), ident[:, :])
                ins.then_inc(signal, 1)

            def product(dst, w, x):
                mm(dst, w[0], x[0], start=True, stop=False)
                mm(dst, w[1], x[0], start=False, stop=False)
                return mm(dst, w[0], x[1], start=False, stop=True)

            def add_half(dst, half, hidden, w):
                for t in range(GT):
                    for c in (2 * half, 2 * half + 1):
                        ins = mm(dst[:, t * P:(t + 1) * P], hidden(c, t), w(c), start=(t == 0 and c == 0),
                                 stop=(t == GT - 1 and c == 3))
                return ins

            def first_block(i, head, tail, late):
                if tail:
                    for q in range(2):
                        pe.wait_ge(qsplit_ready, nth(i, q))
                        for t in range(GT):
                            ins = tr(TA[q][:, :].bitcast(BF16)[:, t * P:(t + 1) * P], q_split[q][:, t, :], identb[:, :])
                        ins.then_inc(qt_psum, 1)
                    for q in range(2):
                        pe.wait_ge(qt_ready, nth(i, q))
                        for c in range(FC):
                            if q == 1 and c % 2 == 0:
                                pe.wait_ge(h_ready, i * 4 + (c // 2 + 1))
                            ins = mm(F[:, c, :], w1k[:, c * P:(c + 1) * P], q_t[q][:, :], start=True, stop=True)
                            if c % 2:
                                ins.then_inc(h_psum, 1)
                    for q in range(2):
                        for half in range(2):
                            pe.wait_ge(h_ready, i * 4 + (2 * q + half + 1))
                            ins = add_half(TB[q], half, lambda c, t: hid[q][:, c, t * P:(t + 1) * P], lambda c: w2t[:, c, :])
                        ins.then_inc(ffn_psum, 1)
                if late:
                    for q in range(2):
                        pe.wait_ge(xf_ready, nth(i, q, -2))
                        four_transposes(TA[q], lambda t: xf[q][:, t, :], xft_psum)
                    for q in range(2):
                        pe.wait_ge(xft_ready, nth(i, q, -2))
                        for t in range(GT):
                            ins = mm(TA[q][:, t * NE:(t + 1) * NE], xft[q][:, t * P:(t + 1) * P], wrt[:, :], start=True, stop=True)
                        ins.then_inc(logit_psum, 1)

            run_pairs(pe, first_block)

            def route(run):
                pe.wait_ge(picked_ready, run + 1)
                chosen = picked[:, :, :].rearrange("p e t -> p (e t)")
                for h in range(2):
                    ins = mm(TB[0][:, h:h + 1], chosen[:, h * P:(h + 1) * P], ones_row[:, 0:1], start=True, stop=True)
                ins.then_inc(count_psum, 1)
                pe.wait_ge(count_ready, run + 1)
                n = NE * NT
                mm(TA[0][:, 0:n], after_tri[:, P:2 * P], chosen, start=True, stop=False)
                mm(TA[0][:, 0:n], count_b[:, 0, :], after_tri[:, P:3 * P], start=False, stop=False)
                mm(TA[0][:, 0:n], count_b[:, 1, :], after_tri[:, 0:2 * P], start=False, stop=True).then_inc(pos_psum, 1)
                for s in range(NTS):
                    pe.wait_ge(lo_ready, run * NTS + s + 1)
                    if s % CPS == 0:
                        pe.wait_ge(hi_row_ready, run * HS + s // CPS + 1)
                        pe.wait_ge(hi_col_ready, run * HS + s // CPS + 1)
                    ins = mm(TB[1][:, 0:2 * NHI], lo_hot[:, s, :], hi_hot[:, s, :, :].rearrange("p k c -> p (k c)"),
                             start=(s == 0), stop=(s == NTS - 1))
                ins.then_inc(inv_psum, 1)

            def experts(run):
                gathers = run * 16 * GT * (NB // 2)
                pe.wait_ge(index_ready, run + 1)

                def turn(i, s):
                    pe.wait_ge(gathered_in[s], i * (16 * GT) + (16 * GT + gathers))
                    four_transposes(TA[s], lambda t: gathered[s][:, t, :], gt_psum)

                def up(i, s, e):
                    pe.wait_ge(gt_ready, nth(i, s, base=run * NB))
                    for c in range(EC):
                        ins = product(F[:, c, :], [w[:, c * P:(c + 1) * P] for w in ew1_part[e]], [x[:, :] for x in xt_part[s]])
                        if c % 2:
                            ins.then_inc(eh_psum, 1)

                def down(i, s, e):
                    for half in range(2):
                        pe.wait_ge(eh_ready, i * 4 + (2 * s + half + 1 + run * 2 * NB))
                        ins = add_half(TB[s], half, lambda c, t: hid[s][:, c, t * P:(t + 1) * P], lambda c: ew2_sb[e][:, c, :])
                    ins.then_inc(eo_psum, 1)

                def pair(k, last=False):
                    for e in range(2):
                        i = k * 2 + e
                        pe.wait_ge(ew_loaded[e], k * 32 + (32 + run * 32 * (NE // 2)))
                        pe.wait_ge(ew1_split, k * 2 + (e + 1 + run * NE))
                        for s in range(2):
                            up(i, s, e)
                            if not (last and e == 1 and s == 1):
                                turn(i + s, 1 - s)
                            down(i, s, e)

                turn(0, 0)
                with pe.Fori(0, NE // 2 - 1) as k:
                    pair(k)
                pair(NE // 2 - 1, last=True)

            route(0)
            experts(0)

            VW = HPC * DH
            wqf_part, wkf_part = proj_part
            pe.wait_ge(proj_split, 2)

            def attention_step(b, head, feat, tail, late):
                h, t_, l_ = b.plus(1), b.plus(-1), b.plus(-2)

                def unit(bb, u, first=False):
                    if not first:
                        pe.wait_ge(S["ang"], bb.k(u - 2, 4))
                    for x_part, w_part in ((0, 0), (0, 1), (1, 0)):
                        if u == 0 and x_part:
                            pe.wait_ge(S["xt_lo"], bb.n())
                        for n in range(2):
                            c = 2 * (u % 2) + n
                            chunk = slice(c * P, (c + 1) * P)
                            rows_in, flags = xt_part[bb.q][x_part], dict(start=x_part == w_part, stop=x_part == 1)
                            if u < 2:
                                ins = mm(F[:, c, :], rows_in[:, chunk], wkf_part[w_part][:, :], **flags)
                            else:
                                ins = mm(F[:, c, :], wqf_part[w_part][:, chunk], rows_in[:, :], **flags)
                    ins.then_inc(S["proj_psum"], 1)

                if feat:
                    unit(b, 1, not tail)
                if tail:
                    pe.wait_ge(S["kvt"], t_.n())
                    if late:
                        pe.wait_ge(S["wo_used"], l_.n())
                    four_transposes(T_B, lambda t: kvt[t_.q][:, t, :], S["kv_psum"])
                if feat:
                    unit(b, 2)
                if tail:
                    pe.wait_ge(S["kvm"], t_.n())
                    pe.wait_ge(S["feat"], t_.k(3, 4))
                    for a, dst in ((0, T_A), (1, T_B)):
                        for sc in range(2):
                            for j in range(NJ):
                                ins = mm(dst[j * VW:(j + 1) * VW, :], kvm[:, 2 * a + sc, j, :], qfeat[t_.q][:, sc, j, :],
                                         start=(sc == 0), stop=(sc == 1), tile_position=(0, j * VW))
                    ins.then_inc(S["num_psum"], 1)
                if late:
                    pe.wait_ge(S["xf"], l_.n())
                    if feat:
                        pe.wait_ge(S["qkv_used"], b.k(3, 4))
                    four_transposes(H_B, lambda t: xf[l_.q][:, t, :], S["xft_psum"])
                if feat:
                    unit(b, 3)
                if late:
                    pe.wait_ge(S["xft"], l_.n())
                    for t in range(GT):
                        ins = mm(H_B[:, t * NE:(t + 1) * NE], xrt[:, t * P:(t + 1) * P], wrt[:, :], start=True, stop=True)
                    ins.then_inc(S["logit_psum"], 1)
                if tail:
                    pe.wait_ge(S["num"], t_.n())
                    for t in range(GT):
                        tr(T_A[:, t * P:(t + 1) * P], num_s[:, t, :], ident[:, :])
                    four_transposes(T_B, lambda t: den_s[:, t, :], S["numt_psum"])
                if feat:
                    pe.wait_ge(S["feat"], b.k(1, 4))
                    pe.wait_ge(S["qkv_used"], b.k(3, 4))
                    for a in range(2):
                        pe.wait_ge(S[("vk", "krep")[a]], b.n())
                        for t in range(GT):
                            for j in range(NJ):
                                ins = mm(H_A[j * VW:(j + 1) * VW, a * 2 * P:(a + 1) * 2 * P].rearrange("p (s c) -> p s c", s=2),
                                         vk[b.q][:, a, t, j * VW:(j + 1) * VW], kfeat[b.q][:, t, :, j * P:(j + 1) * P],
                                         start=(t == 0), stop=(t == GT - 1), tile_position=(0, j * VW))
                    ins.then_inc(S["kvt_psum"], 1)

                def qkv(t):
                    if t >= 2:
                        pe.wait_ge(S["qkv_used"], h.k(t - 2, 4))
                    product((H_A, H_B)[t % 2][:, 0:3 * C], [x[:, t * P:(t + 1) * P] for x in xt_part[h.q]],
                            [w[:, :] for w in wqkv_part])\
                        .then_inc(S["qkv_psum"], 1)
                if head:
                    pe.wait_ge(S["ax"], h.n())
                    if late:
                        pe.wait_ge(S["logit_read"], l_.n())
                    four_transposes(H_B, lambda t: ax[:, t, :], S["axt_psum"])
                if head:
                    pe.wait_ge(S["axt"], h.n())
                    unit(h, 0, not feat)
                if tail:
                    pe.wait_ge(S["att"], t_.n())
                    four_transposes(T_A, lambda t: att[:, t, :], S["attt_psum"])
                if head:
                    if feat:
                        pe.wait_ge(S["kvt"], b.n())
                    qkv(0)
                    qkv(1)
                    qkv(2)
                    qkv(3)
                if tail:
                    pe.wait_ge(S["attt"], t_.n())
                    for t in range(GT):
                        ins = mm(T_B[:, t * P:(t + 1) * P], att_t[:, t * P:(t + 1) * P], wot[:, :], start=True, stop=True)
                    ins.then_inc(S["wo_psum"], 1)

            run_pipeline(pe, attention_step)
            route(1)
            experts(1)


_INS = ["L0_attn_a_x", "L0_attn_a_w1", "L0_attn_a_b1", "L0_attn_a_w2", "L0_attn_a_b2", "L0_attn_a_gamma1", "L0_attn_a_beta1",
        "L0_attn_a_gamma2", "L0_attn_a_beta2", "L0_attn_b_wq", "L0_attn_b_wk", "L0_attn_b_wv", "L0_attn_b_wo",
        "L0_attn_b_rf", "L0_ffn_Wr", "L0_ffn_W1", "L0_ffn_W2"]


def kernel(**inputs):
    import numpy as np
    import concourse.bacc as bacc
    from concourse.bass_utils import run_bass_kernel_spmd

    nc = bacc.Bacc("TRN2", target_bir_lowering=False, num_devices=1)
    arrays, args = {}, []
    for name in _INS:
        a = np.ascontiguousarray(inputs[name])
        if name == "L0_attn_a_x":
            shape = a.shape
            a = a.reshape(-1, a.shape[-1])
        arrays[f"in_{name}"] = a
        args.append(nc.dram_tensor(f"in_{name}", a.shape, mybir.dt.from_np(a.dtype), kind="ExternalInput").ap())
    rows_out = (shape[0] * shape[1], shape[2])
    args.append(nc.dram_tensor("out_dram", rows_out, F32, kind="ExternalOutput").ap())
    build(nc, *args)
    r = run_bass_kernel_spmd(nc, [arrays], core_ids=[0])
    return r.results[0]["out_dram"].reshape(shape)
```
